# Optimizing a Trainium2 kernel written in Bass

```python
import numpy as np
import jax
import jax.numpy as jnp

def _softmax(x, axis=-1):
    return jax.nn.softmax(x, axis=axis)

def _gelu(x):
    return jax.nn.gelu(x, approximate=True)

def _silu(x):
    return jax.nn.silu(x)

def _sigmoid(x):
    return jax.nn.sigmoid(x)

def _layernorm(x, axis=-1, eps=1e-05):
    m = jnp.mean(x, axis=axis, keepdims=True)
    v = jnp.var(x, axis=axis, keepdims=True)
    return (x - m) / jnp.sqrt(v + eps)

def _scatter_add(tgt, idx, src, axis=0):
    return tgt.at[idx].add(src)

def _segment_sum(src, seg, n):
    return jax.ops.segment_sum(src, seg, n)
kernel_name = 'mk_xattn_ffn_d1_seqx_r4_062af2'

def setup_inputs(seed: int=0):
    np.random.seed(seed)
    _w = jnp.asarray

    def _rec_inputs():
        import jax
        import jax.numpy as jnp
        _rk = jax.random.key(seed)
        x = -0.0002928 + 1 * jax.random.normal(jax.random.fold_in(_rk, 1), (2, 1024, 256), jnp.float32)
        _lenS = 1024 - jax.random.randint(jax.random.fold_in(_rk, 7), (2,), 0, max(1, 1024 // 4) + 1, jnp.int32)
        _lenS2 = 77 - jax.random.randint(jax.random.fold_in(_rk, 8), (2,), 0, max(1, 77 // 4) + 1, jnp.int32)
        _ctx_1024P = jax.random.normal(jax.random.fold_in(_rk, 11), (2, 16, 256), jnp.float32)
        _ctx_1024c = jax.random.dirichlet(jax.random.fold_in(_rk, 511), 0.3 * jnp.ones((16,), jnp.float32), (2, 77))
        _ctx_1024t = jnp.einsum('bsk,bkd->bsd', _ctx_1024c, _ctx_1024P)
        _ctx_1024t = _ctx_1024t * jax.lax.rsqrt(jnp.mean(jnp.square(_ctx_1024t)) + 1e-12) * 0.953939
        ctx_1024 = -1.39393e-06 + 0.999914 * (_ctx_1024t + 0.3 * jax.random.normal(jax.random.fold_in(_rk, 611), (2, 77, 256), jnp.float32))
        _validS = jnp.arange(1024)[None, :] < _lenS[:, None]
        _validS2 = jnp.arange(77)[None, :] < _lenS2[:, None]
        _causal = jnp.tril(jnp.ones((1024, 1024), dtype=bool))
        mask_1x1xSxS2_ik0 = jnp.where(jnp.broadcast_to(_validS2[0:1, None, None, :], (1, 1, 1024, 77)), 0, 1).astype(jnp.int32)
        return (x, ctx_1024, mask_1x1xSxS2_ik0)
    x, ctx_1024, mask_1x1xSxS2_ik0 = _rec_inputs()

    def _L0_xattn_setup():
        import jax, jax.numpy as jnp
        import numpy as np
        B, L, E, H = (2, 512, 256, 16)
        Dh = E // H
        key = jax.random.key(seed)
        ks = jax.random.split(key, 12)
        s = 0.02
        inp = {'x_q': jax.random.normal(ks[0], (B, L, E), jnp.float32), 'x_k': jax.random.normal(ks[1], (B, L, E), jnp.float32), 'x_v': jax.random.normal(ks[2], (B, L, E), jnp.float32), 'mask': jnp.tril(jnp.ones((L, L), jnp.int32))[None, None], 'Wq': jax.random.normal(ks[3], (E, E), jnp.float32) * s, 'bq': jnp.zeros((E,), jnp.float32), 'Wk': jax.random.normal(ks[4], (E, E), jnp.float32) * s, 'bk': jnp.zeros((E,), jnp.float32), 'Wv': jax.random.normal(ks[5], (E, E), jnp.float32) * s, 'bv': jnp.zeros((E,), jnp.float32), 'Wo': jax.random.normal(ks[6], (E, E), jnp.float32) * s, 'bo': jnp.zeros((E,), jnp.float32)}
        return inp
    _L0_xattn_all = _L0_xattn_setup()
    _L0_xattn_in = {k: v for k, v in _L0_xattn_all.items() if k in ('Wq', 'bq', 'Wk', 'bk', 'Wv', 'bv', 'Wo', 'bo')}
    del _L0_xattn_all

    def _L0_ffn_setup():
        import jax, jax.numpy as jnp
        import numpy as np
        B, S, D, H, E, K = (4, 512, 256, 1024, 8, 2)
        CAPACITY_FACTOR = 1.5
        C = int(CAPACITY_FACTOR * B * S * K / E)
        key = jax.random.key(seed)
        ks = jax.random.split(key, 6)
        x = jax.random.normal(ks[0], (B, S, D), dtype=jnp.float32)
        w_router = jax.random.normal(ks[1], (D, E), dtype=jnp.float32) * 0.02
        w1 = jax.random.normal(ks[2], (E, D, H), dtype=jnp.float32) * 0.02
        b1 = jnp.zeros((E, H), dtype=jnp.float32)
        w2 = jax.random.normal(ks[3], (E, H, D), dtype=jnp.float32) * 0.02
        b2 = jnp.zeros((E, D), dtype=jnp.float32)
        return {'x': x, 'w_router': w_router, 'w1': w1, 'b1': b1, 'w2': w2, 'b2': b2}
    _L0_ffn_all = _L0_ffn_setup()
    _L0_ffn_in = {k: v for k, v in _L0_ffn_all.items() if k in ('w_router', 'w1', 'b1', 'w2', 'b2')}
    del _L0_ffn_all
    return {'x': x, 'ctx_1024': ctx_1024, 'mask_1x1xSxS2_ik0': mask_1x1xSxS2_ik0, 'L0_xattn_Wq': _L0_xattn_in['Wq'], 'L0_xattn_bq': _L0_xattn_in['bq'], 'L0_xattn_Wk': _L0_xattn_in['Wk'], 'L0_xattn_bk': _L0_xattn_in['bk'], 'L0_xattn_Wv': _L0_xattn_in['Wv'], 'L0_xattn_bv': _L0_xattn_in['bv'], 'L0_xattn_Wo': _L0_xattn_in['Wo'], 'L0_xattn_bo': _L0_xattn_in['bo'], 'L0_ffn_w_router': _L0_ffn_in['w_router'], 'L0_ffn_w1': _L0_ffn_in['w1'], 'L0_ffn_b1': _L0_ffn_in['b1'], 'L0_ffn_w2': _L0_ffn_in['w2'], 'L0_ffn_b2': _L0_ffn_in['b2']}

def reference(x, ctx_1024, mask_1x1xSxS2_ik0, L0_xattn_Wq, L0_xattn_bq, L0_xattn_Wk, L0_xattn_bk, L0_xattn_Wv, L0_xattn_bv, L0_xattn_Wo, L0_xattn_bo, L0_ffn_w_router, L0_ffn_w1, L0_ffn_b1, L0_ffn_w2, L0_ffn_b2):
    import jax
    import jax.numpy as jnp

    def _L0_xattn_ref(x_q, x_k, x_v, mask, Wq, bq, Wk, bk, Wv, bv, Wo, bo):
        import jax, jax.numpy as jnp
        import numpy as np
        B, L, E, H = (2, 512, 256, 16)
        Dh = E // H
        N, Lq, _ = x_q.shape
        Lk = x_k.shape[1]
        q = (x_q @ Wq.T + bq).reshape(N, Lq, H, Dh).transpose(0, 2, 1, 3)
        k = (x_k @ Wk.T + bk).reshape(N, Lk, H, Dh).transpose(0, 2, 1, 3)
        v = (x_v @ Wv.T + bv).reshape(N, Lk, H, Dh).transpose(0, 2, 1, 3)
        scores = jnp.einsum('bhqd,bhkd->bhqk', q, k) / jnp.sqrt(jnp.float32(Dh))
        scores = jnp.where(mask == 0, jnp.float32(-1000000000.0), scores)
        attn = jax.nn.softmax(scores, axis=-1)
        out = jnp.einsum('bhqk,bhkd->bhqd', attn, v)
        out = out.transpose(0, 2, 1, 3).reshape(N, Lq, E)
        return out @ Wo.T + bo

    def _L0_ffn_ref(x, w_router, w1, b1, w2, b2):
        import jax, jax.numpy as jnp
        import numpy as np
        B, S, D, H, E, K = (4, 512, 256, 1024, 8, 2)
        CAPACITY_FACTOR = 1.5
        C = int(CAPACITY_FACTOR * B * S * K / E)
        Bs, Ss, Ds = x.shape
        N = Bs * Ss
        xf = x.reshape(N, Ds)
        logits = xf @ w_router
        probs = jax.nn.softmax(logits, axis=-1)
        gate, eidx = jax.lax.top_k(probs, K)
        gate = gate / jnp.sum(gate, axis=-1, keepdims=True)
        oh = jax.nn.one_hot(eidx, E, dtype=jnp.float32)
        ohf = oh.reshape(N * K, E)
        pos = jnp.cumsum(ohf, axis=0) - 1.0
        posk = jnp.sum(pos * ohf, axis=-1).reshape(N, K).astype(jnp.int32)
        keep = posk < C
        gate = gate * keep.astype(gate.dtype)
        e_flat = eidx.reshape(-1)
        p_flat = jnp.where(keep, posk, 0).reshape(-1)
        contrib = (xf[:, None, :] * keep[..., None].astype(xf.dtype)).reshape(N * K, Ds)
        expert_in = jnp.zeros((E, C, Ds), dtype=xf.dtype).at[e_flat, p_flat].add(contrib)
        h = jax.nn.relu(jnp.einsum('ecd,edh->ech', expert_in, w1) + b1[:, None, :])
        expert_out = jnp.einsum('ech,eho->eco', h, w2) + b2[:, None, :]
        tok = expert_out[e_flat, p_flat].reshape(N, K, -1)
        y = jnp.sum(tok * gate[..., None], axis=1)
        return y.reshape(Bs, Ss, -1)
    x = x + _L0_xattn_ref(_layernorm(x, axis=-1), ctx_1024, ctx_1024, mask_1x1xSxS2_ik0, L0_xattn_Wq, L0_xattn_bq, L0_xattn_Wk, L0_xattn_bk, L0_xattn_Wv, L0_xattn_bv, L0_xattn_Wo, L0_xattn_bo)
    x = x + _L0_ffn_ref(_layernorm(x, axis=-1), L0_ffn_w_router, L0_ffn_w1, L0_ffn_b1, L0_ffn_w2, L0_ffn_b2)
    return x

_drawn_inputs = setup_inputs


def setup_inputs(seed=0):
    import zlib

    import numpy as np

    out = dict(_drawn_inputs(seed))
    spreads = {'L0_xattn_bq': (0.0, 0.8),
     'L0_xattn_bk': (0.0, 0.8),
     'L0_xattn_bv': (0.0, 0.1),
     'L0_xattn_bo': (0.0, 0.1),
     'L0_ffn_b1': (0.0, 0.1),
     'L0_ffn_b2': (0.0, 0.1)}
    factors = {'L0_xattn_Wq': 8.0, 'L0_xattn_Wk': 7.331}
    for name, (base, spread) in spreads.items():
        noise = np.random.default_rng([zlib.crc32(name.encode()), seed]).standard_normal(out[name].shape)
        drawn = base * np.exp(spread * noise) if base else spread * noise
        out[name] = jnp.asarray(drawn.astype(out[name].dtype))
    for name, factor in factors.items():
        out[name] = (out[name] * factor).astype(out[name].dtype)
    return out
```

```python
from contextlib import ExitStack

import concourse.bass as bass
from concourse import mybir

ALU = mybir.AluOpType
ACT = mybir.ActivationFunctionType
AX = mybir.AxisListType
F32 = mybir.dt.float32
F32R = mybir.dt.float32r
F16 = mybir.dt.float16
BF16 = mybir.dt.bfloat16
I32 = mybir.dt.int32
U32 = mybir.dt.uint32

P = 128
NEG = -1.0e9
EPS = 1e-5


class Count:

    def __init__(self, reg, scale=1, offset=0):
        self.reg, self.scale, self.offset = reg, scale, offset

    def __add__(self, n):
        return Count(self.reg, self.scale, self.offset + n)

    def __sub__(self, n):
        return self + -n

    def __mul__(self, n):
        return Count(self.reg, self.scale * n, self.offset * n)

    __radd__, __rmul__ = __add__, __mul__


def at(n):
    if isinstance(n, int):
        return n
    v = n.reg * n.scale if n.scale != 1 else n.reg
    return v + n.offset if n.offset else v


def later(n, first):
    return not isinstance(n, int) or n > first


def at_most(n, top):
    return max(0, min(n, top)) if isinstance(n, int) else n


def xattn_moe_kernel(nc, x, ctx_in, mask, Wq, bq, Wk, bk, Wv, bv, Wo, bo, w_router, w1, b1, w2, b2, out):
    NB, SQ, D = x.shape
    NK = ctx_in.shape[1]
    NE, _, HID = w1.shape
    NH = 16
    DH = D // NH
    KT = D // P
    MT = HID // P
    NTOK = NB * SQ
    NT = NTOK // P
    TPB = SQ // P
    G = 2
    GT = G * P
    NM = NT // G
    MPB = TPB // G
    HH = NH // 2
    CAP = int(1.5 * NTOK * 2 / NE)
    CH = 256
    CPE = CAP // CH
    NCH = NE * CPE
    SLOTS = NE * CAP
    VW = 3 * DH + 1
    UC = HH * NK

    x_v = x.rearrange("b (t p) d -> p (b t) d", p=P)
    out_v = out.rearrange("b (t p) d -> p (b t) d", p=P)
    mask_v = mask.rearrange("a b (t p) k -> p (a b t) k", p=P)
    xe = nc.dram_tensor("expert_in", (SLOTS + 2 * NTOK, D), F32, kind="Internal").ap()
    eo = nc.dram_tensor("expert_out", (SLOTS, D), F32, kind="Internal").ap()
    xe_v = xe[0:SLOTS, :].rearrange("(c t p) d -> p c t d", t=G, p=P)
    eo_v = eo.rearrange("(c t p) d -> p c t d", t=G, p=P)

    with ExitStack() as es:
        def sb(name, shape, dt=F32):
            return es.enter_context(nc.sbuf_tensor(name, shape, dt))

        def sem(name):
            return es.enter_context(nc.semaphore(name))

        shared = sb("shared", [P, 5 * 2 * GT * KT])

        def piece(at_, parts_, *shape):
            n = 1
            for k in shape:
                n *= k
            v = shared[0:parts_, at_:at_ + n]
            if len(shape) == 2:
                return v.rearrange("p (a b) -> p a b", a=shape[0])
            if len(shape) == 3:
                return v.rearrange("p (a b c) -> p a b c", a=shape[0], b=shape[1])
            return v

        wnat = piece(0, P, 4, KT, D)
        cnat = piece(2048, NK, NB, D)
        wkT = piece(2560, P, KT, D)
        wvT = piece(3072, P, KT, D)
        vrest = piece(3584, NK, 2, NB * D)
        vf = piece(4608, NK, NB * D)
        hf = piece(0, P, 2, 2 * CH)
        xc = piece(1024, P, 2, G, D)
        yb = piece(2048, P, 2, G, D)
        ga = piece(3072, P, 3, 2, D)
        fin = piece(4608, P, 2, D)
        wh = sb("wh", [P, 2, 2 * KT * HID], F32R)

        def early(i, flat=False):
            v = wh[:, 1, i * KT * D:(i + 1) * KT * D]
            return v if flat else v.rearrange("p (k d) -> p k d", k=KT)

        wqh, wql, woh, wol, qh, ql = (early(i) for i in range(6))
        oTh, oTl = early(6, True), early(7, True)
        pb = sb("pb", [P, 2, UC])
        mraw = pb[:].rearrange("p a b -> p (a b)")[:, 0:TPB * NK].bitcast(I32).rearrange("p (t k) -> p t k", t=TPB)
        zrow = sb("zrow", [P, D])
        identf = sb("identf", [P, P])
        identb = sb("identb", [P, P], BF16)
        before = sb("before", [P, P], BF16)
        onesb = sb("onesb", [P, P], BF16)
        inv_nk = sb("inv_nk", [NK, P])
        blockh = sb("blockh", [P, HH])
        mhalf = sb("mhalf", [P, G])
        iota_e = sb("iota_e", [P, NE])
        base_e = sb("base_e", [P, NE])
        dump = sb("dump", [P, NT, 2])
        xs = sb("xs", [P, NT, D])
        brow = sb("brow", [NE * MT + 2 * KT, P])
        bcol = sb("bcol", [P, NE * MT + 2 * KT])
        bo_b = sb("bo_b", [P, D])
        bv_b = sb("bv_b", [NK, D])
        b2_b = sb("b2_b", [P, NE, D])
        wr = sb("wr", [P, KT, NE])
        cT = sb("cT", [P, KT, NB * NK])
        ktf = sb("ktf", [P, KT, NB * NK])
        vcat = sb("vcat", [NK, NB, NH, VW], BF16)
        vmean = sb("vmean", [P, NB, D])
        mb = sb("mb", [P, NT, NK], BF16)
        live = sb("live", [P, NT])
        dead = sb("dead", [P, NT])
        mmax = sb("mmax", [P, TPB])
        st = sb("st", [P, G, 6])
        mv = sb("mv", [P, G, 2])
        rstd = sb("rstd", [P, G])
        xn = sb("xn", [P, G, D])
        xTh = sb("xTh", [P, 2, KT * GT], F32R)
        xTl = sb("xTl", [P, 2, KT * GT], F32R)
        mx = sb("mx", [P, 2, HH])
        pth = sb("pth", [NK, 2, HH * P], F16)
        ptl = sb("ptl", [NK, 2, HH * P], F16)
        osum = sb("osum", [P, HH * DH])
        rinv = sb("rinv", [P, HH])
        o = sb("o", [P, G, D])
        odead = sb("odead", [P, G, D])
        xbo = sb("xbo", [P, G, D])
        st2 = sb("st2", [P, G, 6])
        mv2 = sb("mv2", [P, G, 2])
        rstd2 = sb("rstd2", [P, G])
        xn2 = sb("xn2", [P, G, D])
        x2T = sb("x2T", [P, KT * GT])
        lg = sb("lg", [P, G, NE])
        top = sb("top", [P, G, 8])
        tix = sb("tix", [P, G, 8], U32)
        ek = sb("ek", [P, G, 2])
        oh = sb("oh", [P, G, 2, NE])
        ohs = sb("ohs", [P, G, NE], BF16)
        run = sb("run", [P, 2, NE], BF16)
        slotv = sb("slotv", [P, G, NE])
        pick = sb("pick", [P, G, 2, NE])
        sk = sb("sk", [P, G, 2])
        eb = sb("eb", [P, G, 2])
        pos = sb("pos", [P, G, 2])
        kp = sb("kp", [P, G, 2])
        t1 = sb("t1", [P, G, 2])
        t2 = sb("t2", [P, G, 2])
        sidx = sb("sidx", [P, G, 2], I32)
        gidx = sb("gidx", [P, NT, 2], I32)
        keep = sb("keep", [P, NT, 2])
        top2 = sb("top2", [P, NT, 2])
        gd = sb("gd", [P, NT])
        ge = sb("ge", [P, NT])
        g1 = sb("g1", [P, NT])
        gate = sb("gate", [P, NT, 2])
        wraw = sb("wraw", [P, 2 * KT * HID])
        wl = sb("wl", [P, 2, 2 * KT * HID], F32R)
        hh = sb("hh", [P, 2, MT * CH], F32R)
        hl = sb("hl", [P, 2, MT * CH], F32R)
        kbh = hh[:].rearrange("p a b -> p (a b)")[:, 0:NB * KT * UC].rearrange("p (b r c) -> p b r c", b=NB, r=KT)
        kbl = hl[:].rearrange("p a b -> p (a b)")[:, 0:NB * KT * UC].rearrange("p (b r c) -> p b r c", b=NB, r=KT)

        ps = es.enter_context(nc.psum_tensor("ps", [P, 8, 512], F32))
        SC, PT, PV, MISC = 0, 4, 6, 7
        W4 = UC // 2

        def misc(k):
            return ps[:, MISC, :].rearrange("p (a b) -> p a b", a=k)

        S = {n: sem(n) for n in (
            "const_ready", "const_step", "x_loaded", "w_loaded", "small_loaded", "mask_loaded", "zero_done",
            "pe_setup", "act_setup", "dve_setup", "mask_ready",
            "xT_ready", "q_ready", "sc_ready", "pt_ready", "pv_ready", "oT_ready", "wo_ready", "x2T_ready",
            "lg_ready", "pos_ready",
            "stat_step", "rstd_ready", "rstd2_ready", "xn_ready", "xT_split", "xT_rest", "q_split", "q_rest", "max_ready", "diff_ready", "exp_ready",
            "pth_ready", "ptl_ready", "osum_ready", "o_half", "o_ready", "odead_ready", "oT_split", "oT_rest",
            "xbo_ready", "x1_ready", "stat2_step", "xn2_ready", "x2T_copied",
            "lg_copied", "top_ready", "tix_ready", "route_step", "oh_ready", "run_ready", "slot_ready", "pick_ready",
            "sk_ready", "scattered", "osum_part", "vpart_step",
            "wraw_loaded0", "wraw_loaded1", "w_head", "w_rest", "xc_loaded0", "xc_loaded1", "fxT_ready", "fxT_head", "fxT_rest",
            "h_ready", "h_relu", "h_head", "h_rest", "y_ready", "y_copied", "y_stored0", "y_stored1",
            "gate_step", "gate_exp", "gate_ready", "gath0", "gath1", "gath2", "fin_step", "fin_ready",
            "fin_stored0", "fin_stored1",
        )}

        block = es.enter_context(nc.Block())

        def macro_loop(eng, body):
            body(0)
            body(1)
            with eng.Fori(2, NM - 1) as m:
                body(Count(m))
            body(NM - 1)
            body(NM)
            body(NM + 1)

        def wait_apart(eng):
            eng.nop(nofuse=True)

        def batch_of(m):
            return at(m) // MPB

        def parts(m):
            if not isinstance(m, int):
                return True, True, True, True
            return m < NM, m + 1 < NM, 1 <= m <= NM, 2 <= m <= NM + 1

        @block.sync
        def _(sp):
            half = NT // 2
            sp.dma_start(wnat[:, 0], Wq.rearrange("(r p) d -> p r d", p=P)).then_inc(S["w_loaded"], 16)
            sp.dma_start(wnat[:, 1], Wk.rearrange("(r p) d -> p r d", p=P)).then_inc(S["w_loaded"], 16)
            sp.dma_start(cnat, ctx_in.rearrange("b k d -> k b d")).then_inc(S["w_loaded"], 16)
            sp.dma_start(wnat[:, 2], Wv.rearrange("(r p) d -> p r d", p=P)).then_inc(S["w_loaded"], 16)
            sp.dma_start(wnat[:, 3], Wo.rearrange("(r p) d -> p r d", p=P)).then_inc(S["w_loaded"], 16)
            nb1 = NE * MT
            sp.dma_start(brow[0:nb1, :], b1.rearrange("e (m p) -> (e m) p", p=P)).then_inc(S["small_loaded"], 16)
            sp.dma_start(brow[nb1:nb1 + KT, :], bq.rearrange("(m p) -> m p", p=P)).then_inc(S["small_loaded"], 16)
            sp.dma_start(brow[nb1 + KT:nb1 + 2 * KT, :], bk.rearrange("(m p) -> m p", p=P)).then_inc(S["small_loaded"], 16)
            sp.dma_start(bv_b[:], bv.rearrange("(a d) -> a d", a=1).partition_broadcast(NK)).then_inc(S["small_loaded"], 16)
            sp.dma_start(bo_b[:], bo.rearrange("(a d) -> a d", a=1).partition_broadcast(P)).then_inc(S["small_loaded"], 16)
            sp.dma_start(wr[:], w_router.rearrange("(r p) e -> p r e", p=P)).then_inc(S["small_loaded"], 16)
            sp.dma_start(b2_b[:], b2.rearrange("(a e) d -> a e d", a=1).partition_broadcast(P)).then_inc(S["small_loaded"], 16)
            sp.wait_ge(S["const_ready"], 1)
            rows = SLOTS // P
            xz = xe[0:SLOTS, :].rearrange("(p r) d -> p (r d)", p=P)
            for i in range(rows // 8):
                sp.dma_start(xz[:, i * 8 * D:(i + 1) * 8 * D].rearrange("p (r d) -> p r d", d=D),
                             zrow[:].unsqueeze(1).to_broadcast([P, 8, D])).then_inc(S["zero_done"], 16)
            def load_weights(e, half):
                if later(e, 0):
                    sp.wait_ge(S["w_head"], at(2 * e + half - 1))
                    sp.wait_ge(S["w_rest"], at(2 * e + half - 1))
                if half == 0:
                    sp.dma_start(wraw[:, 0:KT * HID].rearrange("p (k h) -> p k h", k=KT),
                                 w1[at(e)].rearrange("(k p) h -> p k h", p=P)).then_inc(S["wraw_loaded0"], 16)
                else:
                    sp.dma_start(wraw[:, KT * HID:].rearrange("p (k d) -> p k d", k=MT),
                                 w2[at(e)].rearrange("(k p) d -> p k d", p=P)).then_inc(S["wraw_loaded1"], 16)

            def load_chunk(c, par):
                if later(c, 1):
                    sp.wait_ge(S["fxT_ready"], at(c - 1))
                sp.dma_start(xc[:, par], xe_v[:, at(c)]).then_inc(S["xc_loaded%d" % par], 16)

            def store_chunk(c, par):
                sp.wait_ge(S["y_copied"], at(c + 1))
                sp.dma_start(eo_v[:, at(c)], yb[:, par]).then_inc(S["y_stored%d" % par], 16)

            sp.wait_ge(S["dve_setup"], 5)
            load_weights(0, 0)
            load_weights(0, 1)
            load_weights(1, 0)
            load_weights(1, 1)
            sp.wait_ge(S["scattered"], at(16 * 2 * NT))
            load_chunk(0, 0)
            load_chunk(1, 1)

            def pair(ep, last):
                for a in range(2):
                    e = ep * 2 + a
                    for j in range(CPE):
                        i = a * CPE + j
                        c = ep * (2 * CPE) + i
                        if not last and j >= 1:
                            load_weights(e + 2, j - 1)
                        if not (last and i >= 2 * CPE - 2):
                            load_chunk(c + 2, i % 2)
                        store_chunk(c, i % 2)

            pair(0, False)
            with sp.Fori(1, NE // 2 - 1) as ep:
                pair(Count(ep), False)
            pair(NE // 2 - 1, True)
            for t in range(NT):
                sp.wait_ge(S["fin_ready"], at(t + 1))
                sp.dma_start(out_v[:, t], fin[:, t % 2]).then_inc(S["fin_stored%d" % (t % 2)], 16)
            sp.wait_ge(S["fin_stored0"], at(16 * NT // 2))
            sp.wait_ge(S["fin_stored1"], at(16 * NT // 2))

        @block.gpsimd
        def _(pool):
            g = nc.gpsimd
            g.memset(zrow[:], 0.0).then_inc(S["const_ready"], 1)
            g.memset(identf[:], 0.0)
            g.memset(identb[:], 0.0)
            g.memset(before[:], 1.0)
            g.memset(onesb[:], 1.0)
            g.memset(mhalf[:], -0.5)
            g.memset(inv_nk[:], 1.0 / NK)
            g.memset(run[:], 0.0)
            g.memset(ohs[:], 0.0)
            g.memset(blockh[:], 1.0)
            g.memset(vcat[:, :, :, 3 * DH:VW], 1.0)
            g.iota(iota_e[:], pattern=[[1, NE]], base=0, channel_multiplier=0, allow_small_or_imprecise_dtypes=True)
            g.iota(base_e[:], pattern=[[CAP, NE]], base=0, channel_multiplier=0, allow_small_or_imprecise_dtypes=True)
            g.iota(dump[:], pattern=[[P, NT], [NTOK, 2]], base=SLOTS, channel_multiplier=1,
                   allow_small_or_imprecise_dtypes=True).then_inc(S["const_step"], 1)
            pool.wait_ge(S["const_step"], 1)
            g.affine_select(out=identf[:], in_=identf[:], compare_op=ALU.not_equal, fill=1.0, base=0,
                            pattern=[[-1, P]], channel_multiplier=1)
            g.affine_select(out=identb[:], in_=identb[:], compare_op=ALU.not_equal, fill=1.0, base=0,
                            pattern=[[-1, P]], channel_multiplier=1)
            g.affine_select(out=before[:], in_=before[:], compare_op=ALU.is_gt, fill=0.0, base=0,
                            pattern=[[1, P]], channel_multiplier=-1)
            g.affine_select(out=blockh[:], in_=blockh[:], compare_op=ALU.is_ge, fill=0.0, base=0,
                            pattern=[[-DH, HH]], channel_multiplier=1).then_inc(S["const_step"], 1)
            pool.wait_ge(S["const_step"], 2)
            g.affine_select(out=blockh[:], in_=blockh[:], compare_op=ALU.is_ge, fill=0.0, base=DH - 1,
                            pattern=[[DH, HH]], channel_multiplier=-1).then_inc(S["const_ready"], 1)

            def inverse_std(m_, r_, tag, done, n):
                pool.wait_ge(S[tag], at(2 * G * (n + 1)))
                wait_apart(pool)
                g.tensor_scalar(r_[:], m_[:, :, 1], EPS, None, ALU.add).then_inc(S[done], 1)
                pool.wait_ge(S[done], at(2 * n + 1))
                wait_apart(pool)
                g.tensor_tensor(r_[:], r_[:], mhalf[:], ALU.pow).then_inc(S[done], 1)

            inverse_std(mv, rstd, "stat_step", "rstd_ready", 0)

            def body(m):
                units, qn, tail, slots = parts(m)
                if slots:
                    n = m - 2
                    base = n * 11
                    pool.wait_ge(S["oh_ready"], at(2 * (n + 1)))
                    wait_apart(pool)
                    g.tensor_tensor(run[:, 0, :], run[:, 1, :], ohs[:, 1, :], ALU.add).then_inc(S["route_step"], 1)
                    pool.wait_ge(S["route_step"], at(base + 1))
                    wait_apart(pool)
                    g.tensor_tensor(ohs[:], oh[:, :, 0, :], oh[:, :, 1, :], ALU.add).then_inc(S["route_step"], 1)
                    pool.wait_ge(S["route_step"], at(base + 2))
                    wait_apart(pool)
                    g.tensor_tensor(run[:, 1, :], run[:, 0, :], ohs[:, 0, :], ALU.add).then_inc(S["run_ready"], 1)
                    g.tensor_scalar(eb[:], ek[:], float(CAP), None, ALU.mult).then_inc(S["route_step"], 1)
                if qn:
                    inverse_std(mv, rstd, "stat_step", "rstd_ready", m + 1)
                if tail:
                    n = m - 1
                    if later(n, 0):
                        pool.wait_ge(S["x1_ready"], at(n))
                        wait_apart(pool)
                    g.tensor_tensor(xbo[:], xs[:, bass.ds(at(n * G), G), :],
                                    bo_b[:].unsqueeze(1).to_broadcast([P, G, D]), ALU.add).then_inc(S["xbo_ready"], 1)
                    pool.wait_ge(S["o_half"], at(4 * (n + 1)))
                    pool.wait_ge(S["odead_ready"], at(n + 1))
                    wait_apart(pool)
                    g.tensor_tensor(o[:], o[:], odead[:], ALU.add).then_inc(S["o_ready"], 1)
                if units:
                    if isinstance(m, int) and m == 0:
                        pool.wait_ge(S["dve_setup"], 8)
                        pool.wait_ge(S["mask_ready"], 4)
                        pool.wait_ge(S["small_loaded"], at(16 * 7))
                    if tail:
                        pool.wait_ge(S["o_ready"], at(m))
                    g.tensor_tensor(odead[:], vmean[:, batch_of(m), :].unsqueeze(1).to_broadcast([P, G, D]),
                                    dead[:, bass.ds(at(m * G), G)].unsqueeze(2).to_broadcast([P, G, D]),
                                    ALU.mult).then_inc(S["odead_ready"], 1)
                if slots:
                    n = m - 2
                    pool.wait_ge(S["slot_ready"], at(n + 1))
                    wait_apart(pool)
                    for t in range(G):
                        g.tensor_tensor(pick[:, t], oh[:, t], slotv[:, t, :].unsqueeze(1).to_broadcast([P, 2, NE]),
                                        ALU.mult).then_inc(S["pick_ready"], 1)
                    pool.wait_ge(S["sk_ready"], at(n + 1))
                    pool.wait_ge(S["route_step"], at(base + 3))
                    wait_apart(pool)
                    g.tensor_tensor(pos[:], sk[:], eb[:], ALU.subtract).then_inc(S["route_step"], 1)
                    pool.wait_ge(S["route_step"], at(base + 4))
                    wait_apart(pool)
                    g.tensor_scalar(kp[:], pos[:], float(CAP), None, ALU.is_lt).then_inc(S["route_step"], 1)
                    g.tensor_tensor(t1[:], sk[:], dump[:, bass.ds(at(n * G), G), :], ALU.subtract).then_inc(S["route_step"], 1)
                    pool.wait_ge(S["route_step"], at(base + 6))
                    wait_apart(pool)
                    g.tensor_tensor(t1[:], t1[:], kp[:], ALU.mult)
                    g.tensor_tensor(t2[:], pos[:], kp[:], ALU.mult)
                    g.tensor_copy(keep[:, bass.ds(at(n * G), G), :], kp[:]).then_inc(S["route_step"], 1)
                    pool.wait_ge(S["route_step"], at(base + 7))
                    wait_apart(pool)
                    g.tensor_tensor(t1[:], t1[:], dump[:, bass.ds(at(n * G), G), :], ALU.add).then_inc(S["route_step"], 1)
                    g.tensor_tensor(t2[:], t2[:], eb[:], ALU.add).then_inc(S["route_step"], 1)
                    pool.wait_ge(S["route_step"], at(base + 9))
                    pool.wait_ge(S["xn2_ready"], at(2 * (n + 1)))
                    wait_apart(pool)
                    g.tensor_copy(sidx[:], t1[:]).then_inc(S["route_step"], 1)
                    g.tensor_copy(gidx[:, bass.ds(at(n * G), G), :], t2[:]).then_inc(S["route_step"], 1)
                    pool.wait_ge(S["route_step"], at(base + 11))
                    wait_apart(pool)
                    for t in range(G):
                        for k in range(2):
                            g.indirect_dma_start(xe, bass.IndirectOffsetOnAxis(ap=sidx[:, t, k:k + 1], axis=0),
                                                 xn2[:, t, :], None).then_inc(S["scattered"], 16)
                if tail:
                    inverse_std(mv2, rstd2, "stat2_step", "rstd2_ready", m - 1)
                if isinstance(m, int) and m == 1:
                    pool.wait_ge(S["zero_done"], at(16 * (SLOTS // P // 8)))

            macro_loop(pool, body)

            def rest(e, par):
                for half in range(2):
                    hs = slice(half * KT * HID, (half + 1) * KT * HID)
                    pool.wait_ge(S["w_head"], at(2 * e + half + 1))
                    wait_apart(pool)
                    g.tensor_tensor(wl[:, par, hs], wraw[:, hs], wh[:, par, hs].bitcast(F32),
                                    ALU.subtract).then_inc(S["w_rest"], 1)

            rest(0, 0)
            rest(1, 1)
            with pool.Fori(1, NE // 2) as ep:
                ep = Count(ep)
                rest(ep * 2, 0)
                rest(ep * 2 + 1, 1)
            pool.wait_ge(S["y_stored0"], at(16 * NCH // 2))
            pool.wait_ge(S["y_stored1"], at(16 * NCH // 2))
            for t in range(NT):
                if t >= 3:
                    pool.wait_ge(S["fin_ready"], at(t - 2))
                for k in range(2):
                    g.indirect_dma_start(ga[:, t % 3, k, :], None, eo,
                                         bass.IndirectOffsetOnAxis(ap=gidx[:, t, k:k + 1], axis=0),
                                         ).then_inc(S["gath%d" % (t % 3)], 16)

        @block.scalar
        def _(act):
            a = nc.scalar
            act.dma_start(xs[:, 0:2], x_v[:, 0:2]).then_inc(S["x_loaded"], 16)
            act.dma_start(mraw, mask_v).then_inc(S["mask_loaded"], 16)
            act.wait_ge(S["x_loaded"], 16)
            act.dma_start(xs[:, 2:NT], x_v[:, 2:NT]).then_inc(S["x_loaded"], 16)
            act.wait_ge(S["pe_setup"], 1)
            a.activation(wqh.rearrange("p k d -> p (k d)"), ps[:, 0, :], ACT.Copy).then_inc(S["act_setup"], 1)
            act.wait_ge(S["pe_setup"], 2)
            a.activation(wkT.rearrange("p k d -> p (k d)"), ps[:, 1, :], ACT.Copy).then_inc(S["act_setup"], 1)
            act.wait_ge(S["pe_setup"], 3)
            a.activation(cT[:].rearrange("p k d -> p (k d)"), ps[:, 2, 0:KT * NB * NK], ACT.Copy).then_inc(S["act_setup"], 1)
            act.wait_ge(S["pe_setup"], 4)
            a.activation(wvT.rearrange("p k d -> p (k d)"), ps[:, 3, :], ACT.Copy).then_inc(S["act_setup"], 1)
            act.wait_ge(S["pe_setup"], 5)
            a.activation(bcol[:], ps[:, 4, 0:NE * MT + 2 * KT], ACT.Copy).then_inc(S["act_setup"], 1)
            act.wait_ge(S["pe_setup"], 6)
            a.activation(woh.rearrange("p k d -> p (k d)"), ps[:, 5, :], ACT.Copy).then_inc(S["act_setup"], 1)
            nb1 = NE * MT

            def split_xT(m):
                act.wait_ge(S["xT_ready"], at(m + 1))
                if later(m, 0):
                    act.wait_ge(S["q_ready"], at(m))
                a.activation(xTh[:, 0, :], ps[:, MISC, :], ACT.Copy).then_inc(S["xT_split"], 1)

            def split_q(m):
                act.wait_ge(S["q_ready"], at(m + 1))
                if later(m, 0):
                    act.wait_ge(S["sc_ready"], at(4 * m))
                for r in range(KT):
                    a.activation(qh[:, r, :], misc(2)[:, r, :], ACT.Identity,
                                 bias=bcol[:, nb1 + r:nb1 + r + 1]).then_inc(S["q_split"], 1)

            def exp(u, par):
                act.wait_ge(S["diff_ready"], at(u + 1))
                a.activation(pb[:, par, :], pb[:, par, :], ACT.Exp).then_inc(S["exp_ready"], 1)

            def head_pt(u, par):
                act.wait_ge(S["pt_ready"], at(u + 1))
                if later(u, 1):
                    act.wait_ge(S["pv_ready"], at(u - 1))
                a.activation(pth[:, par, :].rearrange("p (b c) -> p b c", b=2), ps[0:NK, PT:PT + 2, :],
                             ACT.Copy).then_inc(S["pth_ready"], 1)

            act.wait_ge(S["act_setup"], 5)
            split_xT(0)
            split_q(0)
            exp(0, 0)

            def body(m):
                units, qn, tail, _ = parts(m)
                if units:
                    exp(4 * m + 1, 1)
                    head_pt(4 * m, 0)
                if qn:
                    split_xT(m + 1)
                if tail:
                    act.wait_ge(S["oT_ready"], at(m))
                    if later(m, 1):
                        act.wait_ge(S["wo_ready"], at(m - 1))
                    a.activation(oTh, ps[:, MISC, :], ACT.Copy).then_inc(S["oT_split"], 1)
                if units:
                    exp(4 * m + 2, 0)
                    head_pt(4 * m + 1, 1)
                    exp(4 * m + 3, 1)
                    head_pt(4 * m + 2, 0)
                if qn:
                    split_q(m + 1)
                    exp(4 * m + 4, 0)
                if tail:
                    act.wait_ge(S["x2T_ready"], at(m))
                    if later(m, 1):
                        act.wait_ge(S["lg_ready"], at(m - 1))
                    a.activation(x2T[:], ps[:, MISC, :], ACT.Copy).then_inc(S["x2T_copied"], 1)
                if units:
                    head_pt(4 * m + 3, 1)
                if isinstance(m, int) and m == NM:
                    head(0, 0, 0)
                    head(0, 0, 1)

            def head(e, par, half):
                act.wait_ge(S["wraw_loaded%d" % half], at(16 * (e + 1)))
                if later(e, 1):
                    if half == 0:
                        act.wait_ge(S["h_ready"], at((e - 1) * (CPE * MT // 2)))
                    else:
                        act.wait_ge(S["y_ready"], at((e - 1) * CPE))
                hs = slice(half * KT * HID, (half + 1) * KT * HID)
                a.activation(wh[:, par, hs], wraw[:, hs], ACT.Copy).then_inc(S["w_head"], 1)

            macro_loop(act, body)
            act.wait_ge(S["gate_step"], 1)
            a.activation(ge[:], gd[:], ACT.Exp).then_inc(S["gate_exp"], 1)

            def ffn_xT(c, par):
                act.wait_ge(S["fxT_ready"], at(c + 1))
                a.activation(xTh[:, par, :], ps[:, 6, :], ACT.Copy).then_inc(S["fxT_head"], 1)

            def ffn_h(e, c, par):
                for i in range(MT // 2):
                    act.wait_ge(S["h_ready"], at(c * (MT // 2) + i + 1))
                    if later(c * (MT // 2) + i, 1):
                        act.wait_ge(S["h_rest"], at(c * (MT // 2) + i - 1))
                        wait_apart(act)
                    for s in range(2):
                        ins = a.activation(hf[:, i % 2, s * CH:(s + 1) * CH], ps[:, i, s * CH:(s + 1) * CH], ACT.Relu,
                                           bias=bcol[:, bass.ds(at(e * MT + 2 * i + s), 1)])
                    ins.then_inc(S["h_relu"], 1)
                    act.wait_ge(S["h_relu"], at(c * (MT // 2) + i + 1))
                    if i == 0 and (later(c, 1)):
                        act.wait_ge(S["y_ready"], at(c - 1))
                    a.activation(hh[:, par, 2 * i * CH:2 * (i + 1) * CH], hf[:, i % 2, :],
                                 ACT.Copy).then_inc(S["h_head"], 1)

            ffn_xT(0, 0)
            ffn_h(0, 0, 0)
            ffn_xT(1, 1)

            def pair(ep, last):
                for aa in range(2):
                    for j in range(CPE):
                        i = aa * CPE + j
                        c = ep * (2 * CPE) + i
                        if not (last and i == 2 * CPE - 1):
                            ffn_h(ep * 2 + (i + 1) // CPE, c + 1, 1 - i % 2)
                        if j < 2 and not (last and aa == 1):
                            head(ep * 2 + 1 + aa, 1 - aa, j)
                        if not (last and i >= 2 * CPE - 2):
                            ffn_xT(c + 2, i % 2)

            pair(0, False)
            with act.Fori(1, NE // 2 - 1) as ep:
                pair(Count(ep), False)
            pair(NE // 2 - 1, True)

        @block.vector
        def _(dve):
            v = nc.vector
            nb1 = NE * MT
            dve.wait_ge(S["mask_loaded"], 16)
            for b in range(NB):
                ins = v.tensor_scalar(mb[:, b * TPB:(b + 1) * TPB, :], mraw, 0.0, NEG, ALU.is_equal, ALU.mult)
            ins.then_inc(S["mask_ready"], 1)
            dve.wait_ge(S["mask_ready"], 1)
            v.tensor_reduce(mmax[:], mb[:, 0:TPB, :], AX.X, ALU.max).then_inc(S["mask_ready"], 1)
            dve.wait_ge(S["mask_ready"], 2)
            for b in range(NB):
                v.tensor_scalar(live[:, b * TPB:(b + 1) * TPB], mmax[:], 0.0, None, ALU.is_equal)
                ins = v.tensor_scalar(dead[:, b * TPB:(b + 1) * TPB], mmax[:], 0.0, None, ALU.not_equal)
            ins.then_inc(S["mask_ready"], 2)
            dve.wait_ge(S["mask_ready"], 4)

            def stats(src, s_, m_, tag, n):
                for t in range(G):
                    v.bn_stats(s_[:, t, :], src(t)).then_inc(S[tag], 1)
                for t in range(G):
                    dve.wait_ge(S[tag], at(n * (2 * G) + 1 + t))
                    wait_apart(dve)
                    v.bn_aggr(m_[:, t, :], s_[:, t, :]).then_inc(S[tag], 1)

            def stats1(m):
                if isinstance(m, int):
                    dve.wait_ge(S["x_loaded"], 16 if m == 0 else 32)
                stats(lambda t: xs[:, at(m * G + t), :], st, mv, "stat_step", m)

            def norm1(m):
                dve.wait_ge(S["rstd_ready"], at(2 * (m + 1)))
                if later(m, 0):
                    dve.wait_ge(S["xT_ready"], at(m))
                for t in range(G):
                    v.tensor_scalar(xn[:, t, :], xs[:, at(m * G + t), :], mv[:, t, 0:1], rstd[:, t:t + 1],
                                    ALU.subtract, ALU.mult).then_inc(S["xn_ready"], 1)

            def rest_xT(m):
                dve.wait_ge(S["xT_split"], at(m + 1))
                if later(m, 0):
                    dve.wait_ge(S["q_ready"], at(m))
                v.tensor_tensor(xTl[:, 0, :], ps[:, MISC, :], xTh[:, 0, :].bitcast(F32),
                                ALU.subtract).then_inc(S["xT_rest"], 1)

            def rest_q(m):
                dve.wait_ge(S["q_split"], at(2 * (m + 1)))
                for r in range(KT):
                    v.scalar_tensor_tensor(out=ql[:, r, :], in0=misc(2)[:, r, :], scalar=bcol[:, nb1 + r:nb1 + r + 1],
                                           in1=qh[:, r, :].bitcast(F32), op0=ALU.add,
                                           op1=ALU.subtract).then_inc(S["q_rest"], 1)

            def diff(u, par):
                dve.wait_ge(S["sc_ready"], at(u + 1))
                sc = ps[:, SC + 2 * par:SC + 2 * par + 2, 0:W4].rearrange("p b (h k) -> p b h k", k=NK)
                v.tensor_reduce(mx[:, par, :].rearrange("p (b h) -> p b h", b=2), sc, AX.X,
                                ALU.max).then_inc(S["max_ready"], 1)
                dve.wait_ge(S["max_ready"], at(u + 1))
                if later(u, 1):
                    dve.wait_ge(S["pt_ready"], at(u - 1))
                v.tensor_tensor(pb[:, par, :].rearrange("p (b h k) -> p b h k", b=2, k=NK), sc,
                                mx[:, par, :].rearrange("p (b h) -> p b h", b=2).unsqueeze(3)
                                .to_broadcast([P, 2, HH // 2, NK]), ALU.subtract).then_inc(S["diff_ready"], 1)

            def rest_pt(u, par):
                dve.wait_ge(S["pth_ready"], at(u + 1))
                v.tensor_tensor(ptl[:, par, :].rearrange("p (b c) -> p b c", b=2), ps[0:NK, PT:PT + 2, :],
                                pth[:, par, :].rearrange("p (b c) -> p b c", b=2),
                                ALU.subtract).then_inc(S["ptl_ready"], 1)

            def gather_o(u, n, j):
                dve.wait_ge(S["pv_ready"], at(u + 1))
                if later(u, 0):
                    dve.wait_ge(S["o_half"], at(u))
                pv = ps[:, PV, 0:HH * VW].rearrange("p (h c) -> p h c", h=HH)
                v.tensor_reduce(osum[:].rearrange("p (h d) -> p h d", h=HH),
                                pv[:, :, 0:3 * DH].rearrange("p h (s d) -> p h d s", s=3), AX.X,
                                ALU.add).then_inc(S["osum_part"], 1)
                v.reciprocal(rinv[:], pv[:, :, 3 * DH]).then_inc(S["osum_ready"], 1)
                dve.wait_ge(S["osum_part"], at(u + 1))
                dve.wait_ge(S["osum_ready"], at(u + 1))
                if j == 0 and (later(n, 0)):
                    dve.wait_ge(S["oT_ready"], at(n))
                t, half = j // 2, j % 2
                v.scalar_tensor_tensor(
                    out=o[:, t, half * HH * DH:(half + 1) * HH * DH].rearrange("p (h d) -> p h d", h=HH),
                    in0=osum[:].rearrange("p (h d) -> p h d", h=HH), scalar=live[:, bass.ds(at(n * G + t), 1)],
                    in1=rinv[:].unsqueeze(2).to_broadcast([P, HH, DH]), op0=ALU.mult,
                    op1=ALU.mult).then_inc(S["o_half"], 1)

            stats1(0)
            norm1(0)
            dve.wait_ge(S["act_setup"], 1)
            v.tensor_tensor(wql.rearrange("p k d -> p (k d)"), ps[:, 0, :],
                            wqh.rearrange("p k d -> p (k d)").bitcast(F32), ALU.subtract).then_inc(S["dve_setup"], 1)
            dve.wait_ge(S["pe_setup"], 7)
            dve.wait_ge(S["act_setup"], 5)
            for r in range(KT):
                ins = v.tensor_scalar(ktf[:, r, :], ps[:, 6, r * NB * NK:(r + 1) * NB * NK],
                                      bcol[:, nb1 + KT + r:nb1 + KT + r + 1], DH ** -0.5, ALU.add, ALU.mult)
            ins.then_inc(S["dve_setup"], 1)
            dve.wait_ge(S["dve_setup"], 2)
            dve.wait_ge(S["const_ready"], 2)
            kw = wraw[:, 0:NB * KT * UC].rearrange("p (b r h k) -> p b r h k", b=NB, r=KT, h=HH)
            for b in range(NB):
                for r in range(KT):
                    ins = v.tensor_tensor(kw[:, b, r], ktf[:, r, b * NK:(b + 1) * NK].unsqueeze(1).to_broadcast([P, HH, NK]),
                                          blockh[:].unsqueeze(2).to_broadcast([P, HH, NK]), ALU.mult)
            ins.then_inc(S["dve_setup"], 1)
            dve.wait_ge(S["dve_setup"], 3)
            kflat = wraw[:, 0:NB * KT * UC]
            kbh_f = hh[:].rearrange("p a b -> p (a b)")[:, 0:NB * KT * UC]
            kbl_f = hl[:].rearrange("p a b -> p (a b)")[:, 0:NB * KT * UC]
            v.tensor_copy(kbh_f, kflat).then_inc(S["dve_setup"], 1)
            dve.wait_ge(S["dve_setup"], 4)
            v.tensor_tensor(kbl_f, kflat, kbh_f.bitcast(F32), ALU.subtract).then_inc(S["dve_setup"], 1)
            rest_xT(0)
            dve.wait_ge(S["pe_setup"], 8)
            dve.wait_ge(S["small_loaded"], at(16 * 7))
            v.tensor_tensor(vf.rearrange("p (b d) -> p b d", b=NB), ps[0:NK, 3, :].rearrange("p (b d) -> p b d", b=NB),
                            bv_b[:].unsqueeze(1).to_broadcast([NK, NB, D]), ALU.add).then_inc(S["dve_setup"], 1)
            dve.wait_ge(S["dve_setup"], 6)

            def vpart(i):
                return vcat[:, :, :, i * DH:(i + 1) * DH]

            def vview(t_):
                return t_.rearrange("p (b h d) -> p b h d", b=NB, h=NH)

            v.tensor_copy(vpart(0), vview(vf)).then_inc(S["vpart_step"], 1)
            dve.wait_ge(S["vpart_step"], 1)
            for b in range(NB):
                ins = v.tensor_tensor(vview(vrest[:, 0, :])[:, b], vview(vf)[:, b], vpart(0)[:, b], ALU.subtract)
            ins.then_inc(S["vpart_step"], 1)
            dve.wait_ge(S["vpart_step"], 2)
            v.tensor_copy(vpart(1), vview(vrest[:, 0, :])).then_inc(S["vpart_step"], 1)
            dve.wait_ge(S["vpart_step"], 3)
            for b in range(NB):
                ins = v.tensor_tensor(vview(vrest[:, 1, :])[:, b], vview(vrest[:, 0, :])[:, b], vpart(1)[:, b], ALU.subtract)
            ins.then_inc(S["vpart_step"], 1)
            dve.wait_ge(S["vpart_step"], 4)
            v.tensor_copy(vpart(2), vview(vrest[:, 1, :])).then_inc(S["dve_setup"], 1)
            rest_q(0)
            dve.wait_ge(S["act_setup"], 6)
            v.tensor_tensor(wol.rearrange("p k d -> p (k d)"), ps[:, 5, :],
                            woh.rearrange("p k d -> p (k d)").bitcast(F32), ALU.subtract)
            dve.wait_ge(S["pe_setup"], 9)
            v.tensor_copy(vmean[:].rearrange("p b d -> p (b d)"), ps[:, 4, :]).then_inc(S["dve_setup"], 1)
            diff(0, 0)

            def body(m):
                units, qn, tail, slots = parts(m)
                if tail:
                    gather_o(4 * m - 1, m - 1, 3)
                if qn:
                    stats1(m + 1)
                if units:
                    diff(4 * m + 1, 1)
                if qn:
                    norm1(m + 1)
                if units:
                    rest_pt(4 * m, 0)
                if qn:
                    rest_xT(m + 1)
                if slots:
                    n = m - 2
                    dve.wait_ge(S["pos_ready"], at(n + 1))
                    v.tensor_tensor(slotv[:], ps[:, MISC, 0:G * NE].rearrange("p (t e) -> p t e", t=G),
                                    base_e[:].unsqueeze(1).to_broadcast([P, G, NE]), ALU.add).then_inc(S["slot_ready"], 1)
                if tail:
                    dve.wait_ge(S["oT_split"], at(m))
                    v.tensor_tensor(oTl, ps[:, MISC, :], oTh.bitcast(F32), ALU.subtract).then_inc(S["oT_rest"], 1)
                if units:
                    diff(4 * m + 2, 0)
                if slots:
                    n = m - 2
                    dve.wait_ge(S["pick_ready"], at(2 * (n + 1)))
                    v.tensor_reduce(sk[:], pick[:], AX.X, ALU.add).then_inc(S["sk_ready"], 1)
                if units:
                    rest_pt(4 * m + 1, 1)
                    gather_o(4 * m, m, 0)
                    diff(4 * m + 3, 1)
                if tail:
                    n = m - 1
                    dve.wait_ge(S["wo_ready"], at(m))
                    dve.wait_ge(S["xbo_ready"], at(m))
                    v.tensor_tensor(xs[:, bass.ds(at(n * G), G), :], misc(2)[:, :, :], xbo[:], ALU.add).then_inc(S["x1_ready"], 1)
                    dve.wait_ge(S["x1_ready"], at(m))
                    wait_apart(dve)
                    stats(lambda t: xs[:, at(n * G + t), :], st2, mv2, "stat2_step", n)
                if units:
                    rest_pt(4 * m + 2, 0)
                    gather_o(4 * m + 1, m, 1)
                if tail:
                    dve.wait_ge(S["rstd2_ready"], at(2 * m))
                    if later(n, 0):
                        dve.wait_ge(S["x2T_ready"], at(n))
                        dve.wait_ge(S["scattered"], at(64 * n))
                    for t in range(G):
                        v.tensor_scalar(xn2[:, t, :], xs[:, at(n * G + t), :], mv2[:, t, 0:1], rstd2[:, t:t + 1],
                                        ALU.subtract, ALU.mult).then_inc(S["xn2_ready"], 1)
                if qn:
                    rest_q(m + 1)
                    diff(4 * m + 4, 0)
                if units:
                    rest_pt(4 * m + 3, 1)
                    gather_o(4 * m + 2, m, 2)
                if tail:
                    n = m - 1
                    dve.wait_ge(S["lg_ready"], at(m))
                    v.tensor_copy(lg[:], ps[:, MISC, 0:G * NE].rearrange("p (t e) -> p t e", t=G)).then_inc(S["lg_copied"], 1)
                    dve.wait_ge(S["lg_copied"], at(m))
                    wait_apart(dve)
                    for t in range(G):
                        v.max(top[:, t, :], lg[:, t, :]).then_inc(S["top_ready"], 1)
                    dve.wait_ge(S["top_ready"], at(2 * m))
                    v.tensor_copy(top2[:, bass.ds(at(n * G), G), :], top[:, :, 0:2])
                    for t in range(G):
                        ins = v.max_index(tix[:, t, :], top[:, t, :], lg[:, t, :])
                    ins.then_inc(S["tix_ready"], 1)
                    dve.wait_ge(S["tix_ready"], at(2 * m - 1))
                    if later(n, 0):
                        dve.wait_ge(S["route_step"], at(11 * n - 8))
                    v.tensor_copy(ek[:], tix[:, :, 0:2]).then_inc(S["tix_ready"], 1)
                    dve.wait_ge(S["tix_ready"], at(2 * m))
                    if later(n, 0):
                        dve.wait_ge(S["pick_ready"], at(2 * n))
                    for t in range(G):
                        v.tensor_tensor(oh[:, t], ek[:, t, :].unsqueeze(2).to_broadcast([P, 2, NE]),
                                        iota_e[:].unsqueeze(1).to_broadcast([P, 2, NE]),
                                        ALU.is_equal).then_inc(S["oh_ready"], 1)

            macro_loop(dve, body)

            dve.wait_ge(S["route_step"], at(11 * NM))
            v.tensor_tensor(gd[:], top2[:, :, 1], top2[:, :, 0], ALU.subtract).then_inc(S["gate_step"], 1)

            def gates():
                dve.wait_ge(S["gate_exp"], 1)
                v.tensor_scalar(g1[:], ge[:], 1.0, None, ALU.add).then_inc(S["gate_step"], 1)
                dve.wait_ge(S["gate_step"], 2)
                v.reciprocal(g1[:], g1[:]).then_inc(S["gate_step"], 1)
                dve.wait_ge(S["gate_step"], 3)
                v.tensor_tensor(ge[:], ge[:], g1[:], ALU.mult).then_inc(S["gate_step"], 1)
                dve.wait_ge(S["gate_step"], 4)
                v.tensor_tensor(gate[:, :, 0], g1[:], keep[:, :, 0], ALU.mult)
                v.tensor_tensor(gate[:, :, 1], ge[:], keep[:, :, 1], ALU.mult).then_inc(S["gate_ready"], 1)

            def ffn_xT(c, par):
                dve.wait_ge(S["fxT_head"], at(c + 1))
                v.tensor_tensor(xTl[:, par, :], ps[:, 6, :], xTh[:, par, :].bitcast(F32),
                                ALU.subtract).then_inc(S["fxT_rest"], 1)

            def ffn_h(c, par):
                for i in range(MT // 2):
                    dve.wait_ge(S["h_head"], at(c * (MT // 2) + i + 1))
                    v.tensor_tensor(hl[:, par, 2 * i * CH:2 * (i + 1) * CH], hf[:, i % 2, :],
                                    hh[:, par, 2 * i * CH:2 * (i + 1) * CH].bitcast(F32),
                                    ALU.subtract).then_inc(S["h_rest"], 1)

            def ffn_y(e, c, par, half):
                dve.wait_ge(S["y_ready"], at(c + 1))
                if later(c, 1):
                    dve.wait_ge(S["y_stored%d" % par], at(half * 16))
                v.tensor_tensor(yb[:, par], ps[:, 4 + par, :].rearrange("p (t d) -> p t d", t=G),
                                b2_b[:, at(e), :].unsqueeze(1).to_broadcast([P, G, D]), ALU.add).then_inc(S["y_copied"], 1)

            ffn_xT(0, 0)
            ffn_h(0, 0)
            ffn_xT(1, 1)

            def pair(ep, last):
                for aa in range(2):
                    for j in range(CPE):
                        i = aa * CPE + j
                        c = ep * (2 * CPE) + i
                        if not (last and i == 2 * CPE - 1):
                            ffn_h(c + 1, 1 - i % 2)
                        if not (last and i >= 2 * CPE - 2):
                            ffn_xT(c + 2, i % 2)
                        ffn_y(ep * 2 + aa, c, i % 2, ep * CPE + i // 2)

            pair(0, False)
            with dve.Fori(1, NE // 2 - 1) as ep:
                pair(Count(ep), False)
            pair(NE // 2 - 1, True)
            gates()
            dve.wait_ge(S["gate_ready"], 1)
            for t in range(NT):
                dve.wait_ge(S["gath%d" % (t % 3)], at(32 * (t // 3 + 1)))
                v.scalar_tensor_tensor(out=xs[:, t, :], in0=ga[:, t % 3, 0, :], scalar=gate[:, t, 0:1],
                                       in1=xs[:, t, :], op0=ALU.mult, op1=ALU.add).then_inc(S["fin_step"], 1)
                dve.wait_ge(S["fin_step"], at(t + 1))
                if t >= 2:
                    dve.wait_ge(S["fin_stored%d" % (t % 2)], at(16 * (t // 2)))
                v.scalar_tensor_tensor(out=fin[:, t % 2, :], in0=ga[:, t % 3, 1, :], scalar=gate[:, t, 1:2],
                                       in1=xs[:, t, :], op0=ALU.mult, op1=ALU.add).then_inc(S["fin_ready"], 1)

        @block.tensor
        def _(pe):
            T = nc.tensor

            def mm3(dst, sh, sl, mh, ml, first, last):
                T.matmul(dst, sh, mh, start=first, stop=False)
                T.matmul(dst, sh, ml, start=False, stop=False)
                return T.matmul(dst, sl, mh, start=False, stop=last)

            pe.wait_ge(S["const_ready"], 2)

            def turn_weight(w, b):
                for k in range(KT):
                    for r in range(KT):
                        ins = T.transpose(ps[:, b, k * D + r * P:k * D + (r + 1) * P],
                                          wnat[:, w, r, k * P:(k + 1) * P], identf[:])
                ins.then_inc(S["pe_setup"], 1)

            pe.wait_ge(S["w_loaded"], at(16 * 5))
            turn_weight(0, 0)
            turn_weight(1, 1)
            for k in range(KT):
                for b in range(NB):
                    ins = T.transpose(ps[:, 2, (k * NB + b) * NK:(k * NB + b + 1) * NK],
                                      cnat[:, b, k * P:(k + 1) * P], identf[0:NK, 0:NK])
            ins.then_inc(S["pe_setup"], 1)
            turn_weight(2, 3)
            nrow = NE * MT + 2 * KT
            pe.wait_ge(S["small_loaded"], at(16 * 7))
            T.transpose(ps[:, 4, 0:nrow], brow[:], identf[0:nrow, 0:nrow]).then_inc(S["pe_setup"], 1)
            turn_weight(3, 5)
            pe.wait_ge(S["act_setup"], 3)
            for r in range(KT):
                for k in range(KT):
                    ins = T.matmul(ps[:, 6, r * NB * NK:(r + 1) * NB * NK], wkT[:, k, r * P:(r + 1) * P], cT[:, k, :],
                                   start=(k == 0), stop=(k == KT - 1))
            ins.then_inc(S["pe_setup"], 1)
            pe.wait_ge(S["act_setup"], 4)
            for b in range(NB):
                for k in range(KT):
                    ins = T.matmul(ps[0:NK, 3, b * D:(b + 1) * D], cT[:, k, b * NK:(b + 1) * NK], wvT[:, k, :],
                                   start=(k == 0), stop=(k == KT - 1))
            ins.then_inc(S["pe_setup"], 1)

            def turn_xn(m):
                pe.wait_ge(S["xn_ready"], at(2 * (m + 1)))
                if later(m, 0):
                    pe.wait_ge(S["q_rest"], at(2 * m))
                if later(m, 2):
                    pe.wait_ge(S["lg_copied"], at(m - 2))
                for k in range(KT):
                    for t in range(G):
                        ins = T.transpose(ps[:, MISC, k * GT + t * P:k * GT + (t + 1) * P],
                                          xn[:, t, k * P:(k + 1) * P], identf[:])
                ins.then_inc(S["xT_ready"], 1)

            def project_q(m):
                pe.wait_ge(S["xT_rest"], at(m + 1))
                if later(m, 1):
                    pe.wait_ge(S["x1_ready"], at(m - 1))
                for r in range(KT):
                    for k in range(KT):
                        ks = slice(k * GT, (k + 1) * GT)
                        rs = slice(r * P, (r + 1) * P)
                        ins = mm3(misc(2)[:, r, :], wqh[:, k, rs], wql[:, k, rs], xTh[:, 0, ks], xTl[:, 0, ks],
                                  k == 0, k == KT - 1)
                ins.then_inc(S["q_ready"], 1)

            def scores(m, j, par):
                t, half = j // 2, j % 2
                if j == 0:
                    pe.wait_ge(S["q_rest"], at(2 * (m + 1)))
                if later(4 * m + j, 1):
                    pe.wait_ge(S["diff_ready"], at(4 * m + j - 1))
                ts = slice(t * P, (t + 1) * P)
                b = batch_of(m)
                for w in range(2):
                    dst = ps[:, SC + 2 * par + w, 0:W4]
                    T.matmul(dst, identb[:], mb[:, at(m * G + t), :].unsqueeze(1).to_broadcast([P, HH // 2, NK]),
                             start=True, stop=False)
                    cs = slice(w * W4, (w + 1) * W4)
                    ins = mm3(dst, qh[:, half, ts], ql[:, half, ts], kbh[:, b, half, cs], kbl[:, b, half, cs],
                              False, True)
                ins.then_inc(S["sc_ready"], 1)

            def turn_p(u, par):
                pe.wait_ge(S["exp_ready"], at(u + 1))
                if later(u, 0):
                    pe.wait_ge(S["ptl_ready"], at(u))
                for h in range(HH):
                    ins = T.transpose(ps[0:NK, PT + h // 4, (h % 4) * P:(h % 4 + 1) * P],
                                      pb[:, par, h * NK:(h + 1) * NK], identf[:])
                ins.then_inc(S["pt_ready"], 1)

            def times_v(m, j, par):
                u = 4 * m + j
                pe.wait_ge(S["ptl_ready"], at(u + 1))
                if later(u, 0):
                    pe.wait_ge(S["osum_ready"], at(u))
                half = j % 2
                b = batch_of(m)
                for h in range(HH):
                    dst = ps[:, PV, h * VW:(h + 1) * VW]
                    rhs = vcat[:, b, half * HH + h, :]
                    T.matmul(dst, pth[:, par, h * P:(h + 1) * P], rhs, start=True, stop=False)
                    ins = T.matmul(dst, ptl[:, par, h * P:(h + 1) * P], rhs, start=False, stop=True)
                ins.then_inc(S["pv_ready"], 1)

            turn_xn(0)
            pe.wait_ge(S["dve_setup"], 1)
            project_q(0)
            pe.wait_ge(S["dve_setup"], 6)
            pe.wait_ge(S["act_setup"], 5)
            T.matmul(ps[:, 4, :], inv_nk[:], vf, start=True, stop=True).then_inc(S["pe_setup"], 1)
            pe.wait_ge(S["mask_ready"], 1)
            pe.wait_ge(S["dve_setup"], 7)
            scores(0, 0, 0)

            def body(m):
                units, qn, tail, slots = parts(m)
                if tail:
                    times_v(m - 1, 3, 1)
                if units:
                    if isinstance(m, int) and m == 0:
                        pe.wait_ge(S["dve_setup"], 8)
                    scores(m, 1, 1)
                    turn_p(4 * m, 0)
                if qn:
                    turn_xn(m + 1)
                if slots:
                    n = m - 2
                    pe.wait_ge(S["run_ready"], at(n + 1))
                    pe.wait_ge(S["xT_rest"], at(at_most(m + 2, NM)))
                    pe.wait_ge(S["lg_copied"], at(m - 1))
                    for t in range(G):
                        dst = ps[:, MISC, t * NE:(t + 1) * NE]
                        T.matmul(dst, before[:], ohs[:, t, :], start=True, stop=False)
                        ins = T.matmul(dst, onesb[:], run[:, t, :], start=False, stop=True)
                    ins.then_inc(S["pos_ready"], 1)
                if tail:
                    pe.wait_ge(S["o_ready"], at(m))
                    pe.wait_ge(S["xT_rest"], at(at_most(m + 2, NM)))
                    if slots:
                        pe.wait_ge(S["slot_ready"], at(m - 1))
                    for k in range(KT):
                        for t in range(G):
                            ins = T.transpose(ps[:, MISC, k * GT + t * P:k * GT + (t + 1) * P],
                                              o[:, t, k * P:(k + 1) * P], identf[:])
                    ins.then_inc(S["oT_ready"], 1)
                if units:
                    scores(m, 2, 0)
                    turn_p(4 * m + 1, 1)
                    times_v(m, 0, 0)
                    scores(m, 3, 1)
                if tail:
                    pe.wait_ge(S["oT_rest"], at(m))
                    for t in range(G):
                        for k in range(KT):
                            ks = slice(k * GT + t * P, k * GT + (t + 1) * P)
                            ins = mm3(misc(2)[:, t, :], oTh[:, ks], oTl[:, ks], woh[:, k, :], wol[:, k, :],
                                      k == 0, k == KT - 1)
                    ins.then_inc(S["wo_ready"], 1)
                if units:
                    turn_p(4 * m + 2, 0)
                    times_v(m, 1, 1)
                if qn:
                    project_q(m + 1)
                    scores(m + 1, 0, 0)
                if tail:
                    pe.wait_ge(S["xn2_ready"], at(2 * m))
                    pe.wait_ge(S["q_rest"], at(2 * at_most(m + 2, NM)))
                    pe.wait_ge(S["x1_ready"], at(m))
                    for k in range(KT):
                        for t in range(G):
                            ins = T.transpose(ps[:, MISC, k * GT + t * P:k * GT + (t + 1) * P],
                                              xn2[:, t, k * P:(k + 1) * P], identf[:])
                    ins.then_inc(S["x2T_ready"], 1)
                if units:
                    turn_p(4 * m + 3, 1)
                    times_v(m, 2, 0)
                if tail:
                    pe.wait_ge(S["x2T_copied"], at(m))
                    for t in range(G):
                        for k in range(KT):
                            ins = T.matmul(ps[:, MISC, t * NE:(t + 1) * NE], x2T[:, k * GT + t * P:k * GT + (t + 1) * P],
                                           wr[:, k, :], start=(k == 0), stop=(k == KT - 1))
                    ins.then_inc(S["lg_ready"], 1)

            macro_loop(pe, body)

            def turn_x(c, par, half):
                pe.wait_ge(S["xc_loaded%d" % par], at((half + 1) * 16))
                if later(c, 0):
                    pe.wait_ge(S["fxT_rest"], at(c))
                for k in range(KT):
                    for t in range(G):
                        ins = T.transpose(ps[:, 6, k * CH + t * P:k * CH + (t + 1) * P],
                                          xc[:, par, t, k * P:(k + 1) * P], identf[:])
                ins.then_inc(S["fxT_ready"], 1)

            def hidden(e, c, par, epar, first_of_expert):
                pe.wait_ge(S["fxT_rest"], at(c + 1))
                if first_of_expert:
                    pe.wait_ge(S["w_rest"], at(2 * e + 1))
                for i in range(MT // 2):
                    if later(c, 0):
                        pe.wait_ge(S["h_relu"], at((c - 1) * (MT // 2) + i + 1))
                    for s in range(2):
                        for k in range(KT):
                            ws = slice(k * HID + (2 * i + s) * P, k * HID + (2 * i + s + 1) * P)
                            ks = slice(k * CH, (k + 1) * CH)
                            ins = mm3(ps[:, i, s * CH:(s + 1) * CH], wh[:, epar, ws], wl[:, epar, ws],
                                      xTh[:, par, ks], xTl[:, par, ks], k == 0, k == KT - 1)
                    ins.then_inc(S["h_ready"], 1)

            def output(e, c, par, epar, first_of_expert):
                pe.wait_ge(S["h_rest"], at((c + 1) * (MT // 2)))
                if first_of_expert:
                    pe.wait_ge(S["w_rest"], at(2 * e + 2))
                if later(c, 1):
                    pe.wait_ge(S["y_copied"], at(c - 1))
                for t in range(G):
                    for k in range(MT):
                        hs = slice(k * CH + t * P, k * CH + (t + 1) * P)
                        w2s = slice(KT * HID + k * D, KT * HID + (k + 1) * D)
                        ins = mm3(ps[:, 4 + par, t * D:(t + 1) * D], hh[:, par, hs], hl[:, par, hs],
                                  wh[:, epar, w2s], wl[:, epar, w2s], k == 0, k == MT - 1)
                ins.then_inc(S["y_ready"], 1)

            turn_x(0, 0, 0)
            hidden(0, 0, 0, 0, True)
            turn_x(1, 1, 0)

            def pair(ep, last):
                for aa in range(2):
                    for j in range(CPE):
                        i = aa * CPE + j
                        c = ep * (2 * CPE) + i
                        if not (last and i == 2 * CPE - 1):
                            hidden(ep * 2 + (i + 1) // CPE, c + 1, 1 - i % 2, ((i + 1) // CPE) % 2, (i + 1) % CPE == 0)
                        if not (last and i >= 2 * CPE - 2):
                            turn_x(c + 2, i % 2, ep * CPE + (i + 2) // 2)
                        output(ep * 2 + aa, c, i % 2, aa, j == 0)

            pair(0, False)
            with pe.Fori(1, NE // 2 - 1) as ep:
                pair(Count(ep), False)
            pair(NE // 2 - 1, True)


_INS = ["x", "ctx_1024", "mask_1x1xSxS2_ik0", "L0_xattn_Wq", "L0_xattn_bq", "L0_xattn_Wk", "L0_xattn_bk",
        "L0_xattn_Wv", "L0_xattn_bv", "L0_xattn_Wo", "L0_xattn_bo", "L0_ffn_w_router", "L0_ffn_w1", "L0_ffn_b1",
        "L0_ffn_w2", "L0_ffn_b2"]


def kernel(**inputs):
    import numpy as np
    import concourse.bacc as bacc
    from concourse.bass_utils import run_bass_kernel_spmd

    nc = bacc.Bacc("TRN2", target_bir_lowering=False, num_devices=1)
    arrays, args = {}, []
    for name in _INS:
        a = np.ascontiguousarray(inputs[name])
        arrays[f"in_{name}"] = a
        args.append(nc.dram_tensor(f"in_{name}", a.shape, mybir.dt.from_np(a.dtype), kind="ExternalInput").ap())
    out = nc.dram_tensor("out_0", inputs["x"].shape, F32, kind="ExternalOutput").ap()
    xattn_moe_kernel(nc, *args, out)
    r = run_bass_kernel_spmd(nc, [arrays], core_ids=[0])
    return r.results[0]["out_0"]
```

```python
from contextlib import ExitStack

import concourse.bass as bass
from concourse import mybir

ALU = mybir.AluOpType
ACT = mybir.ActivationFunctionType
AX = mybir.AxisListType
F32 = mybir.dt.float32
F32R = mybir.dt.float32r
F16 = mybir.dt.float16
BF16 = mybir.dt.bfloat16
I32 = mybir.dt.int32
U32 = mybir.dt.uint32

P = 128
NEG = -1.0e30
EPS = 1e-5


class Count:

    def __init__(self, reg, scale=1, offset=0):
        self.reg, self.scale, self.offset = reg, scale, offset

    def __add__(self, n):
        return Count(self.reg, self.scale, self.offset + n)

    def __sub__(self, n):
        return self + -n

    def __mul__(self, n):
        return Count(self.reg, self.scale * n, self.offset * n)

    __radd__, __rmul__ = __add__, __mul__


def at(n):
    if isinstance(n, int):
        return n
    v = n.reg * n.scale if n.scale != 1 else n.reg
    return v + n.offset if n.offset else v


def later(n, first):
    return not isinstance(n, int) or n > first


def at_most(n, top):
    return max(0, min(n, top)) if isinstance(n, int) else n


def xattn_moe_kernel(nc, x, ctx_in, mask, Wq, bq, Wk, bk, Wv, bv, Wo, bo, w_router, w1, b1, w2, b2, out):
    NB, SQ, D = x.shape
    NK = ctx_in.shape[1]
    NE, _, HID = w1.shape
    NH = 16
    DH = D // NH
    KT = D // P
    MT = HID // P
    NTOK = NB * SQ
    NT = NTOK // P
    TPB = SQ // P
    G = 2
    GT = G * P
    NM = NT // G
    MPB = TPB // G
    HK = P // DH
    HU = 4
    UPT = NH // HU
    UPM = G * UPT
    CAP = int(1.5 * NTOK * 2 / NE)
    CH = 256
    CPE = CAP // CH
    NCH = NE * CPE
    SLOTS = NE * CAP
    VW = 3 * DH + 1
    UC = HU * NK
    KC = HK * NK

    x_v = x.rearrange("b (t p) d -> p (b t) d", p=P)
    out_v = out.rearrange("b (t p) d -> p (b t) d", p=P)
    mask_v = mask.rearrange("a b (t p) k -> p (a b t) k", p=P)
    xe = nc.dram_tensor("expert_in", (SLOTS + 2 * NTOK, D), F32, kind="Internal").ap()
    eo = nc.dram_tensor("expert_out", (SLOTS, D), F32, kind="Internal").ap()
    xe_v = xe[0:SLOTS, :].rearrange("(c t p) d -> p c t d", t=G, p=P)
    eo_v = eo.rearrange("(c t p) d -> p c t d", t=G, p=P)

    with ExitStack() as es:
        def sb(name, shape, dt=F32):
            return es.enter_context(nc.sbuf_tensor(name, shape, dt))

        def sem(name):
            return es.enter_context(nc.semaphore(name))

        shared = sb("shared", [P, 5 * 2 * GT * KT])

        def piece(at_, parts_, *shape):
            n = 1
            for k in shape:
                n *= k
            v = shared[0:parts_, at_:at_ + n]
            if len(shape) == 2:
                return v.rearrange("p (a b) -> p a b", a=shape[0])
            if len(shape) == 3:
                return v.rearrange("p (a b c) -> p a b c", a=shape[0], b=shape[1])
            return v

        wnat = piece(0, P, 4, KT, D)
        cnat = piece(2048, NK, NB, D)
        wkT = piece(2560, P, KT, D)
        wvT = piece(3072, P, KT, D)
        vrest = piece(3584, NK, 2, NB * D)
        vf = piece(4608, NK, NB * D)
        hf = piece(0, P, 2, 2 * CH)
        xc = piece(1024, P, 2, G, D)
        yb = piece(2048, P, 2, G, D)
        GR = 6
        ga = piece(3072, P, GR, D)
        fin = piece(4608, P, 2, D)
        rows = piece(0, P, G, D)
        wh = sb("wh", [P, 2, 2 * KT * HID], F32R)

        def early(i, flat=False):
            v = wh[:, 1, i * KT * D:(i + 1) * KT * D]
            return v if flat else v.rearrange("p (k d) -> p k d", k=KT)

        wqh, wql, woh, wol, qh, ql = (early(i) for i in range(6))
        oTh, oTl = early(6, True), early(7, True)
        pb = sb("pb", [P, 2, UC])
        mraw = pb[:].rearrange("p a b -> p (a b)")[:, 0:TPB * NK].bitcast(I32).rearrange("p (t k) -> p t k", t=TPB)
        zrow = sb("zrow", [P, D])
        identf = sb("identf", [P, P])
        identb = sb("identb", [P, P], BF16)
        before = sb("before", [P, P], BF16)
        onesb = sb("onesb", [P, P], BF16)
        blockh = sb("blockh", [P, HK])
        mhalf = sb("mhalf", [P, G])
        iota_e = sb("iota_e", [P, NE])
        base_e = sb("base_e", [P, NE])
        dump = sb("dump", [P, NT, 2])
        xs = sb("xs", [P, NT, D])
        brow = sb("brow", [NE * MT + 2 * KT, P])
        bcol = sb("bcol", [P, NE * MT + 2 * KT])
        bo_b = sb("bo_b", [P, D])
        bv_b = sb("bv_b", [NK, D])
        b2_b = sb("b2_b", [P, NE, D])
        wr = sb("wr", [P, KT, NE])
        cT = sb("cT", [P, KT, NB * NK])
        ktf = sb("ktf", [P, KT, NB * NK])
        kth = sb("kth", [P, KT, NB * NK], F32R)
        ktl = sb("ktl", [P, KT, NB * NK])
        vcat = sb("vcat", [NK, NB, NH, VW], BF16)
        mb = sb("mb", [P, NT, NK], BF16)
        st = sb("st", [P, G, 6])
        mv = sb("mv", [P, G, 2])
        rstd = sb("rstd", [P, G])
        xn = sb("xn", [P, G, D])
        xTh = sb("xTh", [P, 2, KT * GT], F32R)
        xTl = sb("xTl", [P, 2, KT * GT], F32R)
        nmx = sb("nmx", [P, 2, HU])
        pth = sb("pth", [NK, 2, HU * P], F16)
        ptl = sb("ptl", [NK, 2, HU * P], F16)
        osum = sb("osum", [P, HU * DH])
        rinv = sb("rinv", [P, HU])
        o = sb("o", [P, G, D])
        xbo = sb("xbo", [P, G, D])
        st2 = sb("st2", [P, G, 6])
        mv2 = sb("mv2", [P, G, 2])
        rstd2 = sb("rstd2", [P, G])
        xn2 = sb("xn2", [P, G, D])
        x2T = sb("x2T", [P, KT * GT])
        lg = sb("lg", [P, G, NE])
        top = sb("top", [P, G, 8])
        tix = sb("tix", [P, G, 8], U32)
        ek = sb("ek", [P, G, 2])
        oh = sb("oh", [P, G, 2, NE])
        ohs = sb("ohs", [P, G, NE], BF16)
        run = sb("run", [P, 2, NE], BF16)
        slotv = sb("slotv", [P, G, NE])
        pick = sb("pick", [P, G, 2, NE])
        sk = sb("sk", [P, G, 2])
        eb = sb("eb", [P, G, 2])
        pos = sb("pos", [P, G, 2])
        kp = sb("kp", [P, G, 2])
        t1 = sb("t1", [P, G, 2])
        t2 = sb("t2", [P, G, 2])
        sidx = sb("sidx", [P, G, 2], I32)
        gslot = sb("gslot", [P, NT, 2])
        gidx = sb("gidx", [P, NT, 2], I32)
        swap = sb("swap", [P, NT])
        noswap = sb("noswap", [P, NT])
        gw = sb("gw", [P, NT, 2])
        gx = sb("gx", [P, NT, 2])
        keep = sb("keep", [P, NT, 2])
        top2 = sb("top2", [P, NT, 2])
        gd = sb("gd", [P, NT])
        ge = sb("ge", [P, NT])
        g1 = sb("g1", [P, NT])
        gate = sb("gate", [P, NT, 2])
        wraw = sb("wraw", [P, 2 * KT * HID])
        wl = sb("wl", [P, 2, 2 * KT * HID], F32R)
        hh = sb("hh", [P, 2, MT * CH], F32R)
        hl = sb("hl", [P, 2, MT * CH], F32R)
        kbh = hh[:].rearrange("p a b -> p (a b)")[:, 0:NB * KT * KC].rearrange("p (b r c) -> p b r c", b=NB, r=KT)
        kbl = hl[:].rearrange("p a b -> p (a b)")[:, 0:NB * KT * KC].rearrange("p (b r c) -> p b r c", b=NB, r=KT)

        ps = es.enter_context(nc.psum_tensor("ps", [P, 8, 512], F32))
        SC, PT, PV, TR, QB, WB = 0, 2, 4, 5, 6, 7

        def bank(i, k):
            return ps[:, i, :].rearrange("p (a b) -> p a b", a=k)

        S = {n: sem(n) for n in (
            "const_ready", "const_step", "x_loaded", "w_loaded", "w2_loaded", "small_loaded", "b2_loaded", "bias_loaded", "kb_head", "kb_rest", "v_split", "mask_loaded",
            "pe_setup", "act_setup", "dve_setup", "mask_ready",
            "xT_ready", "q_ready", "sc_ready", "pt_ready", "pv_ready", "oT_ready", "wo_ready", "x2T_ready",
            "lg_ready", "pos_ready",
            "stat_step", "rstd_ready", "rstd2_ready", "xn_ready", "xT_split", "xT_rest", "q_split", "q_rest", 
            "max_ready", "exp_ready",
            "pth_ready", "ptl_ready", "o_done", "oT_split", "oT_rest",
            "xbo_ready", "x1_ready", "stat2_step", "xn2_ready", "x2T_copied",
            "lg_copied", "top_ready", "tix_ready", "route_step", "oh_ready", "run_ready", "slot_ready", "pick_ready",
            "sk_ready", "scattered", "zero_done", "rows_ready", "osum_part", "vpart_step",
            "wraw_loaded0", "wraw_loaded1", "w_head", "w_rest", "xc_loaded0", "xc_loaded1", "fxT_ready", "fxT_head", "fxT_rest",
            "h_ready", "h_relu", "h_head", "h_rest", "y_ready", "y_copied", "y_stored0", "y_stored1",
            "gate_step", "gate_exp", "gate_ready", "gidx_step", "gidx_ready", "lower_added", "fin_ready",
            "fin_stored0", "fin_stored1",
        )}
        S.update({"gath%d" % i: sem("gath%d" % i) for i in range(GR)})

        block = es.enter_context(nc.Block())

        def vpart(i):
            return vcat[:, :, :, i * DH:(i + 1) * DH]

        def vview(t_):
            return t_.rearrange("p (b h d) -> p b h d", b=NB, h=NH)

        def macro_loop(eng, body):
            body(0)
            body(1)
            with eng.Fori(2, NM - 2) as m:
                body(Count(m))
            body(NM - 2)
            body(NM - 1)
            body(NM)
            body(NM + 1)

        def wait_apart(eng):
            eng.nop(nofuse=True)

        def batch_of(m):
            return at(m) // MPB

        def parts(m):
            if not isinstance(m, int):
                return True, True, True, True, True
            return m < NM, m + 1 < NM, m + 2 < NM, 1 <= m <= NM, 2 <= m <= NM + 1

        def ending(m):
            return isinstance(m, int) and m >= NM

        @block.sync
        def _(sp):
            half = NT // 2
            sp.dma_start(wnat[:, 0], Wq.rearrange("(r p) d -> p r d", p=P)).then_inc(S["w_loaded"], 16)
            sp.dma_start(wnat[:, 1], Wk.rearrange("(r p) d -> p r d", p=P)).then_inc(S["w_loaded"], 16)
            sp.dma_start(cnat, ctx_in.rearrange("b k d -> k b d")).then_inc(S["w_loaded"], 16)
            sp.dma_start(wnat[:, 2], Wv.rearrange("(r p) d -> p r d", p=P)).then_inc(S["w2_loaded"], 16)
            sp.dma_start(wnat[:, 3], Wo.rearrange("(r p) d -> p r d", p=P)).then_inc(S["w2_loaded"], 16)
            sp.dma_start(bv_b[:], bv.rearrange("(a d) -> a d", a=1).partition_broadcast(NK)).then_inc(S["small_loaded"], 16)
            sp.dma_start(bo_b[:], bo.rearrange("(a d) -> a d", a=1).partition_broadcast(P)).then_inc(S["small_loaded"], 16)
            sp.dma_start(wr[:], w_router.rearrange("(r p) e -> p r e", p=P)).then_inc(S["small_loaded"], 16)
            sp.wait_ge(S["const_ready"], 1)
            xz = xe[0:SLOTS, :].rearrange("(p r) d -> p (r d)", p=P)
            for i in range(SLOTS // P // 8):
                sp.dma_start(xz[:, i * 8 * D:(i + 1) * 8 * D].rearrange("p (r d) -> p r d", d=D),
                             zrow[:].unsqueeze(1).to_broadcast([P, 8, D])).then_inc(S["zero_done"], 16)
            def load_weights(e, half):
                if later(e, 0):
                    sp.wait_ge(S["w_head"], at(2 * e + half - 1))
                    sp.wait_ge(S["w_rest"], at(2 * e + half - 1))
                if half == 0:
                    sp.dma_start(wraw[:, 0:KT * HID].rearrange("p (k h) -> p k h", k=KT),
                                 w1[at(e)].rearrange("(k p) h -> p k h", p=P)).then_inc(S["wraw_loaded0"], 16)
                else:
                    sp.dma_start(wraw[:, KT * HID:].rearrange("p (k d) -> p k d", k=MT),
                                 w2[at(e)].rearrange("(k p) d -> p k d", p=P)).then_inc(S["wraw_loaded1"], 16)

            def load_chunk(c, par):
                if later(c, 1):
                    sp.wait_ge(S["fxT_ready"], at(c - 1))
                sp.dma_start(xc[:, par], xe_v[:, at(c)]).then_inc(S["xc_loaded%d" % par], 16)

            sp.dma_start(b2_b[:], b2.rearrange("(a e) d -> a e d", a=1).partition_broadcast(P)).then_inc(S["b2_loaded"], 16)
            load_weights(0, 0)
            load_weights(0, 1)
            load_weights(1, 0)
            load_weights(1, 1)
            sp.wait_ge(S["scattered"], at(16 * 2 * NT))
            load_chunk(0, 0)
            load_chunk(1, 1)

            def pair(ep, last):
                for a in range(2):
                    e = ep * 2 + a
                    for j in range(CPE):
                        i = a * CPE + j
                        c = ep * (2 * CPE) + i
                        if not (last and i >= 2 * CPE - 2):
                            load_chunk(c + 2, i % 2)
                        if not last and j >= 1:
                            load_weights(e + 2, j - 1)

            pair(0, False)
            with sp.Fori(1, NE // 2 - 1) as ep:
                pair(Count(ep), False)
            pair(NE // 2 - 1, True)
            for t in range(NT):
                sp.wait_ge(S["fin_ready"], at(t + 1))
                sp.dma_start(out_v[:, t], fin[:, t % 2]).then_inc(S["fin_stored%d" % (t % 2)], 16)
            sp.wait_ge(S["fin_stored0"], at(16 * NT // 2))
            sp.wait_ge(S["fin_stored1"], at(16 * NT // 2))

        @block.gpsimd
        def _(pool):
            g = nc.gpsimd
            g.memset(zrow[:], 0.0).then_inc(S["const_ready"], 1)
            g.memset(identf[:], 0.0)
            g.memset(identb[:], 0.0)
            g.memset(before[:], 1.0)
            g.memset(onesb[:], 1.0)
            g.memset(mhalf[:], -0.5)
            g.memset(run[:], 0.0)
            g.memset(ohs[:], 0.0)
            g.memset(blockh[:], 1.0)
            g.memset(vcat[:, :, :, 3 * DH:VW], 1.0)
            g.iota(iota_e[:], pattern=[[1, NE]], base=0, channel_multiplier=0, allow_small_or_imprecise_dtypes=True)
            g.iota(base_e[:], pattern=[[CAP, NE]], base=0, channel_multiplier=0, allow_small_or_imprecise_dtypes=True)
            g.iota(dump[:], pattern=[[P, NT], [NTOK, 2]], base=SLOTS, channel_multiplier=1,
                   allow_small_or_imprecise_dtypes=True).then_inc(S["const_step"], 1)
            pool.wait_ge(S["const_step"], 1)
            g.affine_select(out=identf[:], in_=identf[:], compare_op=ALU.not_equal, fill=1.0, base=0,
                            pattern=[[-1, P]], channel_multiplier=1)
            g.affine_select(out=identb[:], in_=identb[:], compare_op=ALU.not_equal, fill=1.0, base=0,
                            pattern=[[-1, P]], channel_multiplier=1)
            g.affine_select(out=before[:], in_=before[:], compare_op=ALU.is_gt, fill=0.0, base=0,
                            pattern=[[1, P]], channel_multiplier=-1)
            g.affine_select(out=blockh[:], in_=blockh[:], compare_op=ALU.is_ge, fill=0.0, base=0,
                            pattern=[[-DH, HK]], channel_multiplier=1).then_inc(S["const_step"], 1)
            pool.wait_ge(S["const_step"], 2)
            g.affine_select(out=blockh[:], in_=blockh[:], compare_op=ALU.is_ge, fill=0.0, base=DH - 1,
                            pattern=[[DH, HK]], channel_multiplier=-1).then_inc(S["const_ready"], 1)

            def inverse_std(m_, r_, tag, done, n):
                pool.wait_ge(S[tag], at(2 * G * (n + 1)))
                wait_apart(pool)
                g.tensor_scalar(r_[:], m_[:, :, 1], EPS, None, ALU.add).then_inc(S[done], 1)
                pool.wait_ge(S[done], at(2 * n + 1))
                wait_apart(pool)
                g.tensor_tensor(r_[:], r_[:], mhalf[:], ALU.pow).then_inc(S[done], 1)

            def norm1(m):
                if later(m, 0):
                    pool.wait_ge(S["xT_ready"], at(m))
                inverse_std(mv, rstd, "stat_step", "rstd_ready", m)
                pool.wait_ge(S["rstd_ready"], at(2 * (m + 1)))
                wait_apart(pool)
                g.tensor_tensor(xn[:], xs[:, bass.ds(at(m * G), G), :], mv[:, :, 0:1].to_broadcast([P, G, D]),
                                ALU.subtract).then_inc(S["xn_ready"], 1)
                pool.wait_ge(S["xn_ready"], at(2 * m + 1))
                wait_apart(pool)
                g.tensor_tensor(xn[:], xn[:], rstd[:].unsqueeze(2).to_broadcast([P, G, D]),
                                ALU.mult).then_inc(S["xn_ready"], 1)

            norm1(0)
            def blocks(b):
                for r in range(KT):
                    ins = g.tensor_tensor(kbl[:, b, r, :].rearrange("p (h k) -> p h k", h=HK),
                                          ktl[:, r, b * NK:(b + 1) * NK].unsqueeze(1).to_broadcast([P, HK, NK]),
                                          blockh[:].unsqueeze(2).to_broadcast([P, HK, NK]), ALU.mult)
                ins.then_inc(S["kb_rest"], 1)

            norm1(1)
            pool.wait_ge(S["dve_setup"], 4)
            blocks(0)
            pool.wait_ge(S["vpart_step"], 1)
            for b in range(NB):
                ins = g.tensor_tensor(vview(vrest[:, 0, :])[:, b], vview(vf)[:, b], vpart(0)[:, b], ALU.subtract)
            ins.then_inc(S["vpart_step"], 1)
            pool.wait_ge(S["vpart_step"], 3)
            for b in range(NB):
                ins = g.tensor_tensor(vview(vrest[:, 1, :])[:, b], vview(vrest[:, 0, :])[:, b], vpart(1)[:, b], ALU.subtract)
            ins.then_inc(S["vpart_step"], 1)
            blocks(1)
            pool.wait_ge(S["zero_done"], at(16 * (SLOTS // P // 8)))

            def body(m):
                units, qn, pre, tail, slots = parts(m)
                if pre:
                    norm1(m + 2)
                if slots:
                    n = m - 2
                    base = n * 11
                    pool.wait_ge(S["oh_ready"], at(2 * (n + 1)))
                    wait_apart(pool)
                    g.tensor_tensor(run[:, 0, :], run[:, 1, :], ohs[:, 1, :], ALU.add).then_inc(S["route_step"], 1)
                    pool.wait_ge(S["route_step"], at(base + 1))
                    wait_apart(pool)
                    g.tensor_tensor(ohs[:], oh[:, :, 0, :], oh[:, :, 1, :], ALU.add).then_inc(S["route_step"], 1)
                    pool.wait_ge(S["route_step"], at(base + 2))
                    wait_apart(pool)
                    g.tensor_tensor(run[:, 1, :], run[:, 0, :], ohs[:, 0, :], ALU.add).then_inc(S["run_ready"], 1)
                    g.tensor_scalar(eb[:], ek[:], float(CAP), None, ALU.mult).then_inc(S["route_step"], 1)
                if slots:
                    pool.wait_ge(S["slot_ready"], at(n + 1))
                    wait_apart(pool)
                    for t in range(G):
                        g.tensor_tensor(pick[:, t], oh[:, t], slotv[:, t, :].unsqueeze(1).to_broadcast([P, 2, NE]),
                                        ALU.mult).then_inc(S["pick_ready"], 1)
                if tail:
                    inverse_std(mv2, rstd2, "stat2_step", "rstd2_ready", m - 1)
                if units:
                    if later(m, 0):
                        pool.wait_ge(S["x1_ready"], at(m))
                        wait_apart(pool)
                    else:
                        pool.wait_ge(S["small_loaded"], at(16 * 3))
                    g.tensor_tensor(xbo[:], xs[:, bass.ds(at(m * G), G), :],
                                    bo_b[:].unsqueeze(1).to_broadcast([P, G, D]), ALU.add).then_inc(S["xbo_ready"], 1)
                if slots:
                    pool.wait_ge(S["sk_ready"], at(n + 1))
                    pool.wait_ge(S["route_step"], at(base + 3))
                    wait_apart(pool)
                    g.tensor_tensor(pos[:], sk[:], eb[:], ALU.subtract).then_inc(S["route_step"], 1)
                    pool.wait_ge(S["route_step"], at(base + 4))
                    wait_apart(pool)
                    g.tensor_scalar(kp[:], pos[:], float(CAP), None, ALU.is_lt).then_inc(S["route_step"], 1)
                    g.tensor_tensor(t1[:], sk[:], dump[:, bass.ds(at(n * G), G), :], ALU.subtract).then_inc(S["route_step"], 1)
                    pool.wait_ge(S["route_step"], at(base + 6))
                    wait_apart(pool)
                    g.tensor_tensor(t1[:], t1[:], kp[:], ALU.mult).then_inc(S["route_step"], 1)
                    pool.wait_ge(S["route_step"], at(base + 7))
                    wait_apart(pool)
                    g.tensor_tensor(t1[:], t1[:], dump[:, bass.ds(at(n * G), G), :], ALU.add).then_inc(S["route_step"], 1)
                    pool.wait_ge(S["route_step"], at(base + 8))
                    if ending(m):
                        pool.wait_ge(S["scattered"], n * (2 * G * 16))
                    wait_apart(pool)
                    g.tensor_copy(sidx[:], t1[:]).then_inc(S["route_step"], 1)
                    pool.wait_ge(S["route_step"], at(base + 9))
                    pool.wait_ge(S["rows_ready"], at(n + 1))
                    wait_apart(pool)
                    for t in range(G):
                        for k in range(2):
                            g.indirect_dma_start(xe, bass.IndirectOffsetOnAxis(ap=sidx[:, t, k:k + 1], axis=0),
                                                 rows[:, t, :], None).then_inc(S["scattered"], 16)
                    g.tensor_tensor(t2[:], pos[:], kp[:], ALU.mult)
                    g.tensor_copy(keep[:, bass.ds(at(n * G), G), :], kp[:]).then_inc(S["route_step"], 1)
                    pool.wait_ge(S["route_step"], at(base + 10))
                    wait_apart(pool)
                    g.tensor_tensor(gslot[:, bass.ds(at(n * G), G), :], t2[:], eb[:], ALU.add).then_inc(S["route_step"], 1)
                    if not ending(m + 1):
                        pool.wait_ge(S["scattered"], at((n + 1) * (2 * G * 16)))
                if isinstance(m, int) and m == 1:
                    rest(0, 0)

            def rest(e, par):
                for half in range(2):
                    hs = slice(half * KT * HID, (half + 1) * KT * HID)
                    pool.wait_ge(S["w_head"], at(2 * e + half + 1))
                    wait_apart(pool)
                    g.tensor_tensor(wl[:, par, hs], wraw[:, hs], wh[:, par, hs].bitcast(F32),
                                    ALU.subtract).then_inc(S["w_rest"], 1)

            macro_loop(pool, body)
            rest(1, 1)
            with pool.Fori(1, NE // 2) as ep:
                ep = Count(ep)
                rest(ep * 2, 0)
                rest(ep * 2 + 1, 1)
            before_last = (NE - 1) * CPE
            for k in range(2):
                if k == 0:
                    outputs = eo[0:(NE - 1) * CAP, :]
                    pool.wait_ge(S["gidx_ready"], 1)
                    pool.wait_ge(S["y_stored0"], at(16 * ((before_last + 1) // 2)))
                    pool.wait_ge(S["y_stored1"], at(16 * (before_last // 2)))
                else:
                    outputs = eo
                    pool.wait_ge(S["y_stored0"], at(16 * ((NCH + 1) // 2)))
                    pool.wait_ge(S["y_stored1"], at(16 * (NCH // 2)))
                for t in range(NT):
                    i = k * NT + t
                    if i >= GR:
                        pool.wait_ge(S["lower_added"] if i - GR < NT else S["fin_ready"], (i - GR) % NT + 1)
                    g.indirect_dma_start(ga[:, i % GR, :], None, outputs,
                                         bass.IndirectOffsetOnAxis(ap=gidx[:, t, k:k + 1], axis=0),
                                         ).then_inc(S["gath%d" % (i % GR)], 16)

        @block.scalar
        def _(act):
            a = nc.scalar
            act.dma_start(xs[:, 0:2], x_v[:, 0:2]).then_inc(S["x_loaded"], 16)
            nb1 = NE * MT
            act.dma_start(brow[nb1:nb1 + KT, :], bq.rearrange("(m p) -> m p", p=P)).then_inc(S["bias_loaded"], 16)
            act.dma_start(brow[nb1 + KT:nb1 + 2 * KT, :], bk.rearrange("(m p) -> m p", p=P)).then_inc(S["bias_loaded"], 16)
            act.dma_start(mraw, mask_v).then_inc(S["mask_loaded"], 16)
            act.dma_start(brow[0:nb1, :], b1.rearrange("e (m p) -> (e m) p", p=P)).then_inc(S["bias_loaded"], 16)
            act.wait_ge(S["x_loaded"], 16)
            act.dma_start(xs[:, 2:NT], x_v[:, 2:NT]).then_inc(S["x_loaded"], 16)
            act.wait_ge(S["pe_setup"], 1)
            a.activation(wqh.rearrange("p k d -> p (k d)"), ps[:, 0, :], ACT.Copy).then_inc(S["act_setup"], 1)
            act.wait_ge(S["pe_setup"], 2)
            a.activation(wkT.rearrange("p k d -> p (k d)"), ps[:, 1, :], ACT.Copy).then_inc(S["act_setup"], 1)
            act.wait_ge(S["pe_setup"], 3)
            a.activation(cT[:].rearrange("p k d -> p (k d)"), ps[:, 2, 0:KT * NB * NK], ACT.Copy).then_inc(S["act_setup"], 1)
            def split_xT(m):
                act.wait_ge(S["xT_ready"], at(m + 1))
                if later(m, 0):
                    act.wait_ge(S["q_ready"], at(m))
                a.activation(xTh[:, 0, :], ps[:, TR, :], ACT.Copy).then_inc(S["xT_split"], 1)

            def split_q(m, t):
                act.wait_ge(S["q_ready"], at(m + 1))
                if later(m, 0):
                    act.wait_ge(S["sc_ready"], at(UPM * (m - 1) + UPT * (t + 1)))
                if t == 1:
                    act.wait_ge(S["q_rest"], at(2 * m + 1))
                for r in range(KT):
                    ins = a.activation(qh[:, r, t * P:(t + 1) * P], bank(QB, KT)[:, r, t * P:(t + 1) * P], ACT.Identity,
                                       bias=bcol[:, nb1 + r:nb1 + r + 1])
                ins.then_inc(S["q_split"], 1)

            def exp(m, j, par):
                u = UPM * m + j
                act.wait_ge(S["max_ready"], at(u + 1))
                if later(u, 1):
                    act.wait_ge(S["pt_ready"], at(u - 1))
                for h in range(HU):
                    hs = slice(h * NK, (h + 1) * NK)
                    ins = a.activation(pb[:, par, hs], ps[:, SC + par, hs], ACT.Exp, bias=nmx[:, par, h:h + 1])
                ins.then_inc(S["exp_ready"], 1)

            def split_oT(m, t):
                act.wait_ge(S["oT_ready"], at(2 * m + t + 1))
                if later(m, 0):
                    act.wait_ge(S["wo_ready"], at(m))
                o3 = oTh.rearrange("p (k c) -> p k c", k=KT)
                a.activation(o3[:, :, t * P:(t + 1) * P], bank(TR, KT)[:, :, t * P:(t + 1) * P],
                             ACT.Copy).then_inc(S["oT_split"], 1)

            def head_pt(u, par):
                act.wait_ge(S["pt_ready"], at(u + 1))
                if later(u, 1):
                    act.wait_ge(S["pv_ready"], at(u - 1))
                a.activation(pth[:, par, :], ps[0:NK, PT + par, :], ACT.Copy).then_inc(S["pth_ready"], 1)

            split_xT(0)
            act.wait_ge(S["pe_setup"], 5)
            a.activation(bcol[:], ps[:, 4, 0:NE * MT + 2 * KT], ACT.Copy).then_inc(S["act_setup"], 1)
            act.wait_ge(S["pe_setup"], 6)
            a.activation(wvT.rearrange("p k d -> p (k d)"), ps[:, 3, :], ACT.Copy).then_inc(S["act_setup"], 1)
            act.wait_ge(S["act_setup"], 4)
            split_q(0, 0)
            split_q(0, 1)
            act.wait_ge(S["pe_setup"], 8)
            a.activation(woh.rearrange("p k d -> p (k d)"), ps[:, WB, :], ACT.Copy).then_inc(S["act_setup"], 1)
            act.wait_ge(S["dve_setup"], 5)
            a.activation(vpart(0), vview(vf), ACT.Copy).then_inc(S["vpart_step"], 1)
            exp(0, 0, 0)
            act.wait_ge(S["vpart_step"], 2)
            a.activation(vpart(1), vview(vrest[:, 0, :]), ACT.Copy).then_inc(S["vpart_step"], 1)
            act.wait_ge(S["vpart_step"], 4)
            a.activation(vpart(2), vview(vrest[:, 1, :]), ACT.Copy).then_inc(S["v_split"], 1)

            def body(m):
                units, qn, pre, tail, slots = parts(m)
                for j in range(UPM):
                    if units:
                        head_pt(UPM * m + j, j % 2)
                        if j < UPM - 1:
                            exp(m, j + 1, 1 - j % 2)
                        elif qn:
                            exp(m + 1, 0, 0)
                    if j == 0 and slots:
                        act.wait_ge(S["x2T_ready"], at(m - 1))
                        a.activation(x2T[:], ps[:, TR, :], ACT.Copy).then_inc(S["x2T_copied"], 1)
                    if j == 1 and qn:
                        split_xT(m + 1)
                    if j == 3 and qn:
                        split_q(m + 1, 0)
                    if j == 3 and tail:
                        split_oT(m - 1, 1)
                    if j == 5 and slots:
                        n = m - 2
                        act.wait_ge(S["xn2_ready"], at(2 * (n + 1)))
                        if ending(m):
                            act.wait_ge(S["scattered"], n * (2 * G * 16))
                        else:
                            act.wait_ge(S["route_step"], at(11 * n + 1))
                        a.activation(rows, xn2[:], ACT.Copy).then_inc(S["rows_ready"], 1)
                    if j == 6 and qn:
                        split_q(m + 1, 1)
                    if j == 6 and units:
                        split_oT(m, 0)
                    if isinstance(m, int) and m == 1 and j in (2, 5):
                        head(0, 0, j // 3)

            def head(e, par, half):
                act.wait_ge(S["wraw_loaded%d" % half], at(16 * (e + 1)))
                if later(e, 1):
                    if half == 0:
                        act.wait_ge(S["h_ready"], at((e - 1) * (CPE * MT // 2)))
                    else:
                        act.wait_ge(S["y_ready"], at((e - 1) * CPE))
                hs = slice(half * KT * HID, (half + 1) * KT * HID)
                a.activation(wh[:, par, hs], wraw[:, hs], ACT.Copy).then_inc(S["w_head"], 1)

            macro_loop(act, body)
            act.wait_ge(S["gate_step"], 1)
            a.activation(ge[:], gd[:], ACT.Exp).then_inc(S["gate_exp"], 1)

            def ffn_xT(c, par):
                act.wait_ge(S["fxT_ready"], at(c + 1))
                a.activation(xTh[:, par, :], ps[:, 6, :], ACT.Copy).then_inc(S["fxT_head"], 1)

            def ffn_h(e, c, par):
                for i in range(MT // 2):
                    act.wait_ge(S["h_ready"], at(c * (MT // 2) + i + 1))
                    if later(c * (MT // 2) + i, 1):
                        act.wait_ge(S["h_rest"], at(c * (MT // 2) + i - 1))
                        wait_apart(act)
                    for s in range(2):
                        ins = a.activation(hf[:, i % 2, s * CH:(s + 1) * CH], ps[:, i, s * CH:(s + 1) * CH], ACT.Relu,
                                           bias=bcol[:, bass.ds(at(e * MT + 2 * i + s), 1)])
                    ins.then_inc(S["h_relu"], 1)
                    act.wait_ge(S["h_relu"], at(c * (MT // 2) + i + 1))
                    if i == 0 and (later(c, 1)):
                        act.wait_ge(S["y_ready"], at(c - 1))
                    a.activation(hh[:, par, 2 * i * CH:2 * (i + 1) * CH], hf[:, i % 2, :],
                                 ACT.Copy).then_inc(S["h_head"], 1)

            ffn_xT(0, 0)
            ffn_h(0, 0, 0)
            ffn_xT(1, 1)

            def store_chunk(c, par):
                act.wait_ge(S["y_copied"], at(c + 1))
                act.dma_start(eo_v[:, at(c)], yb[:, par]).then_inc(S["y_stored%d" % par], 16)

            def pair(ep, last):
                for aa in range(2):
                    for j in range(CPE):
                        i = aa * CPE + j
                        c = ep * (2 * CPE) + i
                        if later(c, 0):
                            store_chunk(c - 1, 1 - i % 2)
                        if not (last and i == 2 * CPE - 1):
                            ffn_h(ep * 2 + (i + 1) // CPE, c + 1, 1 - i % 2)
                        if j < 2 and not (last and aa == 1):
                            head(ep * 2 + 1 + aa, 1 - aa, j)
                        if not (last and i >= 2 * CPE - 2):
                            ffn_xT(c + 2, i % 2)

            pair(0, False)
            with act.Fori(1, NE // 2 - 1) as ep:
                pair(Count(ep), False)
            pair(NE // 2 - 1, True)
            store_chunk(NCH - 1, (NCH - 1) % 2)

        @block.vector
        def _(dve):
            v = nc.vector
            nb1 = NE * MT
            dve.wait_ge(S["mask_loaded"], 16)
            for b in range(NB):
                ins = v.tensor_scalar(mb[:, b * TPB:(b + 1) * TPB, :], mraw, 0.0, NEG, ALU.is_equal, ALU.mult)
            ins.then_inc(S["mask_ready"], 1)

            def stats(src, s_, m_, tag, n):
                for t in range(G):
                    v.bn_stats(s_[:, t, :], src(t)).then_inc(S[tag], 1)
                for t in range(G):
                    dve.wait_ge(S[tag], at(n * (2 * G) + 1 + t))
                    wait_apart(dve)
                    v.bn_aggr(m_[:, t, :], s_[:, t, :]).then_inc(S[tag], 1)

            def stats1(m):
                if isinstance(m, int):
                    dve.wait_ge(S["x_loaded"], 16 if m == 0 else 32)
                if later(m, 0):
                    dve.wait_ge(S["xn_ready"], at(2 * m - 1))
                    wait_apart(dve)
                stats(lambda t: xs[:, at(m * G + t), :], st, mv, "stat_step", m)

            def rest_xT(m):
                dve.wait_ge(S["xT_split"], at(m + 1))
                if later(m, 0):
                    dve.wait_ge(S["q_ready"], at(m))
                v.tensor_tensor(xTl[:, 0, :], ps[:, TR, :], xTh[:, 0, :].bitcast(F32),
                                ALU.subtract).then_inc(S["xT_rest"], 1)

            def rest_q(m, t):
                dve.wait_ge(S["q_split"], at(2 * m + t + 1))
                ts = slice(t * P, (t + 1) * P)
                for r in range(KT):
                    ins = v.scalar_tensor_tensor(out=ql[:, r, ts], in0=bank(QB, KT)[:, r, ts],
                                                 scalar=bcol[:, nb1 + r:nb1 + r + 1], in1=qh[:, r, ts].bitcast(F32),
                                                 op0=ALU.add, op1=ALU.subtract)
                ins.then_inc(S["q_rest"], 1)

            def maximum(u, par):
                dve.wait_ge(S["sc_ready"], at(u + 1))
                v.tensor_reduce(nmx[:, par, :], ps[:, SC + par, 0:UC].rearrange("p (h k) -> p h k", k=NK), AX.X,
                                ALU.max, negate=True).then_inc(S["max_ready"], 1)

            def rest_oT(m, t):
                dve.wait_ge(S["oT_split"], at(2 * m + t + 1))
                ts = slice(t * P, (t + 1) * P)
                v.tensor_tensor(oTl.rearrange("p (k c) -> p k c", k=KT)[:, :, ts], bank(TR, KT)[:, :, ts],
                                oTh.bitcast(F32).rearrange("p (k c) -> p k c", k=KT)[:, :, ts],
                                ALU.subtract).then_inc(S["oT_rest"], 1)

            def rest_pt(u, par):
                dve.wait_ge(S["pth_ready"], at(u + 1))
                v.tensor_tensor(ptl[:, par, :], ps[0:NK, PT + par, :], pth[:, par, :],
                                ALU.subtract).then_inc(S["ptl_ready"], 1)

            def sum_o(u):
                dve.wait_ge(S["pv_ready"], at(u + 1))
                if later(u, 0):
                    dve.wait_ge(S["o_done"], at(u))
                pv = ps[:, PV, 0:HU * VW].rearrange("p (h c) -> p h c", h=HU)
                v.tensor_reduce(osum[:].rearrange("p (h d) -> p h d", h=HU),
                                pv[:, :, 0:3 * DH].rearrange("p h (s d) -> p h d s", s=3), AX.X,
                                ALU.add).then_inc(S["osum_part"], 1)
                v.reciprocal(rinv[:], pv[:, :, 3 * DH]).then_inc(S["osum_part"], 1)

            def divide_o(m, j):
                dve.wait_ge(S["osum_part"], at(2 * (UPM * m + j + 1)))
                if j % UPT == 0 and later(m, 0):
                    dve.wait_ge(S["oT_ready"], at(2 * m - 1 + j // UPT))
                t, quarter = j // UPT, j % UPT
                v.tensor_tensor(o[:, t, quarter * HU * DH:(quarter + 1) * HU * DH].rearrange("p (h d) -> p h d", h=HU),
                                osum[:].rearrange("p (h d) -> p h d", h=HU),
                                rinv[:].unsqueeze(2).to_broadcast([P, HU, DH]), ALU.mult).then_inc(S["o_done"], 1)

            stats1(0)
            dve.wait_ge(S["act_setup"], 1)
            v.tensor_tensor(wql.rearrange("p k d -> p (k d)"), ps[:, 0, :],
                            wqh.rearrange("p k d -> p (k d)").bitcast(F32), ALU.subtract).then_inc(S["dve_setup"], 1)
            stats1(1)
            rest_xT(0)
            dve.wait_ge(S["pe_setup"], 4)
            dve.wait_ge(S["act_setup"], 4)
            for r in range(KT):
                ins = v.tensor_scalar(ktf[:, r, :], ps[:, 1, r * NB * NK:(r + 1) * NB * NK],
                                      bcol[:, nb1 + KT + r:nb1 + KT + r + 1], DH ** -0.5, ALU.add, ALU.mult)
            ins.then_inc(S["dve_setup"], 1)
            dve.wait_ge(S["dve_setup"], 2)
            v.tensor_copy(kth[:], ktf[:]).then_inc(S["dve_setup"], 1)
            dve.wait_ge(S["dve_setup"], 3)
            v.tensor_tensor(ktl[:], ktf[:], kth[:].bitcast(F32), ALU.subtract).then_inc(S["dve_setup"], 1)
            dve.wait_ge(S["const_ready"], 2)

            def blocks(b):
                for r in range(KT):
                    ins = v.tensor_tensor(kbh[:, b, r, :].rearrange("p (h k) -> p h k", h=HK),
                                          kth[:, r, b * NK:(b + 1) * NK].bitcast(F32).unsqueeze(1).to_broadcast([P, HK, NK]),
                                          blockh[:].unsqueeze(2).to_broadcast([P, HK, NK]), ALU.mult)
                ins.then_inc(S["kb_head"], 1)

            blocks(0)
            rest_q(0, 0)
            rest_q(0, 1)
            dve.wait_ge(S["pe_setup"], 7)
            dve.wait_ge(S["small_loaded"], at(16 * 3))
            v.tensor_tensor(vf.rearrange("p (b d) -> p b d", b=NB), ps[0:NK, 3, :].rearrange("p (b d) -> p b d", b=NB),
                            bv_b[:].unsqueeze(1).to_broadcast([NK, NB, D]), ALU.add).then_inc(S["dve_setup"], 1)
            maximum(0, 0)
            dve.wait_ge(S["act_setup"], 6)
            v.tensor_tensor(wol.rearrange("p k d -> p (k d)"), ps[:, WB, :],
                            woh.rearrange("p k d -> p (k d)").bitcast(F32), ALU.subtract).then_inc(S["dve_setup"], 1)
            maximum(1, 1)

            def slot_values(n, bk_):
                dve.wait_ge(S["pos_ready"], at(n + 1))
                v.tensor_tensor(slotv[:], ps[:, bk_, 0:G * NE].rearrange("p (t e) -> p t e", t=G),
                                base_e[:].unsqueeze(1).to_broadcast([P, G, NE]), ALU.add).then_inc(S["slot_ready"], 1)

            def route(n):
                dve.wait_ge(S["lg_ready"], at(n + 1))
                v.tensor_copy(lg[:], ps[:, QB, 0:G * NE].rearrange("p (t e) -> p t e", t=G)).then_inc(S["lg_copied"], 1)
                dve.wait_ge(S["lg_copied"], at(n + 1))
                wait_apart(dve)
                for t in range(G):
                    v.max(top[:, t, :], lg[:, t, :]).then_inc(S["top_ready"], 1)
                dve.wait_ge(S["top_ready"], at(2 * (n + 1)))
                v.tensor_copy(top2[:, bass.ds(at(n * G), G), :], top[:, :, 0:2])
                for t in range(G):
                    ins = v.max_index(tix[:, t, :], top[:, t, :], lg[:, t, :])
                ins.then_inc(S["tix_ready"], 1)
                dve.wait_ge(S["tix_ready"], at(2 * n + 1))
                v.tensor_copy(ek[:], tix[:, :, 0:2]).then_inc(S["tix_ready"], 1)
                dve.wait_ge(S["tix_ready"], at(2 * n + 2))
                for t in range(G):
                    v.tensor_tensor(oh[:, t], ek[:, t, :].unsqueeze(2).to_broadcast([P, 2, NE]),
                                    iota_e[:].unsqueeze(1).to_broadcast([P, 2, NE]),
                                    ALU.is_equal).then_inc(S["oh_ready"], 1)

            def body(m):
                units, qn, pre, tail, slots = parts(m)
                for j in range(UPM):
                    u = UPM * m + j
                    if units and (qn or j < UPM - 2):
                        maximum(u + 2, j % 2)
                    if isinstance(m, int) and u == 0:
                        blocks(1)
                    if units:
                        rest_pt(u, j % 2)
                    if j == 2 and qn:
                        rest_xT(m + 1)
                    if j == 4 and tail:
                        rest_oT(m - 1, 1)
                    if j == 7 and units:
                        rest_oT(m, 0)
                    if j == 0 and tail:
                        sum_o(u - 1)
                    if units and j > 0:
                        sum_o(u - 1)
                    if j == 0 and pre:
                        stats1(m + 2)
                    if j == 4 and qn:
                        rest_q(m + 1, 0)
                    if j == 4 and slots and not ending(m):
                        slot_values(m - 2, WB)
                    if j == 5 and slots and not tail:
                        slot_values(m - 2, SC)
                    if j == 6 and slots:
                        n = m - 2
                        dve.wait_ge(S["pick_ready"], at(2 * (n + 1)))
                        v.tensor_reduce(sk[:], pick[:], AX.X, ALU.add).then_inc(S["sk_ready"], 1)
                    if j == 0 and tail:
                        divide_o(m - 1, UPM - 1)
                    if units and j > 0:
                        divide_o(m, j - 1)
                    if j == (4 if ending(m) else 2) and slots:
                        route(m - 2)
                    if j == 5 and tail:
                        n = m - 1
                        dve.wait_ge(S["wo_ready"], at(m))
                        dve.wait_ge(S["xbo_ready"], at(m))
                        v.tensor_tensor(xs[:, bass.ds(at(n * G), G), :], bank(WB, G), xbo[:], ALU.add).then_inc(S["x1_ready"], 1)
                        if ending(m):
                            slot_values(m - 2, SC)
                        dve.wait_ge(S["x1_ready"], at(m))
                        wait_apart(dve)
                        stats(lambda t: xs[:, at(n * G + t), :], st2, mv2, "stat2_step", n)
                    if j == 7 and tail:
                        n = m - 1
                        dve.wait_ge(S["rstd2_ready"], at(2 * m))
                        if later(n, 0):
                            dve.wait_ge(S["rows_ready"], at(n))
                            dve.wait_ge(S["x2T_ready"], at(n))
                        for t in range(G):
                            v.tensor_scalar(xn2[:, t, :], xs[:, at(n * G + t), :], mv2[:, t, 0:1],
                                            rstd2[:, t:t + 1], ALU.subtract, ALU.mult).then_inc(S["xn2_ready"], 1)
                    if j == 7 and qn:
                        rest_q(m + 1, 1)

            macro_loop(dve, body)

            dve.wait_ge(S["route_step"], at(11 * NM))
            v.tensor_tensor(gd[:], top2[:, :, 1], top2[:, :, 0], ALU.subtract).then_inc(S["gate_step"], 1)

            def gates():
                dve.wait_ge(S["gate_exp"], 1)
                v.tensor_tensor(swap[:], gslot[:, :, 0], gslot[:, :, 1], ALU.is_gt)
                v.tensor_tensor(noswap[:], gslot[:, :, 0], gslot[:, :, 1], ALU.is_lt)
                v.tensor_tensor(gidx[:, :, 0], gslot[:, :, 0], gslot[:, :, 1], ALU.min)
                v.tensor_tensor(gidx[:, :, 1], gslot[:, :, 0], gslot[:, :, 1], ALU.max).then_inc(S["gidx_ready"], 1)
                v.tensor_scalar(g1[:], ge[:], 1.0, None, ALU.add).then_inc(S["gate_step"], 1)
                dve.wait_ge(S["gate_step"], 2)
                v.reciprocal(g1[:], g1[:]).then_inc(S["gate_step"], 1)
                dve.wait_ge(S["gate_step"], 3)
                v.tensor_tensor(ge[:], ge[:], g1[:], ALU.mult).then_inc(S["gate_step"], 1)
                dve.wait_ge(S["gate_step"], 4)
                v.tensor_tensor(gw[:, :, 0], g1[:], keep[:, :, 0], ALU.mult)
                v.tensor_tensor(gw[:, :, 1], ge[:], keep[:, :, 1], ALU.mult).then_inc(S["gate_step"], 1)
                dve.wait_ge(S["gate_step"], 5)
                v.tensor_tensor(gx[:, :, 0], gw[:, :, 1], swap[:], ALU.mult)
                v.tensor_tensor(gx[:, :, 1], gw[:, :, 0], swap[:], ALU.mult)
                v.tensor_tensor(gate[:], gw[:], noswap[:].unsqueeze(2).to_broadcast([P, NT, 2]),
                                ALU.mult).then_inc(S["gate_step"], 1)
                dve.wait_ge(S["gate_step"], 6)
                v.tensor_tensor(gate[:], gate[:], gx[:], ALU.add).then_inc(S["gate_ready"], 1)

            def gathered(i):
                dve.wait_ge(S["gath%d" % (i % GR)], 16 * (i // GR + 1))

            def add_lower(first, end):
                for t in range(first, end):
                    gathered(t)
                    v.scalar_tensor_tensor(out=xs[:, t, :], in0=ga[:, t % GR, :], scalar=gate[:, t, 0:1],
                                           in1=xs[:, t, :], op0=ALU.mult, op1=ALU.add).then_inc(S["lower_added"], 1)

            def ffn_xT(c, par):
                dve.wait_ge(S["fxT_head"], at(c + 1))
                v.tensor_tensor(xTl[:, par, :], ps[:, 6, :], xTh[:, par, :].bitcast(F32),
                                ALU.subtract).then_inc(S["fxT_rest"], 1)

            def ffn_h(c, par):
                for i in range(MT // 2):
                    dve.wait_ge(S["h_head"], at(c * (MT // 2) + i + 1))
                    v.tensor_tensor(hl[:, par, 2 * i * CH:2 * (i + 1) * CH], hf[:, i % 2, :],
                                    hh[:, par, 2 * i * CH:2 * (i + 1) * CH].bitcast(F32),
                                    ALU.subtract).then_inc(S["h_rest"], 1)

            def ffn_y(e, c, par, half):
                dve.wait_ge(S["y_ready"], at(c + 1))
                if later(c, 1):
                    dve.wait_ge(S["y_stored%d" % par], at(half * 16))
                v.tensor_tensor(yb[:, par], ps[:, 4 + par, :].rearrange("p (t d) -> p t d", t=G),
                                b2_b[:, at(e), :].unsqueeze(1).to_broadcast([P, G, D]), ALU.add).then_inc(S["y_copied"], 1)

            ffn_xT(0, 0)
            ffn_h(0, 0)
            ffn_xT(1, 1)
            gates()
            dve.wait_ge(S["gate_ready"], 1)
            dve.wait_ge(S["b2_loaded"], 16)

            def pair(ep, last):
                for aa in range(2):
                    for j in range(CPE):
                        i = aa * CPE + j
                        c = ep * (2 * CPE) + i
                        if not (last and i == 2 * CPE - 1):
                            ffn_h(c + 1, 1 - i % 2)
                        if not (last and i >= 2 * CPE - 2):
                            ffn_xT(c + 2, i % 2)
                        if last and i >= 2 * CPE - 2:
                            add_lower(*((4, 10), (10, NT))[i - 2 * CPE + 2])
                        ffn_y(ep * 2 + aa, c, i % 2, ep * CPE + i // 2)
                        if last and i == 2 * CPE - 3:
                            add_lower(0, 4)

            pair(0, False)
            with dve.Fori(1, NE // 2 - 1) as ep:
                pair(Count(ep), False)
            pair(NE // 2 - 1, True)
            dve.wait_ge(S["lower_added"], NT)
            for t in range(NT):
                gathered(NT + t)
                if t >= 2:
                    dve.wait_ge(S["fin_stored%d" % (t % 2)], at(16 * (t // 2)))
                v.scalar_tensor_tensor(out=fin[:, t % 2, :], in0=ga[:, (NT + t) % GR, :], scalar=gate[:, t, 1:2],
                                       in1=xs[:, t, :], op0=ALU.mult, op1=ALU.add).then_inc(S["fin_ready"], 1)

        @block.tensor
        def _(pe):
            T = nc.tensor

            def mm3(dst, sh, sl, mh, ml, first, last):
                T.matmul(dst, sh, mh, start=first, stop=False)
                T.matmul(dst, sh, ml, start=False, stop=False)
                return T.matmul(dst, sl, mh, start=False, stop=last)

            pe.wait_ge(S["const_ready"], 2)

            def turn_weight(w, b):
                for k in range(KT):
                    for r in range(KT):
                        ins = T.transpose(ps[:, b, k * D + r * P:k * D + (r + 1) * P],
                                          wnat[:, w, r, k * P:(k + 1) * P], identf[:])
                ins.then_inc(S["pe_setup"], 1)

            pe.wait_ge(S["w_loaded"], at(16 * 3))
            turn_weight(0, 0)
            turn_weight(1, 1)
            for k in range(KT):
                for b in range(NB):
                    ins = T.transpose(ps[:, 2, (k * NB + b) * NK:(k * NB + b + 1) * NK],
                                      cnat[:, b, k * P:(k + 1) * P], identf[0:NK, 0:NK])
            ins.then_inc(S["pe_setup"], 1)

            def bias_rows():
                nrow = NE * MT + 2 * KT
                pe.wait_ge(S["bias_loaded"], at(16 * 3))
                T.transpose(ps[:, 4, 0:nrow], brow[:], identf[0:nrow, 0:nrow]).then_inc(S["pe_setup"], 1)

            def project_k():
                pe.wait_ge(S["act_setup"], 3)
                for r in range(KT):
                    for k in range(KT):
                        ins = T.matmul(ps[:, 1, r * NB * NK:(r + 1) * NB * NK], wkT[:, k, r * P:(r + 1) * P],
                                       cT[:, k, :], start=(k == 0), stop=(k == KT - 1))
                ins.then_inc(S["pe_setup"], 1)

            def project_v():
                pe.wait_ge(S["act_setup"], 5)
                for b in range(NB):
                    for k in range(KT):
                        ins = T.matmul(ps[0:NK, 3, b * D:(b + 1) * D], cT[:, k, b * NK:(b + 1) * NK], wvT[:, k, :],
                                       start=(k == 0), stop=(k == KT - 1))
                ins.then_inc(S["pe_setup"], 1)

            def turn_macro(src, done):
                for k in range(KT):
                    for t in range(G):
                        ins = T.transpose(ps[:, TR, k * GT + t * P:k * GT + (t + 1) * P], src(t)[:, k * P:(k + 1) * P],
                                          identf[:])
                ins.then_inc(S[done], 1)

            def turn_xn(m):
                pe.wait_ge(S["xn_ready"], at(2 * (m + 1)))
                if later(m, 1):
                    pe.wait_ge(S["oT_rest"], at(2 * m - 3))
                if later(m, 2):
                    pe.wait_ge(S["x2T_copied"], at(m - 2))
                turn_macro(lambda t: xn[:, t, :], "xT_ready")

            def turn_o(m, t):
                pe.wait_ge(S["o_done"], at(UPM * m + UPT * (t + 1)))
                for k in range(KT):
                    ins = T.transpose(ps[:, TR, k * GT + t * P:k * GT + (t + 1) * P], o[:, t, k * P:(k + 1) * P], identf[:])
                ins.then_inc(S["oT_ready"], 1)

            def project_q(m):
                pe.wait_ge(S["xT_rest"], at(m + 1))
                if later(m, 2):
                    pe.wait_ge(S["lg_copied"], at(m - 2))
                if later(m, 0):
                    pe.wait_ge(S["q_rest"], at(2 * m))
                for r in range(KT):
                    for k in range(KT):
                        ks = slice(k * GT, (k + 1) * GT)
                        rs = slice(r * P, (r + 1) * P)
                        ins = mm3(bank(QB, KT)[:, r, :], wqh[:, k, rs], wql[:, k, rs], xTh[:, 0, ks], xTl[:, 0, ks],
                                  k == 0, k == KT - 1)
                ins.then_inc(S["q_ready"], 1)

            def scores(m, j, par):
                t, quarter = j // UPT, j % UPT
                r, half = quarter * HU // HK, quarter % (HK // HU)
                if j % UPT == 0:
                    pe.wait_ge(S["q_rest"], at(2 * m + t + 1))
                if later(UPM * m + j, 1):
                    pe.wait_ge(S["exp_ready"], at(UPM * m + j - 1))
                ts = slice(t * P, (t + 1) * P)
                cs = slice(half * UC, (half + 1) * UC)
                b = batch_of(m)
                dst = ps[:, SC + par, 0:UC]
                T.matmul(dst, identb[:], mb[:, at(m * G + t), :].unsqueeze(1).to_broadcast([P, HU, NK]),
                         start=True, stop=False)
                mm3(dst, qh[:, r, ts], ql[:, r, ts], kbh[:, b, r, cs], kbl[:, b, r, cs],
                    False, True).then_inc(S["sc_ready"], 1)

            def turn_p(u, par):
                pe.wait_ge(S["exp_ready"], at(u + 1))
                if later(u, 1):
                    pe.wait_ge(S["ptl_ready"], at(u - 1))
                for h in range(HU):
                    ins = T.transpose(ps[0:NK, PT + par, h * P:(h + 1) * P], pb[:, par, h * NK:(h + 1) * NK], identf[:])
                ins.then_inc(S["pt_ready"], 1)

            def times_v(m, j, par):
                u = UPM * m + j
                pe.wait_ge(S["ptl_ready"], at(u + 1))
                if later(u, 0):
                    pe.wait_ge(S["osum_part"], at(2 * u))
                b = batch_of(m)
                for h in range(HU):
                    dst = ps[:, PV, h * VW:(h + 1) * VW]
                    rhs = vcat[:, b, (j % UPT) * HU + h, :]
                    T.matmul(dst, pth[:, par, h * P:(h + 1) * P], rhs, start=True, stop=False)
                    ins = T.matmul(dst, ptl[:, par, h * P:(h + 1) * P], rhs, start=False, stop=True)
                ins.then_inc(S["pv_ready"], 1)

            def logits(n):
                pe.wait_ge(S["x2T_copied"], at(n + 1))
                pe.wait_ge(S["q_rest"], at(at_most(2 * (n + 3), 2 * NM)))
                for t in range(G):
                    for k in range(KT):
                        ins = T.matmul(ps[:, QB, t * NE:(t + 1) * NE],
                                       x2T[:, k * GT + t * P:k * GT + (t + 1) * P], wr[:, k, :],
                                       start=(k == 0), stop=(k == KT - 1))
                ins.then_inc(S["lg_ready"], 1)

            def positions(n, bk_):
                pe.wait_ge(S["run_ready"], at(n + 1))
                for t in range(G):
                    dst = ps[:, bk_, t * NE:(t + 1) * NE]
                    T.matmul(dst, before[:], ohs[:, t, :], start=True, stop=False)
                    ins = T.matmul(dst, onesb[:], run[:, t, :], start=False, stop=True)
                ins.then_inc(S["pos_ready"], 1)

            project_k()
            turn_xn(0)
            bias_rows()
            pe.wait_ge(S["w2_loaded"], at(16 * 2))
            turn_weight(2, 3)
            pe.wait_ge(S["dve_setup"], 1)
            project_q(0)
            project_v()
            turn_weight(3, WB)
            pe.wait_ge(S["kb_head"], 1)
            pe.wait_ge(S["kb_rest"], 1)
            pe.wait_ge(S["mask_ready"], 1)
            scores(0, 0, 0)
            scores(0, 1, 1)

            def body(m):
                units, qn, pre, tail, slots = parts(m)
                for j in range(UPM):
                    u = UPM * m + j
                    if units:
                        turn_p(u, j % 2)
                        if j < UPM - 2:
                            scores(m, j + 2, j % 2)
                        elif qn:
                            scores(m + 1, j + 2 - UPM, j % 2)
                    if j == 0 and slots:
                        pe.wait_ge(S["xn2_ready"], at(2 * (m - 1)))
                        pe.wait_ge(S["oT_rest"], at(at_most(2 * m - 1, 2 * NM)))
                        turn_macro(lambda t: xn2[:, t, :], "x2T_ready")
                    if j == 1 and qn:
                        turn_xn(m + 1)
                    if j == (3 if ending(m) else 2) and slots:
                        if ending(m) and tail:
                            pe.wait_ge(S["x2T_copied"], m - 1)
                            turn_o(m - 1, 1)
                        logits(m - 2)
                    if j == 3 and tail and not ending(m):
                        pe.wait_ge(S["xT_rest"], at(at_most(m + 2, NM)))
                        if slots:
                            pe.wait_ge(S["x2T_copied"], at(m - 1))
                        turn_o(m - 1, 1)
                    if j == 4 and slots and not ending(m):
                        pe.wait_ge(S["x1_ready"], at(m - 1))
                        positions(m - 2, WB)
                    if j == 6 and units:
                        if later(m, 0):
                            pe.wait_ge(S["oT_rest"], at(2 * m))
                        turn_o(m, 0)
                    if j == 0 and tail:
                        times_v(m - 1, UPM - 1, 1)
                    if units and j > 0:
                        times_v(m, j - 1, 1 - j % 2)
                    if j == 5 and tail:
                        pe.wait_ge(S["oT_rest"], at(2 * m))
                        if slots and not ending(m):
                            pe.wait_ge(S["slot_ready"], at(m - 1))
                        for t in range(G):
                            for k in range(KT):
                                ks = slice(k * GT + t * P, k * GT + (t + 1) * P)
                                ins = mm3(bank(WB, G)[:, t, :], oTh[:, ks], oTl[:, ks], woh[:, k, :], wol[:, k, :],
                                          k == 0, k == KT - 1)
                        ins.then_inc(S["wo_ready"], 1)
                    if j == 5 and ending(m):
                        positions(m - 2, SC)
                    if j == 3 and qn:
                        project_q(m + 1)
                    if isinstance(m, int) and m == 0 and j == 0:
                        pe.wait_ge(S["dve_setup"], 6)
                        pe.wait_ge(S["v_split"], 1)
                    if isinstance(m, int) and m == 1 and j == 0:
                        pe.wait_ge(S["kb_head"], 2)
                        pe.wait_ge(S["kb_rest"], 2)
                        pe.wait_ge(S["small_loaded"], at(16 * 3))

            macro_loop(pe, body)

            def turn_x(c, par, half):
                pe.wait_ge(S["xc_loaded%d" % par], at((half + 1) * 16))
                if later(c, 0):
                    pe.wait_ge(S["fxT_rest"], at(c))
                for k in range(KT):
                    for t in range(G):
                        ins = T.transpose(ps[:, 6, k * CH + t * P:k * CH + (t + 1) * P],
                                          xc[:, par, t, k * P:(k + 1) * P], identf[:])
                ins.then_inc(S["fxT_ready"], 1)

            def hidden(e, c, par, epar, first_of_expert):
                pe.wait_ge(S["fxT_rest"], at(c + 1))
                if first_of_expert:
                    pe.wait_ge(S["w_rest"], at(2 * e + 1))
                for i in range(MT // 2):
                    if later(c, 0):
                        pe.wait_ge(S["h_relu"], at((c - 1) * (MT // 2) + i + 1))
                    for s in range(2):
                        for k in range(KT):
                            ws = slice(k * HID + (2 * i + s) * P, k * HID + (2 * i + s + 1) * P)
                            ks = slice(k * CH, (k + 1) * CH)
                            ins = mm3(ps[:, i, s * CH:(s + 1) * CH], wh[:, epar, ws], wl[:, epar, ws],
                                      xTh[:, par, ks], xTl[:, par, ks], k == 0, k == KT - 1)
                    ins.then_inc(S["h_ready"], 1)

            def output(e, c, par, epar, first_of_expert):
                pe.wait_ge(S["h_rest"], at((c + 1) * (MT // 2)))
                if first_of_expert:
                    pe.wait_ge(S["w_rest"], at(2 * e + 2))
                if later(c, 1):
                    pe.wait_ge(S["y_copied"], at(c - 1))
                for t in range(G):
                    for k in range(MT):
                        hs = slice(k * CH + t * P, k * CH + (t + 1) * P)
                        w2s = slice(KT * HID + k * D, KT * HID + (k + 1) * D)
                        ins = mm3(ps[:, 4 + par, t * D:(t + 1) * D], hh[:, par, hs], hl[:, par, hs],
                                  wh[:, epar, w2s], wl[:, epar, w2s], k == 0, k == MT - 1)
                ins.then_inc(S["y_ready"], 1)

            turn_x(0, 0, 0)
            hidden(0, 0, 0, 0, True)
            turn_x(1, 1, 0)

            def pair(ep, last):
                for aa in range(2):
                    for j in range(CPE):
                        i = aa * CPE + j
                        c = ep * (2 * CPE) + i
                        if not (last and i == 2 * CPE - 1):
                            hidden(ep * 2 + (i + 1) // CPE, c + 1, 1 - i % 2, ((i + 1) // CPE) % 2, (i + 1) % CPE == 0)
                        if not (last and i >= 2 * CPE - 2):
                            turn_x(c + 2, i % 2, ep * CPE + (i + 2) // 2)
                        output(ep * 2 + aa, c, i % 2, aa, j == 0)

            pair(0, False)
            with pe.Fori(1, NE // 2 - 1) as ep:
                pair(Count(ep), False)
            pair(NE // 2 - 1, True)


_INS = ["x", "ctx_1024", "mask_1x1xSxS2_ik0", "L0_xattn_Wq", "L0_xattn_bq", "L0_xattn_Wk", "L0_xattn_bk",
        "L0_xattn_Wv", "L0_xattn_bv", "L0_xattn_Wo", "L0_xattn_bo", "L0_ffn_w_router", "L0_ffn_w1", "L0_ffn_b1",
        "L0_ffn_w2", "L0_ffn_b2"]


def kernel(**inputs):
    import numpy as np
    import concourse.bacc as bacc
    from concourse.bass_utils import run_bass_kernel_spmd

    nc = bacc.Bacc("TRN2", target_bir_lowering=False, num_devices=1)
    arrays, args = {}, []
    for name in _INS:
        a = np.ascontiguousarray(inputs[name])
        arrays[f"in_{name}"] = a
        args.append(nc.dram_tensor(f"in_{name}", a.shape, mybir.dt.from_np(a.dtype), kind="ExternalInput").ap())
    out = nc.dram_tensor("out_0", inputs["x"].shape, F32, kind="ExternalOutput").ap()
    xattn_moe_kernel(nc, *args, out)
    r = run_bass_kernel_spmd(nc, [arrays], core_ids=[0])
    return r.results[0]["out_0"]
```

```python
from contextlib import ExitStack

import concourse.bass as bass
from concourse import mybir

ALU = mybir.AluOpType
ACT = mybir.ActivationFunctionType
AX = mybir.AxisListType
F32 = mybir.dt.float32
F32R = mybir.dt.float32r
F16 = mybir.dt.float16
BF16 = mybir.dt.bfloat16
I32 = mybir.dt.int32
U32 = mybir.dt.uint32

P = 128
NEG = -1.0e30
EPS = 1e-5


class Count:

    def __init__(self, reg, scale=1, offset=0):
        self.reg, self.scale, self.offset = reg, scale, offset

    def __add__(self, n):
        return Count(self.reg, self.scale, self.offset + n)

    def __sub__(self, n):
        return self + -n

    def __mul__(self, n):
        return Count(self.reg, self.scale * n, self.offset * n)

    __radd__, __rmul__ = __add__, __mul__


def at(n):
    if isinstance(n, int):
        return n
    v = n.reg * n.scale if n.scale != 1 else n.reg
    return v + n.offset if n.offset else v


def later(n, first):
    return not isinstance(n, int) or n > first


def at_most(n, top):
    return max(0, min(n, top)) if isinstance(n, int) else n


def xattn_moe_kernel(nc, x, ctx_in, mask, Wq, bq, Wk, bk, Wv, bv, Wo, bo, w_router, w1, b1, w2, b2, out):
    NB, SQ, D = x.shape
    NK = ctx_in.shape[1]
    NE, _, HID = w1.shape
    NH = 16
    DH = D // NH
    KT = D // P
    MT = HID // P
    NTOK = NB * SQ
    NT = NTOK // P
    TPB = SQ // P
    G = 2
    GT = G * P
    NM = NT // G
    MPB = TPB // G
    HK = P // DH
    HU = 4
    UPT = NH // HU
    UPM = G * UPT
    CAP = int(1.5 * NTOK * 2 / NE)
    CH = 256
    CPE = CAP // CH
    NCH = NE * CPE
    SLOTS = NE * CAP
    VW = 3 * DH + 1
    UC = HU * NK
    KC = HK * NK

    x_v = x.rearrange("b (t p) d -> p (b t) d", p=P)
    out_v = out.rearrange("b (t p) d -> p (b t) d", p=P)
    out_rows = out.rearrange("b s d -> (b s) d")
    mask_v = mask.rearrange("a b (t p) k -> p (a b t) k", p=P)
    TOK, GATE, XW = D, D + 1, D + 2
    xe = nc.dram_tensor("expert_in", (SLOTS, XW), F32, kind="Internal").ap()
    xe_v = xe.rearrange("(c t p) d -> p c t d", t=G, p=P)

    with ExitStack() as es:
        def sb(name, shape, dt=F32):
            return es.enter_context(nc.sbuf_tensor(name, shape, dt))

        def sem(name):
            return es.enter_context(nc.semaphore(name))

        shared = sb("shared", [P, 5 * 2 * GT * KT])

        def piece(at_, parts_, *shape):
            n = 1
            for k in shape:
                n *= k
            v = shared[0:parts_, at_:at_ + n]
            if len(shape) == 2:
                return v.rearrange("p (a b) -> p a b", a=shape[0])
            if len(shape) == 3:
                return v.rearrange("p (a b c) -> p a b c", a=shape[0], b=shape[1])
            return v

        wnat = piece(0, P, 4, KT, D)
        cnat = piece(2048, NK, NB, D)
        wkT = piece(2560, P, KT, D)
        wvT = piece(3072, P, KT, D)
        vrest = piece(3584, NK, 2, NB * D)
        vf = piece(4608, NK, NB * D)
        hf = piece(0, P, 2, 2 * CH)
        xc = piece(1024, P, 2, G, XW)
        yb = piece(1024 + 2 * G * XW, P, 2, G, D)
        acc = piece(1024 + 2 * G * (XW + D), P, 2, G, D)
        rows = piece(0, P, G, 2 * XW)
        rows_v = rows.rearrange("p t (k d) -> p t k d", k=2)
        wh = sb("wh", [P, 2, 2 * KT * HID], F32R)

        def early(i, flat=False):
            v = wh[:, 1, i * KT * D:(i + 1) * KT * D]
            return v if flat else v.rearrange("p (k d) -> p k d", k=KT)

        wqh, wql, woh, wol, qh, ql = (early(i) for i in range(6))
        oTh, oTl = early(6, True), early(7, True)
        pb = sb("pb", [P, 2, UC])
        mraw = pb[:].rearrange("p a b -> p (a b)")[:, 0:TPB * NK].bitcast(I32).rearrange("p (t k) -> p t k", t=TPB)
        zrow = sb("zrow", [P, XW])
        identf = sb("identf", [P, P])
        identb = sb("identb", [P, P], BF16)
        before = sb("before", [P, P], BF16)
        onesb = sb("onesb", [P, P], BF16)
        blockh = sb("blockh", [P, HK])
        mhalf = sb("mhalf", [P, G])
        iota_e = sb("iota_e", [P, NE])
        base_e = sb("base_e", [P, NE])
        tokid = sb("tokid", [P, NT, 2])
        xs = sb("xs", [P, NT, D])
        brow = sb("brow", [NE * MT + 2 * KT, P])
        bcol = sb("bcol", [P, NE * MT + 2 * KT])
        bo_b = sb("bo_b", [P, D])
        bv_b = sb("bv_b", [NK, D])
        b2_b = sb("b2_b", [P, NE, D])
        wr = sb("wr", [P, KT, NE])
        cT = sb("cT", [P, KT, NB * NK])
        ktf = sb("ktf", [P, KT, NB * NK])
        kth = sb("kth", [P, KT, NB * NK], F32R)
        ktl = sb("ktl", [P, KT, NB * NK])
        vcat = sb("vcat", [NK, NB, NH, VW], BF16)
        mb = sb("mb", [P, NT, NK], BF16)
        st = sb("st", [P, G, 6])
        mv = sb("mv", [P, G, 2])
        rstd = sb("rstd", [P, G])
        xn = sb("xn", [P, G, D])
        xTh = sb("xTh", [P, 2, KT * GT], F32R)
        xTl = sb("xTl", [P, 2, KT * GT], F32R)
        nmx = sb("nmx", [P, 2, HU])
        pth = sb("pth", [NK, 2, HU * P], F16)
        ptl = sb("ptl", [NK, 2, HU * P], F16)
        osum = sb("osum", [P, HU * DH])
        rinv = sb("rinv", [P, HU])
        o = sb("o", [P, G, D])
        xbo = sb("xbo", [P, G, D])
        st2 = sb("st2", [P, G, 6])
        mv2 = sb("mv2", [P, G, 2])
        rstd2 = sb("rstd2", [P, G])
        xn2 = sb("xn2", [P, G, D])
        x2T = sb("x2T", [P, KT * GT])
        lg = sb("lg", [P, G, NE])
        top = sb("top", [P, G, 8])
        tix = sb("tix", [P, G, 8], U32)
        ek = sb("ek", [P, G, 2])
        oh = sb("oh", [P, G, 2, NE])
        ohs = sb("ohs", [P, G, NE], BF16)
        run = sb("run", [P, 2, NE], BF16)
        slotv = sb("slotv", [P, G, NE])
        pick = sb("pick", [P, G, 2, NE])
        sk = sb("sk", [P, G, 2])
        eb = sb("eb", [P, G, 2])
        pos = sb("pos", [P, G, 2])
        kp = sb("kp", [P, G, 2])
        sidx = sb("sidx", [P, G, 2], I32)
        gd = sb("gd", [P, G])
        ge = sb("ge", [P, G])
        g1 = sb("g1", [P, G])
        gt = sb("gt", [P, G, 2])
        ctok = sb("ctok", [P, 2, G], I32)
        cgate = sb("cgate", [P, 2, G])
        wraw = sb("wraw", [P, 2 * KT * HID])
        wl = sb("wl", [P, 2, 2 * KT * HID], F32R)
        hh = sb("hh", [P, 2, MT * CH], F32R)
        hl = sb("hl", [P, 2, MT * CH], F32R)
        kbh = hh[:].rearrange("p a b -> p (a b)")[:, 0:NB * KT * KC].rearrange("p (b r c) -> p b r c", b=NB, r=KT)
        kbl = hl[:].rearrange("p a b -> p (a b)")[:, 0:NB * KT * KC].rearrange("p (b r c) -> p b r c", b=NB, r=KT)

        ps = es.enter_context(nc.psum_tensor("ps", [P, 8, 512], F32))
        SC, PT, PV, TR, QB, WB = 0, 2, 4, 5, 6, 7

        def bank(i, k):
            return ps[:, i, :].rearrange("p (a b) -> p a b", a=k)

        S = {n: sem(n) for n in (
            "const_ready", "const_step", "x_loaded", "w_loaded", "w2_loaded", "small_loaded", "b2_loaded", "bias_loaded", "kb_head", "kb_rest", "v_split", "mask_loaded",
            "pe_setup", "act_setup", "dve_setup", "mask_ready",
            "xT_ready", "q_ready", "sc_ready", "pt_ready", "pv_ready", "oT_ready", "wo_ready", "x2T_ready",
            "lg_ready", "pos_ready",
            "stat_step", "rstd_ready", "rstd2_ready", "xn_ready", "xT_split", "xT_rest", "q_split", "q_rest", 
            "max_ready", "exp_ready",
            "pth_ready", "ptl_ready", "o_done", "oT_split", "oT_rest",
            "xbo_ready", "x1_ready", "stat2_step", "xn2_ready", "x2T_copied",
            "lg_copied", "top_ready", "tix_ready", "route_step", "oh_ready", "run_ready", "slot_ready", "pick_ready",
            "sk_ready", "scattered", "zero_done", "rows_ready", "osum_part", "vpart_step",
            "wraw_loaded0", "wraw_loaded1", "w_head", "w_rest", "xc_loaded0", "xc_loaded1", "fxT_ready", "fxT_head", "fxT_rest",
            "h_ready", "h_relu", "h_head", "h_rest", "y_ready", "y_copied",
            "gd_ready", "ge_ready", "gate_step", "gates_ready", "x1_stored", "acc_clear", "tags_ready", "acc_gathered0", "acc_gathered1",
            "fin_ready", "y_scattered0", "y_scattered1",
        )}

        block = es.enter_context(nc.Block())

        def vpart(i):
            return vcat[:, :, :, i * DH:(i + 1) * DH]

        def vview(t_):
            return t_.rearrange("p (b h d) -> p b h d", b=NB, h=NH)

        def macro_loop(eng, body):
            body(0)
            body(1)
            with eng.Fori(2, NM - 2) as m:
                body(Count(m))
            body(NM - 2)
            body(NM - 1)
            body(NM)
            body(NM + 1)

        def wait_apart(eng):
            eng.nop(nofuse=True)

        def batch_of(m):
            return at(m) // MPB

        def parts(m):
            if not isinstance(m, int):
                return True, True, True, True, True
            return m < NM, m + 1 < NM, m + 2 < NM, 1 <= m <= NM, 2 <= m <= NM + 1

        def ending(m):
            return isinstance(m, int) and m >= NM

        @block.sync
        def _(sp):
            half = NT // 2
            sp.dma_start(wnat[:, 0], Wq.rearrange("(r p) d -> p r d", p=P)).then_inc(S["w_loaded"], 16)
            sp.dma_start(wnat[:, 1], Wk.rearrange("(r p) d -> p r d", p=P)).then_inc(S["w_loaded"], 16)
            sp.dma_start(cnat, ctx_in.rearrange("b k d -> k b d")).then_inc(S["w_loaded"], 16)
            sp.dma_start(wnat[:, 2], Wv.rearrange("(r p) d -> p r d", p=P)).then_inc(S["w2_loaded"], 16)
            sp.dma_start(wnat[:, 3], Wo.rearrange("(r p) d -> p r d", p=P)).then_inc(S["w2_loaded"], 16)
            sp.dma_start(bv_b[:], bv.rearrange("(a d) -> a d", a=1).partition_broadcast(NK)).then_inc(S["small_loaded"], 16)
            sp.dma_start(bo_b[:], bo.rearrange("(a d) -> a d", a=1).partition_broadcast(P)).then_inc(S["small_loaded"], 16)
            sp.dma_start(wr[:], w_router.rearrange("(r p) e -> p r e", p=P)).then_inc(S["small_loaded"], 16)
            sp.wait_ge(S["const_ready"], 1)
            xz = xe[0:SLOTS, :].rearrange("(p r) d -> p (r d)", p=P)
            for i in range(SLOTS // P // 8):
                sp.dma_start(xz[:, i * 8 * XW:(i + 1) * 8 * XW].rearrange("p (r d) -> p r d", d=XW),
                             zrow[:].unsqueeze(1).to_broadcast([P, 8, XW])).then_inc(S["zero_done"], 16)
            def load_weights(e, half):
                if later(e, 0):
                    sp.wait_ge(S["w_head"], at(2 * e + half - 1))
                    sp.wait_ge(S["w_rest"], at(2 * e + half - 1))
                if half == 0:
                    sp.dma_start(wraw[:, 0:KT * HID].rearrange("p (k h) -> p k h", k=KT),
                                 w1[at(e)].rearrange("(k p) h -> p k h", p=P)).then_inc(S["wraw_loaded0"], 16)
                else:
                    sp.dma_start(wraw[:, KT * HID:].rearrange("p (k d) -> p k d", k=MT),
                                 w2[at(e)].rearrange("(k p) d -> p k d", p=P)).then_inc(S["wraw_loaded1"], 16)

            def load_chunk(c, par):
                if later(c, 1):
                    sp.wait_ge(S["fxT_ready"], at(c - 1))
                    sp.wait_ge(S["tags_ready"], at(c - 1))
                sp.dma_start(xc[:, par], xe_v[:, at(c)]).then_inc(S["xc_loaded%d" % par], 16)

            sp.dma_start(b2_b[:], b2.rearrange("(a e) d -> a e d", a=1).partition_broadcast(P)).then_inc(S["b2_loaded"], 16)
            load_weights(0, 0)
            load_weights(0, 1)
            load_weights(1, 0)
            load_weights(1, 1)
            for i in range(NM // 2):
                ts = slice(i * 2 * G, (i + 1) * 2 * G)
                sp.wait_ge(S["x1_ready"], 2 * (i + 1))
                sp.dma_start(out_v[:, ts], xs[:, ts]).then_inc(S["x1_stored"], 16)
            sp.wait_ge(S["scattered"], at(16 * 2 * NT))
            load_chunk(0, 0)
            load_chunk(1, 1)

            def pair(ep, last):
                for a in range(2):
                    e = ep * 2 + a
                    for j in range(CPE):
                        i = a * CPE + j
                        c = ep * (2 * CPE) + i
                        if not (last and i >= 2 * CPE - 2):
                            load_chunk(c + 2, i % 2)
                        if not last and j >= 1:
                            load_weights(e + 2, j - 1)

            pair(0, False)
            with sp.Fori(1, NE // 2 - 1) as ep:
                pair(Count(ep), False)
            pair(NE // 2 - 1, True)

        @block.gpsimd
        def _(pool):
            g = nc.gpsimd
            g.memset(zrow[:, 0:TOK], 0.0)
            g.memset(zrow[:, TOK:TOK + 1], float(NTOK))
            g.memset(zrow[:, GATE:GATE + 1], 0.0).then_inc(S["const_ready"], 1)
            g.memset(identf[:], 0.0)
            g.memset(identb[:], 0.0)
            g.memset(before[:], 1.0)
            g.memset(onesb[:], 1.0)
            g.memset(mhalf[:], -0.5)
            g.memset(run[:], 0.0)
            g.memset(ohs[:], 0.0)
            g.memset(blockh[:], 1.0)
            g.memset(vcat[:, :, :, 3 * DH:VW], 1.0)
            g.iota(iota_e[:], pattern=[[1, NE]], base=0, channel_multiplier=0, allow_small_or_imprecise_dtypes=True)
            g.iota(base_e[:], pattern=[[CAP, NE]], base=0, channel_multiplier=0, allow_small_or_imprecise_dtypes=True)
            g.iota(tokid[:], pattern=[[P, NT], [0, 2]], base=0, channel_multiplier=1,
                   allow_small_or_imprecise_dtypes=True).then_inc(S["const_step"], 1)
            pool.wait_ge(S["const_step"], 1)
            g.affine_select(out=identf[:], in_=identf[:], compare_op=ALU.not_equal, fill=1.0, base=0,
                            pattern=[[-1, P]], channel_multiplier=1)
            g.affine_select(out=identb[:], in_=identb[:], compare_op=ALU.not_equal, fill=1.0, base=0,
                            pattern=[[-1, P]], channel_multiplier=1)
            g.affine_select(out=before[:], in_=before[:], compare_op=ALU.is_gt, fill=0.0, base=0,
                            pattern=[[1, P]], channel_multiplier=-1)
            g.affine_select(out=blockh[:], in_=blockh[:], compare_op=ALU.is_ge, fill=0.0, base=0,
                            pattern=[[-DH, HK]], channel_multiplier=1).then_inc(S["const_step"], 1)
            pool.wait_ge(S["const_step"], 2)
            g.affine_select(out=blockh[:], in_=blockh[:], compare_op=ALU.is_ge, fill=0.0, base=DH - 1,
                            pattern=[[DH, HK]], channel_multiplier=-1).then_inc(S["const_ready"], 1)

            def inverse_std(m_, r_, tag, done, n):
                pool.wait_ge(S[tag], at(2 * G * (n + 1)))
                wait_apart(pool)
                g.tensor_scalar(r_[:], m_[:, :, 1], EPS, None, ALU.add).then_inc(S[done], 1)
                pool.wait_ge(S[done], at(2 * n + 1))
                wait_apart(pool)
                g.tensor_tensor(r_[:], r_[:], mhalf[:], ALU.pow).then_inc(S[done], 1)

            def norm1(m):
                if later(m, 0):
                    pool.wait_ge(S["xT_ready"], at(m))
                inverse_std(mv, rstd, "stat_step", "rstd_ready", m)
                if isinstance(m, int) and m == 0:
                    return
                pool.wait_ge(S["rstd_ready"], at(2 * (m + 1)))
                wait_apart(pool)
                g.tensor_tensor(xn[:], xs[:, bass.ds(at(m * G), G), :], mv[:, :, 0:1].to_broadcast([P, G, D]),
                                ALU.subtract).then_inc(S["xn_ready"], 1)
                pool.wait_ge(S["xn_ready"], at(2 * m + 1))
                wait_apart(pool)
                g.tensor_tensor(xn[:], xn[:], rstd[:].unsqueeze(2).to_broadcast([P, G, D]),
                                ALU.mult).then_inc(S["xn_ready"], 1)

            norm1(0)
            def blocks(b):
                for r in range(KT):
                    ins = g.tensor_tensor(kbl[:, b, r, :].rearrange("p (h k) -> p h k", h=HK),
                                          ktl[:, r, b * NK:(b + 1) * NK].unsqueeze(1).to_broadcast([P, HK, NK]),
                                          blockh[:].unsqueeze(2).to_broadcast([P, HK, NK]), ALU.mult)
                ins.then_inc(S["kb_rest"], 1)

            pool.wait_ge(S["dve_setup"], 4)
            blocks(0)
            norm1(1)
            blocks(1)
            pool.wait_ge(S["zero_done"], at(16 * (SLOTS // P // 8)))

            def body(m):
                units, qn, pre, tail, slots = parts(m)
                if pre:
                    norm1(m + 2)
                if slots:
                    n = m - 2
                    base = n * 7
                    pool.wait_ge(S["oh_ready"], at(2 * (n + 1)))
                    wait_apart(pool)
                    g.tensor_tensor(run[:, 0, :], run[:, 1, :], ohs[:, 1, :], ALU.add).then_inc(S["route_step"], 1)
                    pool.wait_ge(S["route_step"], at(base + 1))
                    wait_apart(pool)
                    g.tensor_tensor(ohs[:], oh[:, :, 0, :], oh[:, :, 1, :], ALU.add).then_inc(S["route_step"], 1)
                    pool.wait_ge(S["route_step"], at(base + 2))
                    wait_apart(pool)
                    g.tensor_tensor(run[:, 1, :], run[:, 0, :], ohs[:, 0, :], ALU.add).then_inc(S["run_ready"], 1)
                    g.tensor_scalar(eb[:], ek[:], float(CAP), None, ALU.mult).then_inc(S["route_step"], 1)
                if slots:
                    pool.wait_ge(S["slot_ready"], at(n + 1))
                    wait_apart(pool)
                    for t in range(G):
                        g.tensor_tensor(pick[:, t], oh[:, t], slotv[:, t, :].unsqueeze(1).to_broadcast([P, 2, NE]),
                                        ALU.mult).then_inc(S["pick_ready"], 1)
                if tail:
                    inverse_std(mv2, rstd2, "stat2_step", "rstd2_ready", m - 1)
                if units:
                    if later(m, 0):
                        pool.wait_ge(S["x1_ready"], at(m))
                        wait_apart(pool)
                    else:
                        pool.wait_ge(S["small_loaded"], at(16 * 3))
                    g.tensor_tensor(xbo[:], xs[:, bass.ds(at(m * G), G), :],
                                    bo_b[:].unsqueeze(1).to_broadcast([P, G, D]), ALU.add).then_inc(S["xbo_ready"], 1)
                if slots:
                    pool.wait_ge(S["sk_ready"], at(n + 1))
                    pool.wait_ge(S["route_step"], at(base + 3))
                    wait_apart(pool)
                    g.tensor_tensor(pos[:], sk[:], eb[:], ALU.subtract).then_inc(S["route_step"], 1)
                    pool.wait_ge(S["route_step"], at(base + 4))
                    wait_apart(pool)
                    g.tensor_scalar(kp[:], pos[:], float(CAP), float(SLOTS), ALU.is_ge, ALU.mult).then_inc(S["route_step"], 1)
                    pool.wait_ge(S["gates_ready"], at(n + 1))
                    if ending(m):
                        pool.wait_ge(S["scattered"], n * (2 * G * 16))
                    wait_apart(pool)
                    g.tensor_copy(rows_v[:, :, :, TOK], tokid[:, bass.ds(at(n * G), G), :])
                    g.tensor_copy(rows_v[:, :, :, GATE], gt[:])
                    pool.wait_ge(S["route_step"], at(base + 5))
                    wait_apart(pool)
                    g.tensor_tensor(kp[:], kp[:], sk[:], ALU.add).then_inc(S["route_step"], 1)
                    pool.wait_ge(S["route_step"], at(base + 6))
                    wait_apart(pool)
                    g.tensor_copy(sidx[:], kp[:]).then_inc(S["route_step"], 1)
                    pool.wait_ge(S["route_step"], at(base + 7))
                    pool.wait_ge(S["rows_ready"], at(n + 1))
                    wait_apart(pool)
                    for t in range(G):
                        for k in range(2):
                            g.indirect_dma_start(xe, bass.IndirectOffsetOnAxis(ap=sidx[:, t, k:k + 1], axis=0),
                                                 rows[:, t, k * XW:(k + 1) * XW], None, bounds_check=SLOTS - 1,
                                                 oob_is_err=False).then_inc(S["scattered"], 16)
                    if not ending(m + 1):
                        pool.wait_ge(S["scattered"], at((n + 1) * (2 * G * 16)))
                if isinstance(m, int) and m == 1:
                    g.memset(acc, 0.0).then_inc(S["acc_clear"], 1)
                    for half in range(2):
                        hs = slice(half * KT * HID, (half + 1) * KT * HID)
                        pool.wait_ge(S["w_head"], half + 1)
                        g.tensor_tensor(wl[:, 0, hs], wraw[:, hs], wh[:, 0, hs].bitcast(F32),
                                        ALU.subtract).then_inc(S["w_rest"], 1)

            macro_loop(pool, body)

            def tags(c, par, half):
                pool.wait_ge(S["xc_loaded%d" % par], at((half + 1) * 16))
                if later(c, 1):
                    scattered(par, half)
                wait_apart(pool)
                g.tensor_copy(ctok[:, par, :], xc[:, par, :, TOK])
                g.tensor_copy(cgate[:, par, :], xc[:, par, :, GATE]).then_inc(S["tags_ready"], 1)

            def scattered(par, n):
                pool.wait_ge(S["y_scattered%d" % par], at(n * (G * 16)))

            def gather(c, par):
                pool.wait_ge(S["tags_ready"], at(c + 1))
                wait_apart(pool)
                for t in range(G):
                    g.indirect_dma_start(acc[:, par, t, :], None, out_rows,
                                         bass.IndirectOffsetOnAxis(ap=ctok[:, par, t:t + 1], axis=0),
                                         bounds_check=NTOK - 1, oob_is_err=False).then_inc(S["acc_gathered%d" % par], 16)

            def scatter(c, par):
                pool.wait_ge(S["fin_ready"], at(c + 1))
                wait_apart(pool)
                for t in range(G):
                    g.indirect_dma_start(out_rows, bass.IndirectOffsetOnAxis(ap=ctok[:, par, t:t + 1], axis=0),
                                         yb[:, par, t, :], None,
                                         bounds_check=NTOK - 1, oob_is_err=False).then_inc(S["y_scattered%d" % par], 16)

            tags(0, 0, 0)
            pool.wait_ge(S["x1_stored"], 16 * (NM // 2))
            pool.wait_ge(S["acc_clear"], 1)
            gather(0, 0)

            def pair(ep, last):
                for aa in range(2):
                    for j in range(CPE):
                        i = aa * CPE + j
                        c = ep * (2 * CPE) + i
                        half = ep * CPE + (i + 1) // 2
                        more = not (last and i == 2 * CPE - 1)
                        if more:
                            tags(c + 1, 1 - i % 2, half)
                        if j < CPE - 1:
                            gather(c + 1, 1 - i % 2)
                        scatter(c, i % 2)
                        if j == CPE - 1 and more:
                            scattered(0, ep * CPE + i // 2 + 1)
                            scattered(1, ep * CPE + (i + 1) // 2)
                            wait_apart(pool)
                            gather(c + 1, 1 - i % 2)

            pair(0, False)
            with pool.Fori(1, NE // 2 - 1) as ep:
                pair(Count(ep), False)
            pair(NE // 2 - 1, True)
            scattered(0, (NCH + 1) // 2)
            scattered(1, NCH // 2)

        @block.scalar
        def _(act):
            a = nc.scalar
            act.dma_start(xs[:, 0:2], x_v[:, 0:2]).then_inc(S["x_loaded"], 16)
            nb1 = NE * MT
            act.dma_start(brow[nb1:nb1 + KT, :], bq.rearrange("(m p) -> m p", p=P)).then_inc(S["bias_loaded"], 16)
            act.dma_start(brow[nb1 + KT:nb1 + 2 * KT, :], bk.rearrange("(m p) -> m p", p=P)).then_inc(S["bias_loaded"], 16)
            act.dma_start(mraw, mask_v).then_inc(S["mask_loaded"], 16)
            act.dma_start(brow[0:nb1, :], b1.rearrange("e (m p) -> (e m) p", p=P)).then_inc(S["bias_loaded"], 16)
            act.wait_ge(S["x_loaded"], 16)
            act.dma_start(xs[:, 2:NT], x_v[:, 2:NT]).then_inc(S["x_loaded"], 16)
            act.wait_ge(S["pe_setup"], 1)
            a.activation(wqh.rearrange("p k d -> p (k d)"), ps[:, 0, :], ACT.Copy).then_inc(S["act_setup"], 1)
            act.wait_ge(S["pe_setup"], 2)
            a.activation(wkT.rearrange("p k d -> p (k d)"), ps[:, 1, :], ACT.Copy).then_inc(S["act_setup"], 1)
            act.wait_ge(S["pe_setup"], 3)
            a.activation(cT[:].rearrange("p k d -> p (k d)"), ps[:, 2, 0:KT * NB * NK], ACT.Copy).then_inc(S["act_setup"], 1)
            def split_xT(m):
                act.wait_ge(S["xT_ready"], at(m + 1))
                if later(m, 0):
                    act.wait_ge(S["q_ready"], at(m))
                a.activation(xTh[:, 0, :], ps[:, TR, :], ACT.Copy).then_inc(S["xT_split"], 1)

            def split_q(m, t):
                act.wait_ge(S["q_ready"], at(m + 1))
                if later(m, 0):
                    act.wait_ge(S["sc_ready"], at(UPM * (m - 1) + UPT * (t + 1)))
                if t == 1:
                    act.wait_ge(S["q_rest"], at(2 * m + 1))
                for r in range(KT):
                    ins = a.activation(qh[:, r, t * P:(t + 1) * P], bank(QB, KT)[:, r, t * P:(t + 1) * P], ACT.Identity,
                                       bias=bcol[:, nb1 + r:nb1 + r + 1])
                ins.then_inc(S["q_split"], 1)

            def exp(m, j, par):
                u = UPM * m + j
                act.wait_ge(S["max_ready"], at(u + 1))
                if later(u, 1):
                    act.wait_ge(S["pt_ready"], at(u - 1))
                for h in range(HU):
                    hs = slice(h * NK, (h + 1) * NK)
                    ins = a.activation(pb[:, par, hs], ps[:, SC + par, hs], ACT.Exp, bias=nmx[:, par, h:h + 1])
                ins.then_inc(S["exp_ready"], 1)

            def split_oT(m, t):
                act.wait_ge(S["oT_ready"], at(2 * m + t + 1))
                if later(m, 0):
                    act.wait_ge(S["wo_ready"], at(m))
                o3 = oTh.rearrange("p (k c) -> p k c", k=KT)
                a.activation(o3[:, :, t * P:(t + 1) * P], bank(TR, KT)[:, :, t * P:(t + 1) * P],
                             ACT.Copy).then_inc(S["oT_split"], 1)

            def head_pt(u, par):
                act.wait_ge(S["pt_ready"], at(u + 1))
                if later(u, 1):
                    act.wait_ge(S["pv_ready"], at(u - 1))
                a.activation(pth[:, par, :], ps[0:NK, PT + par, :], ACT.Copy).then_inc(S["pth_ready"], 1)

            split_xT(0)
            act.wait_ge(S["pe_setup"], 5)
            a.activation(bcol[:], ps[:, 4, 0:NE * MT + 2 * KT], ACT.Copy).then_inc(S["act_setup"], 1)
            act.wait_ge(S["pe_setup"], 6)
            a.activation(wvT.rearrange("p k d -> p (k d)"), ps[:, 3, :], ACT.Copy).then_inc(S["act_setup"], 1)
            act.wait_ge(S["act_setup"], 4)
            split_q(0, 0)
            split_q(0, 1)
            act.wait_ge(S["pe_setup"], 8)
            a.activation(woh.rearrange("p k d -> p (k d)"), ps[:, WB, :], ACT.Copy).then_inc(S["act_setup"], 1)
            act.wait_ge(S["dve_setup"], 5)
            a.activation(vpart(0), vview(vf), ACT.Copy).then_inc(S["vpart_step"], 1)
            exp(0, 0, 0)
            act.wait_ge(S["vpart_step"], 2)
            a.activation(vpart(1), vview(vrest[:, 0, :]), ACT.Copy).then_inc(S["vpart_step"], 1)
            act.wait_ge(S["vpart_step"], 4)
            a.activation(vpart(2), vview(vrest[:, 1, :]), ACT.Copy).then_inc(S["v_split"], 1)

            def body(m):
                units, qn, pre, tail, slots = parts(m)
                for j in range(UPM):
                    if units:
                        head_pt(UPM * m + j, j % 2)
                        if j < UPM - 1:
                            exp(m, j + 1, 1 - j % 2)
                        elif qn:
                            exp(m + 1, 0, 0)
                    if j == 0 and slots:
                        act.wait_ge(S["x2T_ready"], at(m - 1))
                        a.activation(x2T[:], ps[:, TR, :], ACT.Copy).then_inc(S["x2T_copied"], 1)
                    if j == 1 and qn:
                        split_xT(m + 1)
                    if j == 3 and qn:
                        split_q(m + 1, 0)
                    if j == 3 and tail:
                        split_oT(m - 1, 1)
                    if j == 4 and slots:
                        act.wait_ge(S["gd_ready"], at(m - 1))
                        a.activation(ge[:], gd[:], ACT.Exp).then_inc(S["ge_ready"], 1)
                    if j == 5 and slots:
                        n = m - 2
                        act.wait_ge(S["xn2_ready"], at(2 * (n + 1)))
                        if ending(m):
                            act.wait_ge(S["scattered"], n * (2 * G * 16))
                        else:
                            act.wait_ge(S["route_step"], at(7 * n + 1))
                        a.activation(rows_v[:, :, :, 0:D], xn2[:].unsqueeze(2).to_broadcast([P, G, 2, D]),
                                     ACT.Copy).then_inc(S["rows_ready"], 1)
                    if j == 6 and qn:
                        split_q(m + 1, 1)
                    if j == 6 and units:
                        split_oT(m, 0)
                    if isinstance(m, int) and m == 1 and j in (2, 5):
                        head(0, 0, j // 3)

            def head(e, par, half):
                act.wait_ge(S["wraw_loaded%d" % half], at(16 * (e + 1)))
                if later(e, 1):
                    if half == 0:
                        act.wait_ge(S["h_ready"], at((e - 1) * (CPE * MT // 2)))
                    else:
                        act.wait_ge(S["y_ready"], at((e - 1) * CPE))
                hs = slice(half * KT * HID, (half + 1) * KT * HID)
                a.activation(wh[:, par, hs], wraw[:, hs], ACT.Copy).then_inc(S["w_head"], 1)

            macro_loop(act, body)

            def ffn_xT(c, par):
                act.wait_ge(S["fxT_ready"], at(c + 1))
                a.activation(xTh[:, par, :], ps[:, 6, :], ACT.Copy).then_inc(S["fxT_head"], 1)

            def ffn_h(e, c, par):
                for i in range(MT // 2):
                    act.wait_ge(S["h_ready"], at(c * (MT // 2) + i + 1))
                    if later(c * (MT // 2) + i, 1):
                        act.wait_ge(S["h_rest"], at(c * (MT // 2) + i - 1))
                        wait_apart(act)
                    for s in range(2):
                        ins = a.activation(hf[:, i % 2, s * CH:(s + 1) * CH], ps[:, i, s * CH:(s + 1) * CH], ACT.Relu,
                                           bias=bcol[:, bass.ds(at(e * MT + 2 * i + s), 1)])
                    ins.then_inc(S["h_relu"], 1)
                    act.wait_ge(S["h_relu"], at(c * (MT // 2) + i + 1))
                    if i == 0 and (later(c, 1)):
                        act.wait_ge(S["y_ready"], at(c - 1))
                    a.activation(hh[:, par, 2 * i * CH:2 * (i + 1) * CH], hf[:, i % 2, :],
                                 ACT.Copy).then_inc(S["h_head"], 1)

            ffn_xT(0, 0)
            ffn_xT(1, 1)
            ffn_h(0, 0, 0)

            def pair(ep, last):
                for aa in range(2):
                    for j in range(CPE):
                        i = aa * CPE + j
                        c = ep * (2 * CPE) + i
                        if not (last and i == 2 * CPE - 1):
                            ffn_h(ep * 2 + (i + 1) // CPE, c + 1, 1 - i % 2)
                        if j < 2 and not (last and aa == 1):
                            head(ep * 2 + 1 + aa, 1 - aa, j)
                        if not (last and i >= 2 * CPE - 2):
                            ffn_xT(c + 2, i % 2)

            pair(0, False)
            with act.Fori(1, NE // 2 - 1) as ep:
                pair(Count(ep), False)
            pair(NE // 2 - 1, True)

        @block.vector
        def _(dve):
            v = nc.vector
            nb1 = NE * MT
            dve.wait_ge(S["mask_loaded"], 16)
            for b in range(NB):
                ins = v.tensor_scalar(mb[:, b * TPB:(b + 1) * TPB, :], mraw, 0.0, NEG, ALU.is_equal, ALU.mult)
            ins.then_inc(S["mask_ready"], 1)

            def stats(src, s_, m_, tag, n):
                for t in range(G):
                    v.bn_stats(s_[:, t, :], src(t)).then_inc(S[tag], 1)
                for t in range(G):
                    dve.wait_ge(S[tag], at(n * (2 * G) + 1 + t))
                    wait_apart(dve)
                    v.bn_aggr(m_[:, t, :], s_[:, t, :]).then_inc(S[tag], 1)

            def stats1(m):
                if isinstance(m, int):
                    dve.wait_ge(S["x_loaded"], 16 if m == 0 else 32)
                if later(m, 0):
                    dve.wait_ge(S["xn_ready"], at(2 * m - 1))
                    wait_apart(dve)
                stats(lambda t: xs[:, at(m * G + t), :], st, mv, "stat_step", m)

            def rest_xT(m):
                dve.wait_ge(S["xT_split"], at(m + 1))
                if later(m, 0):
                    dve.wait_ge(S["q_ready"], at(m))
                v.tensor_tensor(xTl[:, 0, :], ps[:, TR, :], xTh[:, 0, :].bitcast(F32),
                                ALU.subtract).then_inc(S["xT_rest"], 1)

            def rest_q(m, t):
                dve.wait_ge(S["q_split"], at(2 * m + t + 1))
                ts = slice(t * P, (t + 1) * P)
                for r in range(KT):
                    ins = v.scalar_tensor_tensor(out=ql[:, r, ts], in0=bank(QB, KT)[:, r, ts],
                                                 scalar=bcol[:, nb1 + r:nb1 + r + 1], in1=qh[:, r, ts].bitcast(F32),
                                                 op0=ALU.add, op1=ALU.subtract)
                ins.then_inc(S["q_rest"], 1)

            def maximum(u, par):
                dve.wait_ge(S["sc_ready"], at(u + 1))
                v.tensor_reduce(nmx[:, par, :], ps[:, SC + par, 0:UC].rearrange("p (h k) -> p h k", k=NK), AX.X,
                                ALU.max, negate=True).then_inc(S["max_ready"], 1)

            def rest_oT(m, t):
                dve.wait_ge(S["oT_split"], at(2 * m + t + 1))
                ts = slice(t * P, (t + 1) * P)
                v.tensor_tensor(oTl.rearrange("p (k c) -> p k c", k=KT)[:, :, ts], bank(TR, KT)[:, :, ts],
                                oTh.bitcast(F32).rearrange("p (k c) -> p k c", k=KT)[:, :, ts],
                                ALU.subtract).then_inc(S["oT_rest"], 1)

            def rest_pt(u, par):
                dve.wait_ge(S["pth_ready"], at(u + 1))
                v.tensor_tensor(ptl[:, par, :], ps[0:NK, PT + par, :], pth[:, par, :],
                                ALU.subtract).then_inc(S["ptl_ready"], 1)

            def sum_o(u):
                dve.wait_ge(S["pv_ready"], at(u + 1))
                if later(u, 0):
                    dve.wait_ge(S["o_done"], at(u))
                pv = ps[:, PV, 0:HU * VW].rearrange("p (h c) -> p h c", h=HU)
                v.tensor_reduce(osum[:].rearrange("p (h d) -> p h d", h=HU),
                                pv[:, :, 0:3 * DH].rearrange("p h (s d) -> p h d s", s=3), AX.X,
                                ALU.add).then_inc(S["osum_part"], 1)
                v.reciprocal(rinv[:], pv[:, :, 3 * DH]).then_inc(S["osum_part"], 1)

            def divide_o(m, j):
                dve.wait_ge(S["osum_part"], at(2 * (UPM * m + j + 1)))
                if j % UPT == 0 and later(m, 0):
                    dve.wait_ge(S["oT_ready"], at(2 * m - 1 + j // UPT))
                t, quarter = j // UPT, j % UPT
                v.tensor_tensor(o[:, t, quarter * HU * DH:(quarter + 1) * HU * DH].rearrange("p (h d) -> p h d", h=HU),
                                osum[:].rearrange("p (h d) -> p h d", h=HU),
                                rinv[:].unsqueeze(2).to_broadcast([P, HU, DH]), ALU.mult).then_inc(S["o_done"], 1)

            def v_rest(i):
                dve.wait_ge(S["vpart_step"], 2 * i + 1)
                whole = vview(vrest[:, 0, :]) if i else vview(vf)
                for b in range(NB):
                    ins = v.tensor_tensor(vview(vrest[:, i, :])[:, b], whole[:, b], vpart(i)[:, b], ALU.subtract)
                ins.then_inc(S["vpart_step"], 1)

            stats1(0)
            dve.wait_ge(S["act_setup"], 1)
            v.tensor_tensor(wql.rearrange("p k d -> p (k d)"), ps[:, 0, :],
                            wqh.rearrange("p k d -> p (k d)").bitcast(F32), ALU.subtract).then_inc(S["dve_setup"], 1)
            dve.wait_ge(S["rstd_ready"], 2)
            for t in range(G):
                v.tensor_scalar(xn[:, t, :], xs[:, t, :], mv[:, t, 0:1], rstd[:, t:t + 1],
                                ALU.subtract, ALU.mult).then_inc(S["xn_ready"], 1)
            rest_xT(0)
            dve.wait_ge(S["pe_setup"], 4)
            dve.wait_ge(S["act_setup"], 4)
            for r in range(KT):
                ins = v.tensor_scalar(ktf[:, r, :], ps[:, 1, r * NB * NK:(r + 1) * NB * NK],
                                      bcol[:, nb1 + KT + r:nb1 + KT + r + 1], DH ** -0.5, ALU.add, ALU.mult)
            ins.then_inc(S["dve_setup"], 1)
            dve.wait_ge(S["dve_setup"], 2)
            v.tensor_copy(kth[:], ktf[:]).then_inc(S["dve_setup"], 1)
            dve.wait_ge(S["dve_setup"], 3)
            v.tensor_tensor(ktl[:], ktf[:], kth[:].bitcast(F32), ALU.subtract).then_inc(S["dve_setup"], 1)
            dve.wait_ge(S["const_ready"], 2)

            def blocks(b):
                for r in range(KT):
                    ins = v.tensor_tensor(kbh[:, b, r, :].rearrange("p (h k) -> p h k", h=HK),
                                          kth[:, r, b * NK:(b + 1) * NK].bitcast(F32).unsqueeze(1).to_broadcast([P, HK, NK]),
                                          blockh[:].unsqueeze(2).to_broadcast([P, HK, NK]), ALU.mult)
                ins.then_inc(S["kb_head"], 1)

            blocks(0)
            rest_q(0, 0)
            stats1(1)
            rest_q(0, 1)
            dve.wait_ge(S["pe_setup"], 7)
            dve.wait_ge(S["small_loaded"], at(16 * 3))
            v.tensor_tensor(vf.rearrange("p (b d) -> p b d", b=NB), ps[0:NK, 3, :].rearrange("p (b d) -> p b d", b=NB),
                            bv_b[:].unsqueeze(1).to_broadcast([NK, NB, D]), ALU.add).then_inc(S["dve_setup"], 1)
            maximum(0, 0)
            v_rest(0)
            dve.wait_ge(S["act_setup"], 6)
            v.tensor_tensor(wol.rearrange("p k d -> p (k d)"), ps[:, WB, :],
                            woh.rearrange("p k d -> p (k d)").bitcast(F32), ALU.subtract).then_inc(S["dve_setup"], 1)
            maximum(1, 1)
            v_rest(1)

            def slot_values(n, bank_no):
                dve.wait_ge(S["pos_ready"], at(n + 1))
                v.tensor_tensor(slotv[:], ps[:, bank_no, 0:G * NE].rearrange("p (t e) -> p t e", t=G),
                                base_e[:].unsqueeze(1).to_broadcast([P, G, NE]), ALU.add).then_inc(S["slot_ready"], 1)

            def gates(n):
                dve.wait_ge(S["ge_ready"], at(n + 1))
                v.tensor_scalar(g1[:], ge[:], 1.0, None, ALU.add).then_inc(S["gate_step"], 1)
                dve.wait_ge(S["gate_step"], at(2 * n + 1))
                v.reciprocal(gt[:, :, 0], g1[:]).then_inc(S["gate_step"], 1)
                dve.wait_ge(S["gate_step"], at(2 * n + 2))
                v.tensor_tensor(gt[:, :, 1], ge[:], gt[:, :, 0], ALU.mult).then_inc(S["gates_ready"], 1)

            def route(n):
                dve.wait_ge(S["lg_ready"], at(n + 1))
                v.tensor_copy(lg[:], ps[:, QB, 0:G * NE].rearrange("p (t e) -> p t e", t=G)).then_inc(S["lg_copied"], 1)
                dve.wait_ge(S["lg_copied"], at(n + 1))
                wait_apart(dve)
                for t in range(G):
                    v.max(top[:, t, :], lg[:, t, :]).then_inc(S["top_ready"], 1)
                dve.wait_ge(S["top_ready"], at(2 * (n + 1)))
                v.tensor_tensor(gd[:], top[:, :, 1], top[:, :, 0], ALU.subtract).then_inc(S["gd_ready"], 1)
                for t in range(G):
                    ins = v.max_index(tix[:, t, :], top[:, t, :], lg[:, t, :])
                ins.then_inc(S["tix_ready"], 1)
                dve.wait_ge(S["tix_ready"], at(2 * n + 1))
                v.tensor_copy(ek[:], tix[:, :, 0:2]).then_inc(S["tix_ready"], 1)
                dve.wait_ge(S["tix_ready"], at(2 * n + 2))
                for t in range(G):
                    v.tensor_tensor(oh[:, t], ek[:, t, :].unsqueeze(2).to_broadcast([P, 2, NE]),
                                    iota_e[:].unsqueeze(1).to_broadcast([P, 2, NE]),
                                    ALU.is_equal).then_inc(S["oh_ready"], 1)

            def body(m):
                units, qn, pre, tail, slots = parts(m)
                for j in range(UPM):
                    u = UPM * m + j
                    if units and (qn or j < UPM - 2):
                        maximum(u + 2, j % 2)
                    if isinstance(m, int) and u == 0:
                        blocks(1)
                    if units:
                        rest_pt(u, j % 2)
                    if j == 2 and qn:
                        rest_xT(m + 1)
                    if j == 4 and tail:
                        rest_oT(m - 1, 1)
                    if j == 7 and units:
                        rest_oT(m, 0)
                    if j == 0 and tail:
                        sum_o(u - 1)
                    if units and j > 0:
                        sum_o(u - 1)
                    if j == 0 and pre:
                        stats1(m + 2)
                    if j == 4 and qn:
                        rest_q(m + 1, 0)
                    if j == 4 and slots and not ending(m):
                        slot_values(m - 2, WB)
                    if j == 5 and slots and not tail:
                        slot_values(m - 2, SC)
                    if j == 6 and slots:
                        n = m - 2
                        dve.wait_ge(S["pick_ready"], at(2 * (n + 1)))
                        v.tensor_reduce(sk[:], pick[:], AX.X, ALU.add).then_inc(S["sk_ready"], 1)
                        gates(n)
                    if j == 6 and tail:
                        n = m - 1
                        dve.wait_ge(S["rstd2_ready"], at(2 * m))
                        if later(n, 0):
                            dve.wait_ge(S["rows_ready"], at(n))
                            dve.wait_ge(S["x2T_ready"], at(n))
                        for t in range(G):
                            v.tensor_scalar(xn2[:, t, :], xs[:, at(n * G + t), :], mv2[:, t, 0:1],
                                            rstd2[:, t:t + 1], ALU.subtract, ALU.mult).then_inc(S["xn2_ready"], 1)
                    if j == 0 and tail:
                        divide_o(m - 1, UPM - 1)
                    if units and j > 0:
                        divide_o(m, j - 1)
                    if j == (4 if ending(m) else 2) and slots:
                        route(m - 2)
                    if j == 5 and tail:
                        n = m - 1
                        dve.wait_ge(S["wo_ready"], at(m))
                        dve.wait_ge(S["xbo_ready"], at(m))
                        v.tensor_tensor(xs[:, bass.ds(at(n * G), G), :], bank(WB, G), xbo[:], ALU.add).then_inc(S["x1_ready"], 1)
                        if ending(m):
                            slot_values(m - 2, SC)
                        dve.wait_ge(S["x1_ready"], at(m))
                        wait_apart(dve)
                        stats(lambda t: xs[:, at(n * G + t), :], st2, mv2, "stat2_step", n)
                    if j == 7 and qn:
                        rest_q(m + 1, 1)

            macro_loop(dve, body)

            def ffn_xT(c, par):
                dve.wait_ge(S["fxT_head"], at(c + 1))
                v.tensor_tensor(xTl[:, par, :], ps[:, 6, :], xTh[:, par, :].bitcast(F32),
                                ALU.subtract).then_inc(S["fxT_rest"], 1)

            def ffn_h(c, par):
                for i in range(MT // 2):
                    dve.wait_ge(S["h_head"], at(c * (MT // 2) + i + 1))
                    v.tensor_tensor(hl[:, par, 2 * i * CH:2 * (i + 1) * CH], hf[:, i % 2, :],
                                    hh[:, par, 2 * i * CH:2 * (i + 1) * CH].bitcast(F32),
                                    ALU.subtract).then_inc(S["h_rest"], 1)

            def rest(e, par, half):
                hs = slice(half * KT * HID, (half + 1) * KT * HID)
                dve.wait_ge(S["w_head"], at(2 * e + half + 1))
                v.tensor_tensor(wl[:, par, hs], wraw[:, hs], wh[:, par, hs].bitcast(F32),
                                ALU.subtract).then_inc(S["w_rest"], 1)

            def ffn_y(e, c, par, half):
                dve.wait_ge(S["y_ready"], at(c + 1))
                if later(c, 1):
                    dve.wait_ge(S["y_scattered%d" % par], at(half * (G * 16)))
                v.tensor_tensor(yb[:, par], ps[:, 4 + par, :].rearrange("p (t d) -> p t d", t=G),
                                b2_b[:, at(e), :].unsqueeze(1).to_broadcast([P, G, D]), ALU.add).then_inc(S["y_copied"], 1)
                dve.wait_ge(S["y_copied"], at(c + 1))
                dve.wait_ge(S["tags_ready"], at(c + 1))
                dve.wait_ge(S["acc_gathered%d" % par], at((half + 1) * (G * 16)))
                for t in range(G):
                    ins = v.scalar_tensor_tensor(out=yb[:, par, t, :], in0=yb[:, par, t, :], scalar=cgate[:, par, t:t + 1],
                                                 in1=acc[:, par, t, :], op0=ALU.mult, op1=ALU.add)
                ins.then_inc(S["fin_ready"], 1)

            ffn_xT(0, 0)
            ffn_xT(1, 1)
            ffn_h(0, 0)
            dve.wait_ge(S["b2_loaded"], 16)

            def pair(ep, last):
                for aa in range(2):
                    for j in range(CPE):
                        i = aa * CPE + j
                        c = ep * (2 * CPE) + i
                        if not (last and i == 2 * CPE - 1):
                            ffn_h(c + 1, 1 - i % 2)
                        if not (last and i >= 2 * CPE - 2):
                            ffn_xT(c + 2, i % 2)
                        if j < 2 and not (last and aa == 1):
                            rest(ep * 2 + aa + 1, 1 - aa, j)
                        ffn_y(ep * 2 + aa, c, i % 2, ep * CPE + i // 2)

            pair(0, False)
            with dve.Fori(1, NE // 2 - 1) as ep:
                pair(Count(ep), False)
            pair(NE // 2 - 1, True)

        @block.tensor
        def _(pe):
            T = nc.tensor

            def mm3(dst, sh, sl, mh, ml, first, last):
                T.matmul(dst, sh, mh, start=first, stop=False)
                T.matmul(dst, sh, ml, start=False, stop=False)
                return T.matmul(dst, sl, mh, start=False, stop=last)

            pe.wait_ge(S["const_ready"], 2)

            def turn_weight(w, b):
                for k in range(KT):
                    for r in range(KT):
                        ins = T.transpose(ps[:, b, k * D + r * P:k * D + (r + 1) * P],
                                          wnat[:, w, r, k * P:(k + 1) * P], identf[:])
                ins.then_inc(S["pe_setup"], 1)

            pe.wait_ge(S["w_loaded"], at(16 * 3))
            turn_weight(0, 0)
            turn_weight(1, 1)
            for k in range(KT):
                for b in range(NB):
                    ins = T.transpose(ps[:, 2, (k * NB + b) * NK:(k * NB + b + 1) * NK],
                                      cnat[:, b, k * P:(k + 1) * P], identf[0:NK, 0:NK])
            ins.then_inc(S["pe_setup"], 1)

            def bias_rows():
                nrow = NE * MT + 2 * KT
                pe.wait_ge(S["bias_loaded"], at(16 * 3))
                T.transpose(ps[:, 4, 0:nrow], brow[:], identf[0:nrow, 0:nrow]).then_inc(S["pe_setup"], 1)

            def project_k():
                pe.wait_ge(S["act_setup"], 3)
                for r in range(KT):
                    for k in range(KT):
                        ins = T.matmul(ps[:, 1, r * NB * NK:(r + 1) * NB * NK], wkT[:, k, r * P:(r + 1) * P],
                                       cT[:, k, :], start=(k == 0), stop=(k == KT - 1))
                ins.then_inc(S["pe_setup"], 1)

            def project_v():
                pe.wait_ge(S["act_setup"], 5)
                for b in range(NB):
                    for k in range(KT):
                        ins = T.matmul(ps[0:NK, 3, b * D:(b + 1) * D], cT[:, k, b * NK:(b + 1) * NK], wvT[:, k, :],
                                       start=(k == 0), stop=(k == KT - 1))
                ins.then_inc(S["pe_setup"], 1)

            def turn_macro(src, done):
                for k in range(KT):
                    for t in range(G):
                        ins = T.transpose(ps[:, TR, k * GT + t * P:k * GT + (t + 1) * P], src(t)[:, k * P:(k + 1) * P],
                                          identf[:])
                ins.then_inc(S[done], 1)

            def turn_xn(m):
                pe.wait_ge(S["xn_ready"], at(2 * (m + 1)))
                if later(m, 1):
                    pe.wait_ge(S["oT_rest"], at(2 * m - 3))
                if later(m, 2):
                    pe.wait_ge(S["x2T_copied"], at(m - 2))
                turn_macro(lambda t: xn[:, t, :], "xT_ready")

            def turn_o(m, t):
                pe.wait_ge(S["o_done"], at(UPM * m + UPT * (t + 1)))
                for k in range(KT):
                    ins = T.transpose(ps[:, TR, k * GT + t * P:k * GT + (t + 1) * P], o[:, t, k * P:(k + 1) * P], identf[:])
                ins.then_inc(S["oT_ready"], 1)

            def project_q(m):
                pe.wait_ge(S["xT_rest"], at(m + 1))
                if later(m, 2):
                    pe.wait_ge(S["lg_copied"], at(m - 2))
                if later(m, 0):
                    pe.wait_ge(S["q_rest"], at(2 * m))
                for r in range(KT):
                    for k in range(KT):
                        ks = slice(k * GT, (k + 1) * GT)
                        rs = slice(r * P, (r + 1) * P)
                        ins = mm3(bank(QB, KT)[:, r, :], wqh[:, k, rs], wql[:, k, rs], xTh[:, 0, ks], xTl[:, 0, ks],
                                  k == 0, k == KT - 1)
                ins.then_inc(S["q_ready"], 1)

            def scores(m, j, par):
                t, quarter = j // UPT, j % UPT
                r, half = quarter * HU // HK, quarter % (HK // HU)
                if j % UPT == 0:
                    pe.wait_ge(S["q_rest"], at(2 * m + t + 1))
                if later(UPM * m + j, 1):
                    pe.wait_ge(S["exp_ready"], at(UPM * m + j - 1))
                ts = slice(t * P, (t + 1) * P)
                cs = slice(half * UC, (half + 1) * UC)
                b = batch_of(m)
                dst = ps[:, SC + par, 0:UC]
                T.matmul(dst, identb[:], mb[:, at(m * G + t), :].unsqueeze(1).to_broadcast([P, HU, NK]),
                         start=True, stop=False)
                mm3(dst, qh[:, r, ts], ql[:, r, ts], kbh[:, b, r, cs], kbl[:, b, r, cs],
                    False, True).then_inc(S["sc_ready"], 1)

            def turn_p(u, par):
                pe.wait_ge(S["exp_ready"], at(u + 1))
                if later(u, 1):
                    pe.wait_ge(S["ptl_ready"], at(u - 1))
                for h in range(HU):
                    ins = T.transpose(ps[0:NK, PT + par, h * P:(h + 1) * P], pb[:, par, h * NK:(h + 1) * NK], identf[:])
                ins.then_inc(S["pt_ready"], 1)

            def times_v(m, j, par):
                u = UPM * m + j
                pe.wait_ge(S["ptl_ready"], at(u + 1))
                if later(u, 0):
                    pe.wait_ge(S["osum_part"], at(2 * u))
                b = batch_of(m)
                for h in range(HU):
                    dst = ps[:, PV, h * VW:(h + 1) * VW]
                    rhs = vcat[:, b, (j % UPT) * HU + h, :]
                    T.matmul(dst, pth[:, par, h * P:(h + 1) * P], rhs, start=True, stop=False)
                    ins = T.matmul(dst, ptl[:, par, h * P:(h + 1) * P], rhs, start=False, stop=True)
                ins.then_inc(S["pv_ready"], 1)

            def logits(n):
                pe.wait_ge(S["x2T_copied"], at(n + 1))
                pe.wait_ge(S["q_rest"], at(at_most(2 * (n + 3), 2 * NM)))
                for t in range(G):
                    for k in range(KT):
                        ins = T.matmul(ps[:, QB, t * NE:(t + 1) * NE],
                                       x2T[:, k * GT + t * P:k * GT + (t + 1) * P], wr[:, k, :],
                                       start=(k == 0), stop=(k == KT - 1))
                ins.then_inc(S["lg_ready"], 1)

            def positions(n, bank_no):
                pe.wait_ge(S["run_ready"], at(n + 1))
                for t in range(G):
                    dst = ps[:, bank_no, t * NE:(t + 1) * NE]
                    T.matmul(dst, before[:], ohs[:, t, :], start=True, stop=False)
                    ins = T.matmul(dst, onesb[:], run[:, t, :], start=False, stop=True)
                ins.then_inc(S["pos_ready"], 1)

            project_k()
            turn_xn(0)
            bias_rows()
            pe.wait_ge(S["w2_loaded"], at(16 * 2))
            turn_weight(2, 3)
            pe.wait_ge(S["dve_setup"], 1)
            project_q(0)
            project_v()
            turn_weight(3, WB)
            pe.wait_ge(S["kb_head"], 1)
            pe.wait_ge(S["kb_rest"], 1)
            pe.wait_ge(S["mask_ready"], 1)
            scores(0, 0, 0)
            scores(0, 1, 1)

            def body(m):
                units, qn, pre, tail, slots = parts(m)
                for j in range(UPM):
                    u = UPM * m + j
                    if units:
                        turn_p(u, j % 2)
                        if j < UPM - 2:
                            scores(m, j + 2, j % 2)
                        elif qn:
                            scores(m + 1, j + 2 - UPM, j % 2)
                    if j == 0 and slots:
                        pe.wait_ge(S["xn2_ready"], at(2 * (m - 1)))
                        pe.wait_ge(S["oT_rest"], at(at_most(2 * m - 1, 2 * NM)))
                        turn_macro(lambda t: xn2[:, t, :], "x2T_ready")
                    if j == 1 and qn:
                        turn_xn(m + 1)
                    if j == (3 if ending(m) else 2) and slots:
                        if ending(m) and tail:
                            pe.wait_ge(S["x2T_copied"], m - 1)
                            turn_o(m - 1, 1)
                        logits(m - 2)
                    if j == 3 and tail and not ending(m):
                        pe.wait_ge(S["xT_rest"], at(at_most(m + 2, NM)))
                        if slots:
                            pe.wait_ge(S["x2T_copied"], at(m - 1))
                        turn_o(m - 1, 1)
                    if j == 4 and slots and not ending(m):
                        pe.wait_ge(S["x1_ready"], at(m - 1))
                        positions(m - 2, WB)
                    if j == 6 and units:
                        if later(m, 0):
                            pe.wait_ge(S["oT_rest"], at(2 * m))
                        turn_o(m, 0)
                    if j == 0 and tail:
                        times_v(m - 1, UPM - 1, 1)
                    if units and j > 0:
                        times_v(m, j - 1, 1 - j % 2)
                    if j == 5 and tail:
                        pe.wait_ge(S["oT_rest"], at(2 * m))
                        if slots and not ending(m):
                            pe.wait_ge(S["slot_ready"], at(m - 1))
                        for t in range(G):
                            for k in range(KT):
                                ks = slice(k * GT + t * P, k * GT + (t + 1) * P)
                                ins = mm3(bank(WB, G)[:, t, :], oTh[:, ks], oTl[:, ks], woh[:, k, :], wol[:, k, :],
                                          k == 0, k == KT - 1)
                        ins.then_inc(S["wo_ready"], 1)
                    if j == 5 and ending(m):
                        positions(m - 2, SC)
                    if j == 3 and qn:
                        project_q(m + 1)
                    if isinstance(m, int) and m == 0 and j == 0:
                        pe.wait_ge(S["dve_setup"], 6)
                        pe.wait_ge(S["v_split"], 1)
                    if isinstance(m, int) and m == 1 and j == 0:
                        pe.wait_ge(S["kb_head"], 2)
                        pe.wait_ge(S["kb_rest"], 2)
                        pe.wait_ge(S["small_loaded"], at(16 * 3))

            macro_loop(pe, body)

            def turn_x(c, par, half):
                pe.wait_ge(S["xc_loaded%d" % par], at((half + 1) * 16))
                if later(c, 0):
                    pe.wait_ge(S["fxT_rest"], at(c))
                for k in range(KT):
                    for t in range(G):
                        ins = T.transpose(ps[:, 6, k * CH + t * P:k * CH + (t + 1) * P],
                                          xc[:, par, t, k * P:(k + 1) * P], identf[:])
                ins.then_inc(S["fxT_ready"], 1)

            def hidden(e, c, par, epar, first_of_expert):
                pe.wait_ge(S["fxT_rest"], at(c + 1))
                if first_of_expert:
                    pe.wait_ge(S["w_rest"], at(2 * e + 1))
                for i in range(MT // 2):
                    if later(c, 0):
                        pe.wait_ge(S["h_relu"], at((c - 1) * (MT // 2) + i + 1))
                    for s in range(2):
                        for k in range(KT):
                            ws = slice(k * HID + (2 * i + s) * P, k * HID + (2 * i + s + 1) * P)
                            ks = slice(k * CH, (k + 1) * CH)
                            ins = mm3(ps[:, i, s * CH:(s + 1) * CH], wh[:, epar, ws], wl[:, epar, ws],
                                      xTh[:, par, ks], xTl[:, par, ks], k == 0, k == KT - 1)
                    ins.then_inc(S["h_ready"], 1)

            def output(e, c, par, epar, first_of_expert):
                pe.wait_ge(S["h_rest"], at((c + 1) * (MT // 2)))
                if first_of_expert:
                    pe.wait_ge(S["w_rest"], at(2 * e + 2))
                if later(c, 1):
                    pe.wait_ge(S["y_copied"], at(c - 1))
                for t in range(G):
                    for k in range(MT):
                        hs = slice(k * CH + t * P, k * CH + (t + 1) * P)
                        w2s = slice(KT * HID + k * D, KT * HID + (k + 1) * D)
                        ins = mm3(ps[:, 4 + par, t * D:(t + 1) * D], hh[:, par, hs], hl[:, par, hs],
                                  wh[:, epar, w2s], wl[:, epar, w2s], k == 0, k == MT - 1)
                ins.then_inc(S["y_ready"], 1)

            turn_x(0, 0, 0)
            turn_x(1, 1, 0)
            hidden(0, 0, 0, 0, True)

            def pair(ep, last):
                for aa in range(2):
                    for j in range(CPE):
                        i = aa * CPE + j
                        c = ep * (2 * CPE) + i
                        if not (last and i == 2 * CPE - 1):
                            hidden(ep * 2 + (i + 1) // CPE, c + 1, 1 - i % 2, ((i + 1) // CPE) % 2, (i + 1) % CPE == 0)
                        if not (last and i >= 2 * CPE - 2):
                            turn_x(c + 2, i % 2, ep * CPE + (i + 2) // 2)
                        output(ep * 2 + aa, c, i % 2, aa, j == 0)

            pair(0, False)
            with pe.Fori(1, NE // 2 - 1) as ep:
                pair(Count(ep), False)
            pair(NE // 2 - 1, True)


_INS = ["x", "ctx_1024", "mask_1x1xSxS2_ik0", "L0_xattn_Wq", "L0_xattn_bq", "L0_xattn_Wk", "L0_xattn_bk",
        "L0_xattn_Wv", "L0_xattn_bv", "L0_xattn_Wo", "L0_xattn_bo", "L0_ffn_w_router", "L0_ffn_w1", "L0_ffn_b1",
        "L0_ffn_w2", "L0_ffn_b2"]


def kernel(**inputs):
    import numpy as np
    import concourse.bacc as bacc
    from concourse.bass_utils import run_bass_kernel_spmd

    nc = bacc.Bacc("TRN2", target_bir_lowering=False, num_devices=1)
    arrays, args = {}, []
    for name in _INS:
        a = np.ascontiguousarray(inputs[name])
        arrays[f"in_{name}"] = a
        args.append(nc.dram_tensor(f"in_{name}", a.shape, mybir.dt.from_np(a.dtype), kind="ExternalInput").ap())
    out = nc.dram_tensor("out_0", inputs["x"].shape, F32, kind="ExternalOutput").ap()
    xattn_moe_kernel(nc, *args, out)
    r = run_bass_kernel_spmd(nc, [arrays], core_ids=[0])
    return r.results[0]["out_0"]
```
